# Optimizing a Trainium2 kernel written in Bass

```python
import numpy as np
import jax
import jax.numpy as jnp

def _softmax(x, axis=-1):
    return jax.nn.softmax(x, axis=axis)

def _gelu(x):
    return jax.nn.gelu(x, approximate=True)

def _silu(x):
    return jax.nn.silu(x)

def _sigmoid(x):
    return jax.nn.sigmoid(x)

def _layernorm(x, axis=-1, eps=1e-05):
    m = jnp.mean(x, axis=axis, keepdims=True)
    v = jnp.var(x, axis=axis, keepdims=True)
    return (x - m) / jnp.sqrt(v + eps)

def _scatter_add(tgt, idx, src, axis=0):
    return tgt.at[idx].add(src)

def _segment_sum(src, seg, n):
    return jax.ops.segment_sum(src, seg, n)
kernel_name = 'mk_xattn_ffn_d2_seqx_r8_8f30dc'

def setup_inputs(seed: int=0):
    np.random.seed(seed)
    _w = jnp.asarray

    def _rec_inputs():
        import jax
        import jax.numpy as jnp
        _rk = jax.random.key(seed)
        x = -0.000125 + 0.9999 * jax.random.normal(jax.random.fold_in(_rk, 1), (8, 128, 512), jnp.float32)
        _lenS = 128 - jax.random.randint(jax.random.fold_in(_rk, 7), (8,), 0, max(1, 128 // 4) + 1, jnp.int32)
        _lenS2 = 128 - jax.random.randint(jax.random.fold_in(_rk, 8), (8,), 0, max(1, 128 // 4) + 1, jnp.int32)
        _ctx_4096P = jax.random.normal(jax.random.fold_in(_rk, 11), (8, 16, 512), jnp.float32)
        _ctx_4096c = jax.random.dirichlet(jax.random.fold_in(_rk, 511), 0.3 * jnp.ones((16,), jnp.float32), (8, 128))
        _ctx_4096t = jnp.einsum('bsk,bkd->bsd', _ctx_4096c, _ctx_4096P)
        _ctx_4096t = _ctx_4096t * jax.lax.rsqrt(jnp.mean(jnp.square(_ctx_4096t)) + 1e-12) * 0.953939
        ctx_4096 = -1.52775e-05 + 0.999936 * (_ctx_4096t + 0.3 * jax.random.normal(jax.random.fold_in(_rk, 611), (8, 128, 512), jnp.float32))
        _validS = jnp.arange(128)[None, :] < _lenS[:, None]
        _validS2 = jnp.arange(128)[None, :] < _lenS2[:, None]
        _causal = jnp.tril(jnp.ones((128, 128), dtype=bool))
        mask_Bx1x4096_ff1 = jnp.where(jnp.ones((8, 1, 512), dtype=bool), 1.0, 0.0).astype(jnp.float32)
        mask_1x1xSxS2_ff0 = jnp.where(jnp.ones((1, 1, 128, 128), dtype=bool), 0.0, -1000000000.0).astype(jnp.float32)
        return (x, ctx_4096, mask_Bx1x4096_ff1, mask_1x1xSxS2_ff0)
    x, ctx_4096, mask_Bx1x4096_ff1, mask_1x1xSxS2_ff0 = _rec_inputs()

    def _L0_xattn_setup():
        import jax, jax.numpy as jnp
        import numpy as np
        W = 128
        H = 8
        D = 128
        DK = D // 2

        def _to_patches(x):
            b, d, s = x.shape
            np_ = s // W
            return x.reshape(b, d, np_, W).transpose(0, 2, 1, 3).reshape(b * np_, d, W)
        key = jax.random.key(seed)
        ks = jax.random.split(key, 10)
        B, S = (8, 512)
        qk = jax.random.normal(ks[0], (B, D, S), dtype=jnp.float32)
        v = jax.random.normal(ks[1], (B, D, S), dtype=jnp.float32)
        masks = jnp.ones((B, 1, S), dtype=jnp.float32)
        sc = 1.0 / np.sqrt(D)
        Wq = jax.random.normal(ks[2], (DK, D), dtype=jnp.float32) * sc
        bq = jnp.zeros((DK,), dtype=jnp.float32)
        Wk = jax.random.normal(ks[3], (DK, D), dtype=jnp.float32) * sc
        bk = jnp.zeros((DK,), dtype=jnp.float32)
        Wv = jax.random.normal(ks[4], (DK, D), dtype=jnp.float32) * sc
        bv = jnp.zeros((DK,), dtype=jnp.float32)
        Wo = jax.random.normal(ks[5], (D, DK), dtype=jnp.float32) * (1.0 / np.sqrt(DK))
        bo = jnp.zeros((D,), dtype=jnp.float32)
        return dict(qk=qk, v=v, masks=masks, Wq=Wq, bq=bq, Wk=Wk, bk=bk, Wv=Wv, bv=bv, Wo=Wo, bo=bo)
    _L0_xattn_all = _L0_xattn_setup()
    _L0_xattn_in = {k: v for k, v in _L0_xattn_all.items() if k in ('Wq', 'bq', 'Wk', 'bk', 'Wv', 'bv', 'Wo', 'bo')}
    del _L0_xattn_all

    def _L0_ffn_setup():
        import jax, jax.numpy as jnp
        import numpy as np
        HIDDEN = 512
        INTER = 1376
        key = jax.random.key(seed)
        k0, k1, k2, k3 = jax.random.split(key, 4)
        scale_h = 1.0 / np.sqrt(HIDDEN)
        scale_i = 1.0 / np.sqrt(INTER)
        return {'x': jax.random.normal(k0, (4, 32, HIDDEN), dtype=jnp.float32), 'w_gate': jax.random.normal(k1, (INTER, HIDDEN), dtype=jnp.float32) * scale_h, 'w_up': jax.random.normal(k2, (INTER, HIDDEN), dtype=jnp.float32) * scale_h, 'w_down': jax.random.normal(k3, (HIDDEN, INTER), dtype=jnp.float32) * scale_i}
    _L0_ffn_all = _L0_ffn_setup()
    _L0_ffn_in = {k: v for k, v in _L0_ffn_all.items() if k in ('w_gate', 'w_up', 'w_down')}
    del _L0_ffn_all

    def _L1_xattn_setup():
        import jax, jax.numpy as jnp
        import numpy as np
        B, Q, K, D = (1, 128, 6404, 512)
        H, KVH, HD = (32, 8, 128)
        GROUPS = H // KVH
        EPS = 1e-05

        def _rmsnorm(x, w):
            xf = x.astype(jnp.float32)
            var = jnp.mean(xf * xf, axis=-1, keepdims=True)
            return (xf * jax.lax.rsqrt(var + EPS)).astype(x.dtype) * w
        key = jax.random.key(seed)
        ks = jax.random.split(key, 8)
        s = 0.02
        return {'hidden_states': jax.random.normal(ks[0], (B, Q, D), jnp.float32), 'cross_attention_states': jax.random.normal(ks[1], (B, K, D), jnp.float32), 'attention_mask': jnp.zeros((B, 1, Q, K), jnp.float32), 'Wq': jax.random.normal(ks[2], (H * HD, D), jnp.float32) * s, 'Wk': jax.random.normal(ks[3], (KVH * HD, D), jnp.float32) * s, 'Wv': jax.random.normal(ks[4], (KVH * HD, D), jnp.float32) * s, 'Wo': jax.random.normal(ks[5], (D, H * HD), jnp.float32) * s, 'q_norm_w': jnp.ones((HD,), jnp.float32), 'k_norm_w': jnp.ones((HD,), jnp.float32)}
    _L1_xattn_all = _L1_xattn_setup()
    _L1_xattn_in = {k: v for k, v in _L1_xattn_all.items() if k in ('Wq', 'Wk', 'Wv', 'Wo', 'q_norm_w', 'k_norm_w')}
    del _L1_xattn_all

    def _L1_ffn_setup():
        import jax, jax.numpy as jnp
        import numpy as np
        M = 512
        K = 512

        def _make_2to4_mask(key, shape):
            scores = jax.random.normal(key, shape)
            g = scores.reshape(shape[0], shape[1] // 4, 4)
            rank = jnp.argsort(jnp.argsort(-jnp.abs(g), axis=-1), axis=-1)
            return (rank < 2).reshape(shape).astype(jnp.float32)
        key = jax.random.key(seed)
        k_x, k_w12, k_b12, k_w3, k_b3, k_m = jax.random.split(key, 6)
        x = jax.random.normal(k_x, (4, 256, K), dtype=jnp.float32)
        w12_dense = jax.random.normal(k_w12, (2 * M, K), dtype=jnp.float32) * (1.0 / np.sqrt(K))
        mask12 = _make_2to4_mask(k_m, (2 * M, K))
        w12 = w12_dense * mask12
        b12 = jax.random.normal(k_b12, (2 * M,), dtype=jnp.float32) * 0.01
        w3 = jax.random.normal(k_w3, (M, M), dtype=jnp.float32) * (1.0 / np.sqrt(M))
        b3 = jax.random.normal(k_b3, (M,), dtype=jnp.float32) * 0.01
        return {'x': x, 'w12': w12, 'b12': b12, 'w3': w3, 'b3': b3}
    _L1_ffn_all = _L1_ffn_setup()
    _L1_ffn_in = {k: v for k, v in _L1_ffn_all.items() if k in ('w12', 'b12', 'w3', 'b3')}
    del _L1_ffn_all
    return {'x': x, 'ctx_4096': ctx_4096, 'mask_Bx1x4096_ff1': mask_Bx1x4096_ff1, 'mask_1x1xSxS2_ff0': mask_1x1xSxS2_ff0, 'L0_xattn_Wq': _L0_xattn_in['Wq'], 'L0_xattn_bq': _L0_xattn_in['bq'], 'L0_xattn_Wk': _L0_xattn_in['Wk'], 'L0_xattn_bk': _L0_xattn_in['bk'], 'L0_xattn_Wv': _L0_xattn_in['Wv'], 'L0_xattn_bv': _L0_xattn_in['bv'], 'L0_xattn_Wo': _L0_xattn_in['Wo'], 'L0_xattn_bo': _L0_xattn_in['bo'], 'L0_ffn_w_gate': _L0_ffn_in['w_gate'], 'L0_ffn_w_up': _L0_ffn_in['w_up'], 'L0_ffn_w_down': _L0_ffn_in['w_down'], 'L1_xattn_Wq': _L1_xattn_in['Wq'], 'L1_xattn_Wk': _L1_xattn_in['Wk'], 'L1_xattn_Wv': _L1_xattn_in['Wv'], 'L1_xattn_Wo': _L1_xattn_in['Wo'], 'L1_xattn_q_norm_w': _L1_xattn_in['q_norm_w'], 'L1_xattn_k_norm_w': _L1_xattn_in['k_norm_w'], 'L1_ffn_w12': _L1_ffn_in['w12'], 'L1_ffn_b12': _L1_ffn_in['b12'], 'L1_ffn_w3': _L1_ffn_in['w3'], 'L1_ffn_b3': _L1_ffn_in['b3']}

def reference(x, ctx_4096, mask_Bx1x4096_ff1, mask_1x1xSxS2_ff0, L0_xattn_Wq, L0_xattn_bq, L0_xattn_Wk, L0_xattn_bk, L0_xattn_Wv, L0_xattn_bv, L0_xattn_Wo, L0_xattn_bo, L0_ffn_w_gate, L0_ffn_w_up, L0_ffn_w_down, L1_xattn_Wq, L1_xattn_Wk, L1_xattn_Wv, L1_xattn_Wo, L1_xattn_q_norm_w, L1_xattn_k_norm_w, L1_ffn_w12, L1_ffn_b12, L1_ffn_w3, L1_ffn_b3):
    import jax
    import jax.numpy as jnp

    def _L0_xattn_ref(qk, v, masks, Wq, bq, Wk, bk, Wv, bv, Wo, bo):
        import jax, jax.numpy as jnp
        import numpy as np
        W = 128
        H = 8
        D = 128
        DK = D // 2

        def _to_patches(x):
            b, d, s = x.shape
            np_ = s // W
            return x.reshape(b, d, np_, W).transpose(0, 2, 1, 3).reshape(b * np_, d, W)
        B, _, S = qk.shape
        np_ = S // W
        qp = _to_patches(qk)
        vp = _to_patches(v)
        mp = _to_patches(masks)
        q = jnp.einsum('ed,bdw->bew', Wq, qp) + bq[:, None]
        k = jnp.einsum('ed,bdw->bew', Wk, qp) + bk[:, None]
        val = jnp.einsum('ed,bdw->bew', Wv, vp) + bv[:, None]
        BN = q.shape[0]
        dh = DK // H
        qh = q.reshape(BN, H, dh, W)
        kh = k.reshape(BN, H, dh, W)
        vh = val.reshape(BN, H, dh, W)
        scores = jnp.einsum('bhdi,bhdj->bhij', qh, kh) / jnp.sqrt(jnp.asarray(dh, qh.dtype))
        scores = jnp.where(mp[:, :, None, :] > 0, scores, jnp.asarray(-1000000000.0, scores.dtype))
        attn = jax.nn.softmax(scores, axis=-1)
        o = jnp.einsum('bhij,bhdj->bhdi', attn, vh).reshape(BN, DK, W)
        o = jax.nn.gelu(o, approximate=False)
        out = jnp.einsum('de,bew->bdw', Wo, o) + bo[:, None]
        out = out.reshape(B, np_, D, W).transpose(0, 2, 1, 3).reshape(B, D, S)
        out = out * masks
        return out

    def _L0_ffn_ref(x, w_gate, w_up, w_down):
        import jax, jax.numpy as jnp
        import numpy as np
        HIDDEN = 512
        INTER = 1376
        gate = jax.nn.silu(jnp.einsum('bsh,ih->bsi', x, w_gate))
        up = jnp.einsum('bsh,ih->bsi', x, w_up)
        return jnp.einsum('bsi,hi->bsh', gate * up, w_down)

    def _L1_xattn_ref(hidden_states, cross_attention_states, attention_mask, Wq, Wk, Wv, Wo, q_norm_w, k_norm_w):
        import jax, jax.numpy as jnp
        import numpy as np
        B, Q, K, D = (1, 128, 6404, 512)
        H, KVH, HD = (32, 8, 128)
        GROUPS = H // KVH
        EPS = 1e-05

        def _rmsnorm(x, w):
            xf = x.astype(jnp.float32)
            var = jnp.mean(xf * xf, axis=-1, keepdims=True)
            return (xf * jax.lax.rsqrt(var + EPS)).astype(x.dtype) * w
        bsz, q_len, _ = hidden_states.shape
        kv_len = cross_attention_states.shape[1]
        q = (hidden_states @ Wq.T).reshape(bsz, q_len, H, HD).transpose(0, 2, 1, 3)
        k = (cross_attention_states @ Wk.T).reshape(bsz, kv_len, KVH, HD).transpose(0, 2, 1, 3)
        v = (cross_attention_states @ Wv.T).reshape(bsz, kv_len, KVH, HD).transpose(0, 2, 1, 3)
        q = _rmsnorm(q, q_norm_w)
        k = jnp.repeat(k, GROUPS, axis=1)
        v = jnp.repeat(v, GROUPS, axis=1)
        k = _rmsnorm(k, k_norm_w)
        scale = 1.0 / np.sqrt(HD)
        scores = jnp.einsum('bhqd,bhkd->bhqk', q, k) * scale
        scores = scores + attention_mask[:, :, :, :kv_len]
        probs = jax.nn.softmax(scores.astype(jnp.float32), axis=-1).astype(q.dtype)
        out = jnp.einsum('bhqk,bhkd->bhqd', probs, v)
        out = out.transpose(0, 2, 1, 3).reshape(bsz, q_len, H * HD)
        return out @ Wo.T

    def _L1_ffn_ref(x, w12, b12, w3, b3):
        import jax, jax.numpy as jnp
        import numpy as np
        M = 512
        K = 512

        def _make_2to4_mask(key, shape):
            scores = jax.random.normal(key, shape)
            g = scores.reshape(shape[0], shape[1] // 4, 4)
            rank = jnp.argsort(jnp.argsort(-jnp.abs(g), axis=-1), axis=-1)
            return (rank < 2).reshape(shape).astype(jnp.float32)
        x12 = jnp.einsum('bsk,mk->bsm', x, w12) + b12
        x1, x2 = jnp.split(x12, 2, axis=-1)
        x4 = jax.nn.silu(x1) * x2
        return jnp.einsum('bsm,nm->bsn', x4, w3) + b3
    x = x + _L0_xattn_ref(_layernorm(x, axis=-1), ctx_4096, mask_Bx1x4096_ff1, L0_xattn_Wq, L0_xattn_bq, L0_xattn_Wk, L0_xattn_bk, L0_xattn_Wv, L0_xattn_bv, L0_xattn_Wo, L0_xattn_bo)
    x = x + _L0_ffn_ref(_layernorm(x, axis=-1), L0_ffn_w_gate, L0_ffn_w_up, L0_ffn_w_down)
    x = x + _L1_xattn_ref(_layernorm(x, axis=-1), ctx_4096, mask_1x1xSxS2_ff0, L1_xattn_Wq, L1_xattn_Wk, L1_xattn_Wv, L1_xattn_Wo, L1_xattn_q_norm_w, L1_xattn_k_norm_w)
    x = x + _L1_ffn_ref(_layernorm(x, axis=-1), L1_ffn_w12, L1_ffn_b12, L1_ffn_w3, L1_ffn_b3)
    return x

_drawn_inputs = setup_inputs


def setup_inputs(seed=0):
    import zlib

    import numpy as np

    out = dict(_drawn_inputs(seed))
    spreads = {'L0_xattn_bq': (0.0, 0.788),
     'L0_xattn_bk': (0.0, 0.8),
     'L0_xattn_bv': (0.0, 0.1),
     'L0_xattn_bo': (0.0, 0.1),
     'L1_xattn_q_norm_w': (1.0, 0.6),
     'L1_xattn_k_norm_w': (1.0, 0.6)}
    factors = {'L1_ffn_b12': 8.0, 'L1_ffn_b3': 8.0}
    for name, (base, spread) in spreads.items():
        noise = np.random.default_rng([zlib.crc32(name.encode()), seed]).standard_normal(out[name].shape)
        drawn = base * np.exp(spread * noise) if base else spread * noise
        out[name] = jnp.asarray(drawn.astype(out[name].dtype))
    for name, factor in factors.items():
        out[name] = (out[name] * factor).astype(out[name].dtype)
    return out
```

```python
from contextlib import ExitStack

import concourse.bass as bass
from concourse import mybir

F32 = mybir.dt.float32
FR = mybir.dt.float32r
ACT = mybir.ActivationFunctionType
ALU = mybir.AluOpType
AX_X = mybir.AxisListType.X

P = 128
NB = 8
D = 512
KC = D // P
TOK = NB * P
HALF = TOK // 2
EPS = 1e-5

H0, DH0 = 8, 8
E0 = H0 * DH0
STACK = 32
NPATCH = D // P
MASKED = -1e30

KVH, GROUP, HD = 8, 4, 128

INTER = 1376
CH0 = (INTER + P - 1) // P
CH1 = D // P


def wait(eng, sem, value):
    if isinstance(value, int) and value <= 0:
        return
    eng.wait_ge(sem, value)


def build(nc, A, out):
    with ExitStack() as ctx:
        def alloc(stack):
            return lambda name, shape, dt=F32: stack.enter_context(nc.sbuf_tensor(name, shape, dt))

        def sem(name):
            return ctx.enter_context(nc.semaphore(name))

        ps = ctx.enter_context(nc.psum_tensor("ps", [P, 8, 512], F32))

        g_ = alloc(ctx)
        x = g_("x", [P, NB, D])
        ffn_stage = g_("ffn_stage", [P, 2, 3 * D])
        ident = g_("ident", [P, P])
        ones_col = g_("ones_col", [P, 1])
        neghalf = g_("neghalf", [P, NB * 4])
        stats = g_("stats", [P, NB, 6])
        meanvar = g_("meanvar", [P, NB, 2])
        vareps = g_("vareps", [P, NB])
        rstd = g_("rstd", [P, NB])

        kT_dram = nc.dram_tensor("kT_scratch", (KVH, HD, TOK), F32, kind="Internal").ap()
        v_dram = nc.dram_tensor("v_scratch", (KVH, P, NB, HD), F32, kind="Internal").ap()

        with ExitStack() as l0:
            a_ = alloc(l0)
            wkv_hi = a_("wkv_hi", [P, 2, KC, KVH * HD], FR)
            wkv_lo = a_("wkv_lo", [P, 2, KC, KVH * HD], FR)
            work0 = a_("work0", [P, 2, 4, 4, P])
            kv_stage = work0[:].rearrange("p a b c d -> p (a b c d)").rearrange("p (k n) -> p k n", k=KC)
            pT0 = a_("pT0", [P, 4, 4, P])
            q_stack = a_("q_stack", [P, 2, 512], FR)
            k_stack = a_("k_stack", [P, 2, 512], FR)
            neg_hi = a_("neg_hi", [P, 4, 512], FR)
            xn0 = a_("xn0", [P, 512])
            xn0_hi = a_("xn0_hi", [P, 512], FR)
            xn0_lo = a_("xn0_lo", [P, 512], FR)
            ctxT_stage = a_("ctxT_stage", [P, KC, P])
            ctxT_hi = a_("ctxT_hi", [P, KC, P], FR)
            ctxT_lo = a_("ctxT_lo", [P, KC, P], FR)
            k_raw = a_("k_raw", [P, KVH, HD])
            k_norm = a_("k_norm", [P, KVH, HD])
            kT_out = a_("kT_out", [P, KVH, P])
            v_out = a_("v_out", [P, KVH, HD])
            ksum = a_("ksum", [P, KVH])
            kvar = a_("kvar", [P, KVH])
            krstd = a_("krstd", [P, KVH])
            ctx_nat = a_("ctx_nat", [P, 512])
            v_aug = a_("v_aug", [P, NPATCH, H0, DH0 + 1])
            smax0 = a_("smax0", [P, 16])
            rden0 = a_("rden0", [P, 2, H0])
            wst_stage = a_("wst_stage", [P, 4, P])
            wst_hi = a_("wst_hi", [P, 4, P], FR)
            wst_lo = a_("wst_lo", [P, 4, P], FR)
            stack_col = a_("stack_col", [P, 10])
            wv0 = a_("wv0", [P, E0])
            bv0 = a_("bv0", [P, E0])
            mask_sel = a_("mask_sel", [1, P], FR)
            mask_sel_s = a_("mask_sel_s", [1, P])
            mask_row = a_("mask_row", [1, 512])
            mask_step = a_("mask_step", [1, 512])
            mask_bias = a_("mask_bias", [1, 512], FR)
            knorm_w = a_("knorm_w", [P, 3])
            o_all = a_("o_all", [P, NB * NPATCH, E0])
            mask_b = a_("mask_b", [P, 2, 512])
            wo0_stage = a_("wo0_stage", [E0, P])
            wo0_hi = a_("wo0_hi", [E0, P], FR)
            wo0_lo = a_("wo0_lo", [E0, P], FR)
            bo0 = a_("bo0", [P, 1])
            gel = a_("gel", [E0, 2, 512])
            gel_hi = a_("gel_hi", [E0, 2, 512], FR)
            gel_lo = a_("gel_lo", [E0, 2, 512], FR)
            delta0 = work0[:, 0].rearrange("p a s n -> p a (s n)")[:, 0:2]

        rest = ctx.enter_context(ExitStack())
        r_ = alloc(rest)
        hT_hi = r_("hT_hi", [P, KC, TOK], FR)
        hT_lo = r_("hT_lo", [P, KC, TOK], FR)
        xn = r_("xn", [P, 2, D])
        wq_stage = r_("wq_stage", [P, GROUP, KC, P])
        wo_stage = r_("wo_stage", [P, GROUP, D])
        kT_stage = r_("kT_stage", [P, TOK])
        v_stage = r_("v_stage", [P, NB, HD])
        wq_hi = r_("wq_hi", [P, GROUP, KC, P], FR)
        wq_lo = r_("wq_lo", [P, GROUP, KC, P], FR)
        wo_hi = r_("wo_hi", [P, GROUP, D], FR)
        wo_lo = r_("wo_lo", [P, GROUP, D], FR)
        kT_hi = r_("kT_hi", [P, TOK], FR)
        kT_lo = r_("kT_lo", [P, TOK], FR)
        v_hi = r_("v_hi", [P, NB, HD], FR)
        v_lo = r_("v_lo", [P, NB, HD], FR)
        prob = r_("prob", [P, 4, GROUP, P])
        pT_hi = r_("pT_hi", [P, 2, GROUP * P], FR)
        pT_lo = r_("pT_lo", [P, 2, GROUP * P], FR)
        mask1 = r_("mask1", [P, P])
        qvar = r_("qvar", [P, 4, GROUP])
        rq = r_("rq", [P, 2, 4, GROUP])
        negmax = r_("negmax", [P, NB, GROUP])
        psum1 = r_("psum1", [P, NB, GROUP])
        rden1 = r_("rden1", [P, NB, GROUP])
        b12 = r_("b12", [P, 2, CH1])
        b3 = r_("b3", [P, D])
        with ExitStack() as att:
            t_ = alloc(att)
            qT_hi = t_("qT_hi", [P, GROUP, HALF], FR)
            qT_lo = t_("qT_lo", [P, GROUP, HALF], FR)
            q_sq = t_("q_sq", [P, GROUP, HALF])
            oT_hi = t_("oT_hi", [P, 4, GROUP, P], FR)
            oT_lo = t_("oT_lo", [P, 4, GROUP, P], FR)
        with ExitStack() as ff:
            t_ = alloc(ff)
            ffn_hi = t_("ffn_hi", [P, 2, 3 * D], FR)
            ffn_lo = t_("ffn_lo", [P, 2, 3 * D], FR)
            silu = t_("silu", [P, 2, 512])
            gated = t_("gated", [P, 2, 512])
            gT_hi = t_("gT_hi", [P, 2, 512], FR)
            gT_lo = t_("gT_lo", [P, 2, 512], FR)

        names = """const_in x_in kvw_in0 kvw_in1 ctxT_in ctx_in mask_in maskb_ready maskb_in0 maskb_in1 kT_written v_written
            const_ready ident_zero ident_ready col_ready wst_hi_ready wst_lo_ready kvw_hi_ready kvw_lo_ready
            factor_ready stat_step l0_rstd_ready xn_ready xh_ready xl_ready th_ready tl_ready vaug_ready
            k_done k_copied ksum_ready krstd_step knorm_ready stack_done neghi_ready stack_ready v0_done
            v0_ready v_done v_copied kT_done kT_copied
            s0_done max0_ready sub0_ready exp0_ready t0_done t0_by_act t0_by_dve pv0_done rden0_ready o0_ready
            oT0_done gelu_ready gelhi_ready gello_ready wo0_done delta0_ready x0_ready wo0_split
            wq_in wo_in kT_in v_in att_const_in out_written
            wq_hi_ready wq_lo_ready wo_hi_ready wo_lo_ready kT_hi_ready kT_lo_ready v_hi_ready v_lo_ready
            q_done sq_ready qhi_ready qlo_ready ss_done qvar_ready rq_step rq_ready
            s_done masked_ready negmax_ready exp_ready rden_ready pn_ready
            t_done pthi_ready ptlo_ready pv_done ohi_ready olo_ready wo_done x_added""".split()
        S = {n: sem(n) for n in names}
        LN = [{n: sem(f"ln{i}_{n}") for n in ("step", "rstd_ready", "xn_ready", "t_done", "hi_ready", "lo_ready")}
              for i in range(3)]
        FF = [{n: sem(f"ffn{i}_{n}") for n in (
            "w_in0", "w_in1", "whi_ready", "wlo_ready", "gu_done", "silu_ready", "gated_ready", "ghi_ready",
            "glo_ready", "down_done", "x_added")} for i in range(2)]

        A_BANK, B_BANK = 6, 7
        scores0 = ps[:, 0:4, :].rearrange("p a (s n) -> p a s n", s=4)

        block = ctx.enter_context(nc.Block())

        @block.sync
        def _(sp):
            for dst, src in ((wst_stage[:], A["wst"]), (stack_col[:, 0:6], A["stack_col"]), (wv0[:], A["wv0"]),
                             (mask_sel_s[:], A["mask_sel"]),
                             (bv0[:], A["bv0"].partition_broadcast(P)), (wo0_stage[:], A["wo0"]),
                             (bo0[:], A["bo0"]), (knorm_w[:, 0:2], A["norm_w"])):
                sp.dma_start(dst, src).then_inc(S["const_in"], 16)
            sp.dma_start(x[:], A["x"].rearrange("b p s -> p b s")).then_inc(S["x_in"], 16)
            sp.dma_start(mask_row[:], A["mask_row"][0:1]).then_inc(S["mask_in"], 16)
            sp.dma_start(ctxT_stage[:], A["ctxT"][:, :, 0:P]).then_inc(S["ctxT_in"], 16)
            sp.dma_start(ctx_nat[:], A["ctx"][0]).then_inc(S["ctx_in"], 16)
            sp.dma_start(kv_stage, A["wk"]).then_inc(S["kvw_in0"], 16)
            sp.wait_ge(S["kvw_lo_ready"], 1)
            sp.dma_start(kv_stage, A["wv"]).then_inc(S["kvw_in1"], 16)
            for c in range(2):
                sp.dma_start(ffn_stage[:, c], A["ffn0"][c]).then_inc(FF[0][f"w_in{c}"], 16)

            def l0_step(b, last=False):
                if not last:
                    sp.wait_ge(S["th_ready"], b + 1)
                    sp.wait_ge(S["tl_ready"], b + 1)
                    sp.dma_start(ctxT_stage[:], A["ctxT"][:, :, bass.ds((b + 1) * P, P)]).then_inc(S["ctxT_in"], 16)
                    sp.wait_ge(S["maskb_ready"], 2 * b + 2)
                    sp.dma_start(mask_row[:], A["mask_row"][bass.ds(b + 1, 1)]).then_inc(S["mask_in"], 16)
                    sp.wait_ge(S["v0_done"], b + 1)
                    sp.dma_start(ctx_nat[:], A["ctx"][bass.ds(b + 1, 1)].rearrange("a p s -> p (a s)"))\
                      .then_inc(S["ctx_in"], 16)
                sp.wait_ge(S["v_copied"], 2 * b + 2)
                sp.dma_start(v_dram[:, :, bass.ds(b, 1), :].rearrange("g p a d -> p g (a d)"), v_out[:])\
                  .then_inc(S["v_written"], 16)
                sp.wait_ge(S["kT_copied"], 2 * b + 2)
                sp.dma_start(kT_dram[:, :, bass.ds(b * P, P)].rearrange("g d t -> d g t"), kT_out[:])\
                  .then_inc(S["kT_written"], 16)

            l0_step(0)
            with sp.Fori(1, NB - 1) as b:
                l0_step(b)
            l0_step(NB - 1, last=True)
            for b in range(NB):
                if b >= 2:
                    sp.wait_ge(S["delta0_ready"], b - 1)
                sp.dma_start(mask_b[:, b % 2], A["mask"][b].partition_broadcast(P)).then_inc(S[f"maskb_in{b % 2}"], 16)

            def ffn_load(i, c, slot):
                sp.wait_ge(FF[i]["wlo_ready"], c - 1)
                sp.dma_start(ffn_stage[:, slot], A[f"ffn{i}"][bass.ds(c, 1)].rearrange("a p n -> p (a n)"))\
                  .then_inc(FF[i][f"w_in{slot}"], 16)
            ffn_load(0, 2, 0)
            sp.wait_ge(S["x0_ready"], NB)
            sp.dma_start(mask1[:], A["mask1"]).then_inc(S["att_const_in"], 16)
            sp.dma_start(b12[:], A["b12"]).then_inc(S["att_const_in"], 16)
            sp.dma_start(b3[:], A["b3"].partition_broadcast(P)).then_inc(S["att_const_in"], 16)
            sp.wait_ge(S["kT_written"], 16 * NB)
            sp.wait_ge(S["v_written"], 16 * NB)

            def att_load(g):
                wait(sp, S["wq_lo_ready"], g)
                sp.dma_start(wq_stage[:], A["wq"][bass.ds(g, 1)].rearrange("a p h k n -> p (a h) k n"))\
                  .then_inc(S["wq_in"], 16)
                wait(sp, S["kT_lo_ready"], g)
                sp.dma_start(kT_stage[:], kT_dram[bass.ds(g, 1)].rearrange("a p n -> p (a n)")).then_inc(S["kT_in"], 16)
                wait(sp, S["v_lo_ready"], g)
                sp.dma_start(v_stage[:], v_dram[bass.ds(g, 1)].rearrange("a p b d -> p (a b) d")).then_inc(S["v_in"], 16)
                wait(sp, S["wo_lo_ready"], g)
                sp.dma_start(wo_stage[:], A["wo"][bass.ds(g, 1)].rearrange("a p h n -> p (a h) n"))\
                  .then_inc(S["wo_in"], 16)
            att_load(0)
            with sp.Fori(3, CH0 - 1, 2) as c:
                ffn_load(0, c, 1)
                ffn_load(0, c + 1, 0)
            with sp.Fori(1, KVH) as g:
                att_load(g)
            sp.wait_ge(FF[0]["wlo_ready"], CH0)
            for c in range(2):
                sp.dma_start(ffn_stage[:, c], A["ffn1"][c]).then_inc(FF[1][f"w_in{c}"], 16)
            for c in range(2, CH1):
                ffn_load(1, c, c % 2)
            for t in range(NB):
                sp.wait_ge(FF[1]["x_added"], NB * (CH1 - 1) + t + 1)
                sp.dma_start(out[t], x[:, t]).then_inc(S["out_written"], 16)
            sp.wait_ge(S["out_written"], 16 * NB)

        @block.gpsimd
        def _(pool):
            V = nc.gpsimd
            V.memset(ident[:], 0.0).then_inc(S["ident_zero"], 1)
            V.memset(neghalf[:], -0.5).then_inc(S["const_ready"], 1)
            V.memset(ones_col[:], 1.0).then_inc(S["const_ready"], 1)
            V.memset(v_aug[:], 1.0).then_inc(S["vaug_ready"], 1)
            pool.wait_ge(S["ident_zero"], 1)
            V.affine_select(out=ident[:], in_=ident[:], compare_op=ALU.not_equal, fill=1.0, base=0,
                            pattern=[[-1, P]], channel_multiplier=1).then_inc(S["ident_ready"], 1)
            pool.wait_ge(S["wst_hi_ready"], 1)
            V.tensor_tensor(wst_lo[:], wst_stage[:], wst_hi[:].bitcast(F32), ALU.subtract).then_inc(S["wst_lo_ready"], 1)
            pool.wait_ge(S["const_ready"], 2)
            pool.wait_ge(S["stat_step"], 17)
            V.tensor_tensor(rstd[:], vareps[:], neghalf[:, 0:NB], ALU.pow).then_inc(S["l0_rstd_ready"], 1)

            def lows(b):
                pool.wait_ge(S["th_ready"], b + 1)
                V.tensor_tensor(ctxT_lo[:], ctxT_stage[:], ctxT_hi[:].bitcast(F32), ALU.subtract)\
                 .then_inc(S["tl_ready"], 1)
                pool.wait_ge(S["xh_ready"], b + 1)
                V.tensor_tensor(xn0_lo[:], xn0[:], xn0_hi[:].bitcast(F32), ALU.subtract).then_inc(S["xl_ready"], 1)
            lows(0)
            pool.wait_ge(S["kvw_hi_ready"], 1)
            V.tensor_tensor(wkv_lo[:, 0], kv_stage, wkv_hi[:, 0].bitcast(F32), ALU.subtract).then_inc(S["kvw_lo_ready"], 1)
            pool.wait_ge(S["kvw_hi_ready"], 2)
            V.tensor_tensor(wkv_lo[:, 1], kv_stage, wkv_hi[:, 1].bitcast(F32), ALU.subtract).then_inc(S["kvw_lo_ready"], 1)

            def l0_step(b, last=False):
                pool.wait_ge(S["krstd_step"], 2 * b + 1)
                V.tensor_tensor(krstd[:], kvar[:], neghalf[:, 0:KVH], ALU.pow).then_inc(S["krstd_step"], 1)
                pool.wait_ge(S["krstd_step"], 2 * b + 2)
                wait(pool, S["kT_done"], 2 * b)
                V.tensor_tensor(k_norm[:], k_raw[:], krstd[:].unsqueeze(2).broadcast_to([P, KVH, HD]), ALU.mult)\
                 .then_inc(S["knorm_ready"], 1)
                if not last:
                    lows(b + 1)
            l0_step(0)
            with pool.Fori(1, NB - 1) as b:
                l0_step(b)
            l0_step(NB - 1, last=True)

            def ln_rstd(i):
                pool.wait_ge(LN[i]["step"], 17)
                V.tensor_tensor(rstd[:], vareps[:], neghalf[:, 0:NB], ALU.pow).then_inc(LN[i]["rstd_ready"], 1)

            def ffn_low(i, c, slot):
                pool.wait_ge(FF[i]["whi_ready"], c + 1)
                V.tensor_tensor(ffn_lo[:, slot], ffn_stage[:, slot], ffn_hi[:, slot].bitcast(F32), ALU.subtract)\
                 .then_inc(FF[i]["wlo_ready"], 1)

            def ffn(i, n):
                for c in range(2):
                    ffn_low(i, c, c)
                if n > 4:
                    with pool.Fori(2, n - 1, 2) as c:
                        ffn_low(i, c, 0)
                        ffn_low(i, c + 1, 1)
                    ffn_low(i, n - 1, 0)
                else:
                    for c in range(2, n):
                        ffn_low(i, c, c % 2)

            ln_rstd(0)
            ffn(0, CH0)

            def low(name, lo, stage, hi, g):
                pool.wait_ge(S[f"{name}_hi_ready"], g + 1)
                V.tensor_tensor(lo[:], stage[:], hi[:].bitcast(F32), ALU.subtract).then_inc(S[f"{name}_lo_ready"], 1)

            def q_rstd(g, half):
                pool.wait_ge(S["qvar_ready"], 2 * g + half + 1)
                V.tensor_tensor(rq[:, half], qvar[:], neghalf[:].rearrange("p (a b) -> p a b", b=GROUP)[:, 0:4],
                                ALU.pow).then_inc(S["rq_ready"], 1)

            def normalise(g, b):
                pool.wait_ge(S["rden_ready"], NB * g + b + 1)
                V.tensor_tensor(prob[:, b % 4], prob[:, b % 4],
                                rden1[:, b].unsqueeze(2).broadcast_to([P, GROUP, P]), ALU.mult)\
                 .then_inc(S["pn_ready"], 1)

            def att_step(g, last=False):
                low("kT", kT_lo, kT_stage, kT_hi, g)
                q_rstd(g, 0)
                low("v", v_lo, v_stage, v_hi, g)
                for b in range(4):
                    normalise(g, b)
                low("wo", wo_lo, wo_stage, wo_hi, g)
                q_rstd(g, 1)
                if not last:
                    low("wq", wq_lo, wq_stage, wq_hi, g + 1)
                for b in range(4, 8):
                    normalise(g, b)
            low("wq", wq_lo, wq_stage, wq_hi, 0)
            ln_rstd(1)
            with pool.Fori(0, KVH - 1) as g:
                att_step(g)
            att_step(KVH - 1, last=True)
            ln_rstd(2)
            ffn(1, CH1)

        @block.scalar
        def _(act):
            def copy(o, i):
                return nc.scalar.activation(o, i, ACT.Copy)

            act.wait_ge(S["const_in"], 16 * 8)
            copy(wst_hi[:], wst_stage[:]).then_inc(S["wst_hi_ready"], 1)
            copy(mask_sel[:], mask_sel_s[:]).then_inc(S["wst_hi_ready"], 1)
            copy(wo0_hi[:], wo0_stage[:]).then_inc(S["wo0_split"], 1)
            act.wait_ge(S["ctxT_in"], 16)
            copy(ctxT_hi[:], ctxT_stage[:]).then_inc(S["th_ready"], 1)
            act.wait_ge(S["xn_ready"], 1)
            copy(xn0_hi[:], xn0[:]).then_inc(S["xh_ready"], 1)
            act.wait_ge(S["kvw_in0"], 16)
            copy(wkv_hi[:, 0], kv_stage).then_inc(S["kvw_hi_ready"], 1)
            act.wait_ge(S["kvw_in1"], 16)
            copy(wkv_hi[:, 1], kv_stage).then_inc(S["kvw_hi_ready"], 1)
            act.wait_ge(S["col_ready"], 1)
            act.wait_ge(S["factor_ready"], 1)

            def evac_t0(pair, r):
                act.wait_ge(S["t0_done"], 4 * pair + r + 1)
                wait(act, S["pv0_done"], pair)
                copy(pT0[:, r], ps[:, 4 + r % 2].rearrange("p (s n) -> p s n", s=4)).then_inc(S["t0_by_act"], 1)

            def exp0(pair, q):
                act.wait_ge(S["sub0_ready"], pair + 1)
                nc.scalar.activation(work0[:, q], work0[:, q], ACT.Exp, scale=float(DH0) ** -0.5)\
                  .then_inc(S["exp0_ready"], 1)

            def l0_step(b, first=False, last=False):
                wait(act, S["knorm_ready"], b)
                for n, bank in ((0, A_BANK), (1, B_BANK)):
                    act.wait_ge(S["k_done"], 2 * b + n + 1)
                    copy(k_raw[:, 4 * n:4 * n + 4], ps[:, bank].rearrange("p (h d) -> p h d", h=4))\
                        .then_inc(S["k_copied"], 1)
                if not first:
                    evac_t0(2 * b - 1, 0)
                    evac_t0(2 * b - 1, 2)
                wait(act, S["stack_ready"], 4 * b)
                for n, bank in enumerate((B_BANK, A_BANK, B_BANK, A_BANK)):
                    act.wait_ge(S["stack_done"], 4 * b + n + 1)
                    nc.scalar.activation(neg_hi[:, n], ps[:, bank], ACT.Identity, bias=stack_col[:, 6 + n:7 + n],
                                         scale=stack_col[:, 4 + n % 2:5 + n % 2]).then_inc(S["neghi_ready"], 1)
                act.wait_ge(S["k_copied"], 2 * b + 2)
                for h in range(KVH):
                    last_sq = nc.scalar.activation(k_norm[:, h], k_raw[:, h], ACT.Square, accum_out=ksum[:, h:h + 1])
                last_sq.then_inc(S["ksum_ready"], 1)
                wait(act, S["v_written"], 16 * b)
                for n, bank in ((0, A_BANK), (1, B_BANK)):
                    act.wait_ge(S["v_done"], 2 * b + n + 1)
                    copy(v_out[:, 4 * n:4 * n + 4], ps[:, bank].rearrange("p (h d) -> p h d", h=4))\
                        .then_inc(S["v_copied"], 1)
                exp0(2 * b, 0)
                wait(act, S["kT_written"], 16 * b)
                for n, bank in ((0, A_BANK), (1, B_BANK)):
                    act.wait_ge(S["kT_done"], 2 * b + n + 1)
                    nc.scalar.activation(kT_out[:, 4 * n:4 * n + 4], ps[:, bank].rearrange("p (h d) -> p h d", h=4),
                                         ACT.Copy, scale=knorm_w[:, 2:3]).then_inc(S["kT_copied"], 1)
                if not last:
                    act.wait_ge(S["ctxT_in"], 16 * (b + 2))
                    copy(ctxT_hi[:], ctxT_stage[:]).then_inc(S["th_ready"], 1)
                    act.wait_ge(S["xn_ready"], b + 2)
                    copy(xn0_hi[:], xn0[:]).then_inc(S["xh_ready"], 1)
                evac_t0(2 * b, 0)
                evac_t0(2 * b, 2)
                exp0(2 * b + 1, 1)

            l0_step(0, first=True)
            with act.Fori(1, NB - 1) as b:
                l0_step(b)
            l0_step(NB - 1, last=True)
            evac_t0(2 * NB - 1, 0)
            evac_t0(2 * NB - 1, 2)
            for b in range(NB):
                act.wait_ge(S["oT0_done"], b + 1)
                if b >= 2:
                    act.wait_ge(S["gello_ready"], b - 1)
                nc.scalar.activation(gel[:, b % 2], ps[0:E0, b % 2], ACT.Gelu).then_inc(S["gelu_ready"], 1)
                act.wait_ge(S["gelu_ready"], b + 1)
                if b >= 2:
                    act.wait_ge(S["wo0_done"], b - 1)
                copy(gel_hi[:, b % 2], gel[:, b % 2]).then_inc(S["gelhi_ready"], 1)

            def ln(i):
                for t in range(NB):
                    act.wait_ge(LN[i]["t_done"], t + 1)
                    copy(hT_hi[:, :, t * P:(t + 1) * P], ps[:, t % 2].rearrange("p (k n) -> p k n", k=KC))\
                        .then_inc(LN[i]["hi_ready"], 1)

            def ffn_high(i, c, slot):
                act.wait_ge(FF[i][f"w_in{slot}"], 8 * c + (8 if slot else 16))
                wait(act, FF[i]["down_done"], NB * (c - 1))
                copy(ffn_hi[:, slot], ffn_stage[:, slot]).then_inc(FF[i]["whi_ready"], 1)

            def ffn_act(i, c, slot, prefetch):
                for half in range(2):
                    act.wait_ge(FF[i]["gu_done"], 2 * c + half + 1)
                    wait(act, FF[i]["gated_ready"], 2 * c + half - 1)
                    bias = b12[:, 0, c:c + 1] if i == 1 else 0.0
                    nc.scalar.activation(silu[:, half], ps[:, half], ACT.Silu, bias=bias)\
                      .then_inc(FF[i]["silu_ready"], 1)
                    act.wait_ge(FF[i]["gated_ready"], 2 * c + half + 1)
                    wait(act, FF[i]["down_done"], NB * (c - 1) + 4 + 4 * half)
                    copy(gT_hi[:, half], gated[:, half]).then_inc(FF[i]["ghi_ready"], 1)
                    if half == 0 and prefetch:
                        ffn_high(i, c + 1, 1 - slot)

            def ffn(i, n):
                ffn_high(i, 0, 0)
                ffn_act(i, 0, 0, True)
                if n > 4:
                    with act.Fori(1, n - 2, 2) as c:
                        ffn_act(i, c, 1, True)
                        ffn_act(i, c + 1, 0, True)
                    ffn_act(i, n - 2, 1, True)
                    ffn_act(i, n - 1, 0, False)
                else:
                    for c in range(1, n):
                        ffn_act(i, c, c % 2, c < n - 1)

            act.wait_ge(S["kT_written"], 16 * NB)
            act.wait_ge(S["v_written"], 16 * NB)
            ln(0)
            ffn(0, CH0)

            def high(name, hi, stage, g):
                act.wait_ge(S[f"{name}_in"], 16 * (g + 1))
                copy(hi[:], stage[:]).then_inc(S[f"{name}_hi_ready"], 1)

            def q_out(g, half, h):
                n = 8 * g + 4 * half + h
                act.wait_ge(S["q_done"], n + 1)
                wait(act, S["ss_done"], n - 3)
                nc.scalar.activation(q_sq[:, h], ps[:, h % 2], ACT.Square).then_inc(S["sq_ready"], 1)
                if h == 0:
                    wait(act, S["s_done"], 8 * g + 4 * half)
                copy(qT_hi[:, h], ps[:, h % 2]).then_inc(S["qhi_ready"], 1)

            def exps(g, b):
                act.wait_ge(S["negmax_ready"], 8 * g + b + 1)
                for h in range(GROUP):
                    e = nc.scalar.activation(prob[:, b % 4, h], prob[:, b % 4, h], ACT.Exp,
                                             bias=negmax[:, b, h:h + 1], accum_out=psum1[:, b, h:h + 1])
                e.then_inc(S["exp_ready"], 1)

            def p_part(g, b):
                n = 8 * g + b
                act.wait_ge(S["t_done"], n + 1)
                wait(act, S["pv_done"], n - 1)
                copy(pT_hi[:, b % 2], ps[:, 4]).then_inc(S["pthi_ready"], 1)

            def o_high(g, b):
                n = 8 * g + b
                act.wait_ge(S["pv_done"], n + 1)
                wait(act, S["wo_done"], n - 3)
                copy(oT_hi[:, b % 4], ps[:, 5].rearrange("p (h n) -> p h n", h=GROUP)).then_inc(S["ohi_ready"], 1)

            def att_step(g, first=False, last=False):
                if first:
                    high("kT", kT_hi, kT_stage, g)
                for j in range(4):
                    q_out(g, 0, j)
                    if not first:
                        p_part(g - 1, 4 + j)
                        if j == 0:
                            high("kT", kT_hi, kT_stage, g)
                        else:
                            o_high(g - 1, 3 + j)
                if not first:
                    o_high(g - 1, 7)
                high("v", v_hi, v_stage, g)
                for j in range(4):
                    exps(g, j)
                if not first:
                    act.wait_ge(S["wo_done"], 8 * g)
                high("wo", wo_hi, wo_stage, g)
                for j in range(4):
                    q_out(g, 1, j)
                    p_part(g, j)
                    if j >= 1:
                        o_high(g, j - 1)
                o_high(g, 3)
                if not last:
                    act.wait_ge(S["q_done"], 8 * g + 8)
                    high("wq", wq_hi, wq_stage, g + 1)
                for j in range(4, 8):
                    exps(g, j)

            high("wq", wq_hi, wq_stage, 0)
            ln(1)
            att_step(0, first=True)
            with act.Fori(1, KVH - 1) as g:
                att_step(g)
            att_step(KVH - 1, last=True)
            for j in range(4):
                p_part(KVH - 1, 4 + j)
                if j >= 1:
                    o_high(KVH - 1, 3 + j)
            o_high(KVH - 1, 7)
            ln(2)
            ffn(1, CH1)

        @block.vector
        def _(dve):
            V = nc.vector

            dve.wait_ge(S["const_in"], 16 * 8)
            V.tensor_scalar(knorm_w[:, 2:3], knorm_w[:, 0:1], knorm_w[:, 1:2], float(HD) ** -0.5,
                            ALU.mult, ALU.mult).then_inc(S["factor_ready"], 1)
            V.tensor_tensor(stack_col[:, 6:10].rearrange("p (a b) -> p a b", b=2),
                            stack_col[:, 0:4].rearrange("p (a b) -> p a b", b=2),
                            stack_col[:, 4:6].unsqueeze(1).broadcast_to([P, 2, 2]), ALU.mult)\
             .then_inc(S["col_ready"], 1)

            def layer_stats(s, before):
                for t in range(NB):
                    before(t)
                    V.bn_stats(stats[:, t], x[:, t]).then_inc(s, 1)
                for t in range(NB):
                    dve.wait_ge(s, t + 1)
                    a = V.bn_aggr(meanvar[:, t], stats[:, t])
                    a.then_inc(s, 1)
                dve.wait_ge(s, 2 * NB)
                V.tensor_scalar(vareps[:], meanvar[:, :, 1], EPS, None, ALU.add).then_inc(s, 1)

            layer_stats(S["stat_step"], lambda t: dve.wait_ge(S["x_in"], 16) if t == 0 else None)

            def normal0(b):
                wait(dve, S["xl_ready"], b)
                V.tensor_scalar(xn0[:], x[:, bass.ds(b, 1)].rearrange("p a s -> p (a s)"),
                                meanvar[:, bass.ds(b, 1), 0:1].rearrange("p a s -> p (a s)"),
                                rstd[:, bass.ds(b, 1)], ALU.subtract, ALU.mult).then_inc(S["xn_ready"], 1)
                dve.wait_ge(S["mask_in"], 16 * (b + 1))
                V.tensor_scalar(mask_step[:], mask_row[:], 0.0, -MASKED, ALU.is_gt, ALU.mult)\
                 .then_inc(S["maskb_ready"], 1)
                dve.wait_ge(S["maskb_ready"], 2 * b + 1)
                wait(dve, S["stack_done"], 4 * b)
                V.tensor_scalar(mask_bias[:], mask_step[:], MASKED, None, ALU.add).then_inc(S["maskb_ready"], 1)
            dve.wait_ge(S["l0_rstd_ready"], 1)
            normal0(0)
            dve.wait_ge(S["vaug_ready"], 1)
            dve.wait_ge(S["wo0_split"], 1)
            V.tensor_tensor(wo0_lo[:], wo0_stage[:], wo0_hi[:].bitcast(F32), ALU.subtract).then_inc(S["wo0_split"], 1)
            dve.wait_ge(S["kvw_lo_ready"], 2)

            def evac_t0(pair, r):
                dve.wait_ge(S["t0_done"], 4 * pair + r + 1)
                wait(dve, S["pv0_done"], pair)
                V.tensor_copy(pT0[:, r], ps[:, 4 + r % 2].rearrange("p (s n) -> p s n", s=4))\
                 .then_inc(S["t0_by_dve"], 1)

            def out0(b, pair, q, bank):
                dve.wait_ge(S["pv0_done"], pair + 1)
                pv = ps[:, bank, 0:2 * H0 * (DH0 + 1)].rearrange("p (s h e) -> p s h e", s=2, h=H0)
                V.reciprocal(rden0[:].unsqueeze(3), pv[:, :, :, DH0:DH0 + 1]).then_inc(S["rden0_ready"], 1)
                dve.wait_ge(S["rden0_ready"], pair + 1)
                o = o_all[:, bass.ds(NPATCH * b + 2 * q, 2)].rearrange("p s (h e) -> p s h e", e=DH0)
                V.tensor_tensor(o, pv[:, :, :, 0:DH0], rden0[:].unsqueeze(3).broadcast_to([P, 2, H0, DH0]), ALU.mult)\
                 .then_inc(S["o0_ready"], 1)

            def soft0(pair, q):
                dve.wait_ge(S["s0_done"], pair + 1)
                flat = ps[:, 0:4].rearrange("p a (s n) -> p (a s) n", n=P)
                V.tensor_reduce(smax0[:], flat, AX_X, ALU.max).then_inc(S["max0_ready"], 1)
                dve.wait_ge(S["max0_ready"], pair + 1)
                wait(dve, S["t0_done"], 4 * (pair - 1))
                V.tensor_tensor(work0[:, q].rearrange("p a s n -> p (a s) n"), flat,
                                smax0[:].unsqueeze(2).broadcast_to([P, 16, P]), ALU.subtract)\
                 .then_inc(S["sub0_ready"], 1)

            def l0_step(b, first=False, last=False):
                if not first:
                    evac_t0(2 * b - 1, 1)
                    evac_t0(2 * b - 1, 3)
                    out0(b - 1, 2 * b - 1, 1, A_BANK)
                wait(dve, S["s0_done"], 2 * b)
                for n, bank in enumerate((B_BANK, A_BANK, B_BANK, A_BANK)):
                    dve.wait_ge(S["neghi_ready"], 4 * b + n + 1)
                    dst = (k_stack, q_stack)[n % 2][:, n // 2]
                    V.scalar_tensor_tensor(dst, ps[:, bank], stack_col[:, n:n + 1], neg_hi[:, n].bitcast(F32),
                                           ALU.add, ALU.add).then_inc(S["stack_ready"], 1)
                dve.wait_ge(S["v0_done"], b + 1)
                V.tensor_tensor(v_aug[:, :, :, 0:DH0],
                                ps[:, B_BANK, 0:NPATCH * E0].rearrange("p (s h e) -> p s h e", s=NPATCH, h=H0),
                                bv0[:].rearrange("p (h e) -> p h e", e=DH0).unsqueeze(1)
                                .broadcast_to([P, NPATCH, H0, DH0]), ALU.add).then_inc(S["v0_ready"], 1)
                dve.wait_ge(S["ksum_ready"], b + 1)
                V.tensor_scalar(kvar[:], ksum[:], 1.0 / HD, EPS, ALU.mult, ALU.add).then_inc(S["krstd_step"], 1)
                soft0(2 * b, 0)
                if not last:
                    normal0(b + 1)
                soft0(2 * b + 1, 1)
                evac_t0(2 * b, 1)
                evac_t0(2 * b, 3)
                out0(b, 2 * b, 0, A_BANK)

            l0_step(0, first=True)
            with dve.Fori(1, NB - 1) as b:
                l0_step(b)
            l0_step(NB - 1, last=True)
            evac_t0(2 * NB - 1, 1)
            evac_t0(2 * NB - 1, 3)
            out0(NB - 1, 2 * NB - 1, 1, A_BANK)

            def gel_low(b):
                dve.wait_ge(S["gelhi_ready"], b + 1)
                V.tensor_tensor(gel_lo[:, b % 2], gel[:, b % 2], gel_hi[:, b % 2].bitcast(F32), ALU.subtract)\
                 .then_inc(S["gello_ready"], 1)

            def add0(b):
                dve.wait_ge(S["wo0_done"], b + 1)
                dve.wait_ge(S[f"maskb_in{b % 2}"], 16 * (b // 2 + 1))
                V.scalar_tensor_tensor(delta0[:, b % 2], ps[:, 2 + b % 2], bo0[:], mask_b[:, b % 2],
                                       ALU.add, ALU.mult).then_inc(S["delta0_ready"], 1)
                dve.wait_ge(S["delta0_ready"], b + 1)
                V.tensor_tensor(x[:, b], x[:, b], delta0[:, b % 2], ALU.add).then_inc(S["x0_ready"], 1)
            gel_low(0)
            for b in range(NB):
                if b + 1 < NB:
                    gel_low(b + 1)
                add0(b)

            def ln(i, before):
                layer_stats(LN[i]["step"], before)
                dve.wait_ge(LN[i]["rstd_ready"], 1)

                def xn_tile(t):
                    if t >= 2:
                        dve.wait_ge(LN[i]["t_done"], t - 1)
                    V.tensor_scalar(xn[:, t % 2], x[:, t], meanvar[:, t, 0:1], rstd[:, t:t + 1],
                                    ALU.subtract, ALU.mult).then_inc(LN[i]["xn_ready"], 1)
                xn_tile(0)
                for t in range(NB):
                    if t + 1 < NB:
                        xn_tile(t + 1)
                    dve.wait_ge(LN[i]["hi_ready"], t + 1)
                    V.tensor_tensor(hT_lo[:, :, t * P:(t + 1) * P], ps[:, t % 2].rearrange("p (k n) -> p k n", k=KC),
                                    hT_hi[:, :, t * P:(t + 1) * P].bitcast(F32), ALU.subtract)\
                     .then_inc(LN[i]["lo_ready"], 1)

            def ffn_gate(i, c, half):
                dve.wait_ge(FF[i]["silu_ready"], 2 * c + half + 1)
                bias = b12[:, 1, c:c + 1] if i == 1 else 0.0
                wait(dve, FF[i]["glo_ready"], 2 * c + half - 1)
                V.scalar_tensor_tensor(gated[:, half], ps[:, 2 + half], bias, silu[:, half], ALU.add, ALU.mult)\
                 .then_inc(FF[i]["gated_ready"], 1)
                dve.wait_ge(FF[i]["ghi_ready"], 2 * c + half + 1)
                V.tensor_tensor(gT_lo[:, half], gated[:, half], gT_hi[:, half].bitcast(F32), ALU.subtract)\
                 .then_inc(FF[i]["glo_ready"], 1)

            def ffn_add(i, c, half):
                for t in range(4 * half, 4 * half + 4):
                    dve.wait_ge(FF[i]["down_done"], NB * c + t + 1)
                    V.tensor_tensor(x[:, t], x[:, t], ps[:, 4 + t % 4], ALU.add).then_inc(FF[i]["x_added"], 1)

            def ffn_step(i, c, first=False):
                ffn_gate(i, c, 0)
                if not first:
                    ffn_add(i, c - 1, 1)
                ffn_gate(i, c, 1)
                ffn_add(i, c, 0)

            def ffn(i, n):
                ffn_step(i, 0, first=True)
                if n > 4:
                    with dve.Fori(1, n) as c:
                        ffn_step(i, c)
                else:
                    for c in range(1, n):
                        ffn_step(i, c)
                ffn_add(i, n - 1, 1)

            ln(0, lambda t: dve.wait_ge(S["x0_ready"], t + 1))
            ffn(0, CH0)

            def q_low(g, half, h):
                n = 8 * g + 4 * half + h
                dve.wait_ge(S["qhi_ready"], n + 1)
                V.tensor_tensor(qT_lo[:, h], ps[:, h % 2], qT_hi[:, h].bitcast(F32), ALU.subtract)\
                 .then_inc(S["qlo_ready"], 1)

            def q_var(g, half):
                dve.wait_ge(S["ss_done"], 8 * g + 4 * half + 4)
                wait(dve, S["rq_ready"], 2 * g + half)
                V.tensor_scalar(qvar[:], ps[:, 7, 0:16].rearrange("p (b h) -> p b h", b=4), 1.0 / HD, EPS,
                                ALU.mult, ALU.add).then_inc(S["qvar_ready"], 1)

            def soft(g, b):
                n = 8 * g + b
                dve.wait_ge(S["s_done"], n + 1)
                dve.wait_ge(S["rq_ready"], 2 * g + b // 4 + 1)
                wait(dve, S["t_done"], n - 3)
                for h in range(GROUP):
                    m = V.scalar_tensor_tensor(prob[:, b % 4, h], ps[:, 2 + b % 2, h * P:(h + 1) * P],
                                               rq[:, b // 4, b % 4, h:h + 1], mask1[:], ALU.mult, ALU.add)
                m.then_inc(S["masked_ready"], 1)
                dve.wait_ge(S["masked_ready"], n + 1)
                V.tensor_reduce(negmax[:, b], prob[:, b % 4], AX_X, ALU.max, negate=True)\
                 .then_inc(S["negmax_ready"], 1)

            def denominators(g, b):
                n = 8 * g + b
                dve.wait_ge(S["exp_ready"], n + 1)
                V.reciprocal(rden1[:, b], psum1[:, b]).then_inc(S["rden_ready"], 1)

            def p_part(g, b):
                n = 8 * g + b
                dve.wait_ge(S["pthi_ready"], n + 1)
                V.tensor_tensor(pT_lo[:, b % 2], ps[:, 4], pT_hi[:, b % 2].bitcast(F32), ALU.subtract)\
                 .then_inc(S["ptlo_ready"], 1)

            def o_low(g, b):
                n = 8 * g + b
                dve.wait_ge(S["ohi_ready"], n + 1)
                V.tensor_tensor(oT_lo[:, b % 4], ps[:, 5].rearrange("p (h n) -> p h n", h=GROUP),
                                oT_hi[:, b % 4].bitcast(F32), ALU.subtract).then_inc(S["olo_ready"], 1)

            def x_add(g, t):
                n = 8 * g + t
                dve.wait_ge(S["wo_done"], n + 1)
                V.tensor_tensor(x[:, t], x[:, t], ps[:, t % 2], ALU.add).then_inc(S["x_added"], 1)

            def att_step(g, first=False):
                for j in range(4):
                    q_low(g, 0, j)
                    if not first:
                        p_part(g - 1, 4 + j)
                        if j >= 1:
                            o_low(g - 1, 3 + j)
                if not first:
                    o_low(g - 1, 7)
                for j in range(4):
                    if not first:
                        x_add(g - 1, 4 + j)
                    if j == 0:
                        q_var(g, 0)
                    soft(g, j)
                    if j >= 1:
                        denominators(g, j - 1)
                denominators(g, 3)
                for j in range(4):
                    q_low(g, 1, j)
                    p_part(g, j)
                    if j >= 1:
                        o_low(g, j - 1)
                o_low(g, 3)
                for j in range(4):
                    x_add(g, j)
                    if j == 0:
                        q_var(g, 1)
                    soft(g, 4 + j)
                    if j >= 1:
                        denominators(g, 4 + j - 1)
                denominators(g, 7)

            ln(1, lambda t: dve.wait_ge(FF[0]["x_added"], NB * (CH0 - 1) + t + 1))
            dve.wait_ge(S["att_const_in"], 48)
            att_step(0, first=True)
            with dve.Fori(1, KVH) as g:
                att_step(g)
            for j in range(4):
                p_part(KVH - 1, 4 + j)
                if j >= 1:
                    o_low(KVH - 1, 3 + j)
            o_low(KVH - 1, 7)
            for j in range(4):
                x_add(KVH - 1, 4 + j)
            ln(2, lambda t: dve.wait_ge(S["x_added"], NB * (KVH - 1) + t + 1))
            V.tensor_tensor(x[:], x[:], b3[:].unsqueeze(1).broadcast_to([P, NB, D]), ALU.add).then_inc(S["stat_step"], 1)
            dve.wait_ge(S["stat_step"], 18)
            ffn(1, CH1)

        @block.tensor
        def _(pe):
            T = nc.tensor

            def three(o, w_hi, w_lo, m_hi, m_lo, start, stop):
                T.matmul(o, w_hi, m_hi, start=start, stop=False)
                T.matmul(o, w_hi, m_lo, start=False, stop=False)
                return T.matmul(o, w_lo, m_hi, start=False, stop=stop)

            def project(o, w, bank, done):
                for k in range(KC):
                    last = three(o, ctxT_hi[:, k], ctxT_lo[:, k], wkv_hi[:, w, k, bank * 512:(bank + 1) * 512],
                                 wkv_lo[:, w, k, bank * 512:(bank + 1) * 512], k == 0, k == KC - 1)
                last.then_inc(S[done], 1)

            def scores(pair, q):
                wait(pe, S["sub0_ready"], pair)
                for s in range(4):
                    grp, patch = s // 2, 2 * q + s % 2
                    for h in range(4):
                        rows = slice(STACK * h, STACK * h + STACK)
                        cols = slice(patch * P, patch * P + P)
                        last = T.matmul(scores0[:, h, s], q_stack[rows, grp, cols], k_stack[rows, grp, cols],
                                        start=True, stop=True)
                last.then_inc(S["s0_done"], 1)

            def spread(pair, q, bank):
                pe.wait_ge(S["exp0_ready"], pair + 1)
                pv = ps[:, bank, 0:2 * H0 * (DH0 + 1)].rearrange("p (s h e) -> p s h e", s=2, h=H0)

                def turn(r):
                    wait(pe, S[("t0_by_act", "t0_by_dve")[r % 2]], 2 * pair + r // 2)
                    for s in range(4):
                        last = T.transpose(ps[:, 4 + r % 2, s * P:(s + 1) * P], work0[:, q, r, s], ident[:])
                    last.then_inc(S["t0_done"], 1)

                def times_v(r):
                    pe.wait_ge(S[("t0_by_act", "t0_by_dve")[r % 2]], 2 * pair + r // 2 + 1)
                    for s in range(4):
                        head, patch = 4 * (s // 2) + r, s % 2
                        last = T.matmul(pv[:, patch, head], pT0[:, r, s], v_aug[:, 2 * q + patch, head],
                                        start=True, stop=True)
                    return last
                turn(0)
                turn(1)
                times_v(0)
                turn(2)
                times_v(1)
                turn(3)
                times_v(2)
                times_v(3).then_inc(S["pv0_done"], 1)

            def l0_step(b, first=False):
                pe.wait_ge(S["tl_ready"], b + 1)
                wait(pe, S["o0_ready"], 2 * b - 1)
                project(ps[:, A_BANK], 0, 0, "k_done")
                wait(pe, S["kT_copied"], 2 * b)
                project(ps[:, B_BANK], 0, 1, "k_done")
                if not first:
                    pe.wait_ge(S["k_copied"], 2 * b + 1)
                    spread(2 * b - 1, 1, A_BANK)
                pe.wait_ge(S["xl_ready"], b + 1)
                pe.wait_ge(S["maskb_ready"], 2 * b + 2)
                for n, bank in enumerate((B_BANK, A_BANK, B_BANK, A_BANK)):
                    if n == 0:
                        pe.wait_ge(S["k_copied"], 2 * b + 2)
                    elif n == 1:
                        pe.wait_ge(S["k_copied"], 2 * b + 1)
                        wait(pe, S["o0_ready"], 2 * b)
                    else:
                        pe.wait_ge(S["stack_ready"], 4 * b + n - 1)
                    last = three(ps[:, bank], wst_hi[:, n], wst_lo[:, n], xn0_hi[:], xn0_lo[:], True, n % 2 == 1)
                    if n % 2 == 0:
                        last = T.matmul(ps[:, bank], mask_sel[:], mask_bias[:],
                                        start=False, stop=True)
                    last.then_inc(S["stack_done"], 1)
                pe.wait_ge(S["ctx_in"], 16 * (b + 1))
                pe.wait_ge(S["stack_ready"], 4 * b + 3)
                for s in range(NPATCH):
                    last = T.matmul(ps[:, B_BANK, s * E0:(s + 1) * E0], ctx_nat[:, s * P:(s + 1) * P], wv0[:],
                                    start=True, stop=True)
                last.then_inc(S["v0_done"], 1)
                pe.wait_ge(S["stack_ready"], 4 * b + 4)
                project(ps[:, A_BANK], 1, 0, "v_done")
                scores(2 * b, 0)
                pe.wait_ge(S["v0_ready"], b + 1)
                project(ps[:, B_BANK], 1, 1, "v_done")
                pe.wait_ge(S["knorm_ready"], b + 1)
                for n, bank in ((0, A_BANK), (1, B_BANK)):
                    pe.wait_ge(S["v_copied"], 2 * b + n + 1)
                    for h in range(4):
                        last = T.transpose(ps[:, bank, h * P:(h + 1) * P], k_norm[:, 4 * n + h], ident[:])
                    last.then_inc(S["kT_done"], 1)
                scores(2 * b + 1, 1)
                pe.wait_ge(S["kT_copied"], 2 * b + 1)
                spread(2 * b, 0, A_BANK)

            pe.wait_ge(S["ident_ready"], 1)
            pe.wait_ge(S["wst_hi_ready"], 2)
            pe.wait_ge(S["wst_lo_ready"], 1)
            pe.wait_ge(S["kvw_lo_ready"], 2)
            pe.wait_ge(S["vaug_ready"], 1)
            l0_step(0, first=True)
            with pe.Fori(1, NB) as b:
                l0_step(b)
            pe.wait_ge(S["o0_ready"], 2 * NB - 1)
            spread(2 * NB - 1, 1, A_BANK)

            def turn_o(b):
                if b < 2:
                    pe.wait_ge(S["o0_ready"], 2 * NB)
                else:
                    pe.wait_ge(S["gelu_ready"], b - 1)
                for s in range(NPATCH):
                    last = T.transpose(ps[0:E0, b % 2, s * P:(s + 1) * P], o_all[:, NPATCH * b + s], ident[:])
                last.then_inc(S["oT0_done"], 1)
            turn_o(0)
            pe.wait_ge(S["wo0_split"], 2)
            for b in range(NB):
                if b + 1 < NB:
                    turn_o(b + 1)
                pe.wait_ge(S["gello_ready"], b + 1)
                wait(pe, S["delta0_ready"], b - 1)
                three(ps[:, 2 + b % 2], wo0_hi[:], wo0_lo[:], gel_hi[:, b % 2], gel_lo[:, b % 2], True, True)\
                    .then_inc(S["wo0_done"], 1)

            def ln(i):
                for t in range(NB):
                    pe.wait_ge(LN[i]["xn_ready"], t + 1)
                    wait(pe, LN[i]["lo_ready"], t - 1)
                    for k in range(KC):
                        last = T.transpose(ps[:, t % 2, k * P:(k + 1) * P], xn[:, t % 2, k * P:(k + 1) * P], ident[:])
                    last.then_inc(LN[i]["t_done"], 1)

            def gate_up(i, c, slot, half):
                pe.wait_ge(FF[i]["wlo_ready"], c + 1)
                wait(pe, FF[i]["gated_ready"], 2 * c + half - 1)
                for u, bank in ((0, half), (1, 2 + half)):
                    for k in range(KC):
                        cols = slice(u * D + k * P, u * D + (k + 1) * P)
                        toks = slice(half * HALF, (half + 1) * HALF)
                        last = three(ps[:, bank], ffn_hi[:, slot, cols], ffn_lo[:, slot, cols],
                                     hT_hi[:, k, toks], hT_lo[:, k, toks], k == 0, k == KC - 1)
                last.then_inc(FF[i]["gu_done"], 1)

            def down(i, c, slot, half):
                pe.wait_ge(FF[i]["glo_ready"], 2 * c + half + 1)
                for t in range(4 * half, 4 * half + 4):
                    wait(pe, FF[i]["x_added"], NB * c + t - 3)
                    toks = slice((t % 4) * P, (t % 4 + 1) * P)
                    three(ps[:, 4 + t % 4], gT_hi[:, half, toks], gT_lo[:, half, toks],
                          ffn_hi[:, slot, 2 * D:], ffn_lo[:, slot, 2 * D:], True, True)\
                        .then_inc(FF[i]["down_done"], 1)

            def ffn_step(i, c, slot, first=False):
                gate_up(i, c, slot, 0)
                if not first:
                    down(i, c - 1, 1 - slot, 1)
                gate_up(i, c, slot, 1)
                down(i, c, slot, 0)

            def ffn(i, n):
                pe.wait_ge(LN[i * 2]["lo_ready"], NB)
                ffn_step(i, 0, 0, first=True)
                if n > 4:
                    with pe.Fori(1, n, 2) as c:
                        ffn_step(i, c, 1)
                        ffn_step(i, c + 1, 0)
                else:
                    for c in range(1, n):
                        ffn_step(i, c, c % 2)
                down(i, n - 1, (n - 1) % 2, 1)

            ln(0)
            ffn(0, CH0)

            def square_sums(g, half, h):
                pe.wait_ge(S["sq_ready"], 8 * g + 4 * half + h + 1)
                if h == 0:
                    wait(pe, S["qvar_ready"], 2 * g + half)
                for b in range(4):
                    last = T.matmul(ps[:, 7, 4 * b + h:4 * b + h + 1], q_sq[:, h, b * P:(b + 1) * P], ones_col[:],
                                    start=True, stop=True)
                last.then_inc(S["ss_done"], 1)

            def score(g, b):
                n = 8 * g + b
                if b == 0:
                    pe.wait_ge(S["kT_lo_ready"], g + 1)
                if b % 4 == 0:
                    pe.wait_ge(S["qlo_ready"], n + 4)
                wait(pe, S["masked_ready"], n - 1)
                for h in range(GROUP):
                    q, k = slice((b % 4) * P, (b % 4 + 1) * P), slice(b * P, (b + 1) * P)
                    last = three(ps[:, 2 + b % 2, h * P:(h + 1) * P], qT_hi[:, h, q], qT_lo[:, h, q],
                                 kT_hi[:, k], kT_lo[:, k], True, True)
                last.then_inc(S["s_done"], 1)

            def turn_p(g, b):
                n = 8 * g + b
                pe.wait_ge(S["pn_ready"], n + 1)
                wait(pe, S["ptlo_ready"], n)
                for h in range(GROUP):
                    last = T.transpose(ps[:, 4, h * P:(h + 1) * P], prob[:, b % 4, h], ident[:])
                last.then_inc(S["t_done"], 1)

            def times_v(g, b):
                n = 8 * g + b
                if b == 0:
                    pe.wait_ge(S["v_lo_ready"], g + 1)
                pe.wait_ge(S["ptlo_ready"], n + 1)
                wait(pe, S["olo_ready"], n)
                three(ps[:, 5], v_hi[:, b], v_lo[:, b], pT_hi[:, b % 2], pT_lo[:, b % 2], True, True)\
                    .then_inc(S["pv_done"], 1)

            def output(g, t, after_output=False):
                n = 8 * g + t
                if t == 0:
                    pe.wait_ge(S["wo_lo_ready"], g + 1)
                pe.wait_ge(S["olo_ready"], n + 1)
                if t % 4 < 2 and not after_output:
                    pe.wait_ge(S["qlo_ready"], 8 * g + (7 if t < 4 else 11) + t % 4)
                else:
                    pe.wait_ge(S["x_added"], n - 1)
                for h in range(GROUP):
                    last = three(ps[:, t % 2], oT_hi[:, t % 4, h], oT_lo[:, t % 4, h], wo_hi[:, h], wo_lo[:, h],
                                 h == 0, h == GROUP - 1)
                last.then_inc(S["wo_done"], 1)

            def att_step(g, first=False):
                for j in range(4):
                    queries_after(g, 0, j, first)
                    if j >= 1:
                        square_sums(g, 0, j - 1)
                    if not first:
                        turn_p(g - 1, 4 + j)
                        if j >= 1:
                            times_v(g - 1, 3 + j)
                if not first:
                    times_v(g - 1, 7)
                for j in range(4):
                    if not first:
                        output(g - 1, 4 + j)
                    if j == 0:
                        square_sums(g, 0, 3)
                    score(g, j)
                for j in range(4):
                    queries_after(g, 1, j, first)
                    if j >= 1:
                        square_sums(g, 1, j - 1)
                    turn_p(g, j)
                    if j >= 1:
                        times_v(g, j - 1)
                times_v(g, 3)
                for j in range(4):
                    output(g, j)
                    if j == 0:
                        square_sums(g, 1, 3)
                    score(g, 4 + j)

            def queries_after(g, half, h, first):
                n = 8 * g + 4 * half + h
                pe.wait_ge(S["wq_lo_ready"], g + 1)
                if h >= 2:
                    pe.wait_ge(S["qlo_ready"], n - 1)
                elif half == 0 and not first:
                    pe.wait_ge(S["x_added"], 8 * g - 5 + h)
                elif half == 1 and not first:
                    pe.wait_ge(S["x_added"], 8 * g - 1 + h)
                elif half == 1:
                    pe.wait_ge(S["qlo_ready"], 3 + h)
                for k in range(KC):
                    toks = slice(half * HALF, (half + 1) * HALF)
                    last = three(ps[:, h % 2], wq_hi[:, h, k], wq_lo[:, h, k], hT_hi[:, k, toks], hT_lo[:, k, toks],
                                 k == 0, k == KC - 1)
                last.then_inc(S["q_done"], 1)

            ln(1)
            pe.wait_ge(LN[1]["lo_ready"], NB)
            att_step(0, first=True)
            with pe.Fori(1, KVH) as g:
                att_step(g)
            for j in range(4):
                turn_p(KVH - 1, 4 + j)
                if j >= 1:
                    times_v(KVH - 1, 3 + j)
            times_v(KVH - 1, 7)
            for j in range(4):
                output(KVH - 1, 4 + j, after_output=True)
            ln(2)
            ffn(1, CH1)


def kernel(**inputs):
    import numpy as np
    import concourse.bacc as _bacc
    from concourse.bass_utils import run_bass_kernel_spmd as _run

    a = {k: np.asarray(v) for k, v in inputs.items()}

    def chunks(w, rows=P):
        return np.ascontiguousarray(w.T.reshape(-1, P, w.shape[0]).transpose(1, 0, 2))

    def stack(w, group, parts):
        o = np.zeros((P,) + w.shape[1:], w.dtype)
        for h in range(4):
            for r in range(parts):
                at = STACK * h + DH0 * r
                o[at:at + DH0] = w[(4 * group + h) * DH0:(4 * group + h + 1) * DH0]
        return o

    wst = np.zeros((P, 4, P), np.float32)
    stack_col = np.zeros((P, 6), np.float32)
    mask_sel = np.zeros((1, P), np.float32)
    for grp in range(2):
        wst[:, 2 * grp] = stack(a["L0_xattn_Wk"], grp, 3).T
        wst[:, 2 * grp + 1] = stack(a["L0_xattn_Wq"], grp, 3).T
        stack_col[:, 2 * grp] = stack(a["L0_xattn_bk"], grp, 3)
        stack_col[:, 2 * grp + 1] = stack(a["L0_xattn_bq"], grp, 3)
        stack_col[3 * DH0::STACK, 2 * grp + 1] = 1.0
    for h in range(4):
        stack_col[STACK * h + DH0:STACK * h + 2 * DH0, 4] = -1.0
        stack_col[STACK * h + 2 * DH0:STACK * h + 3 * DH0, 5] = -1.0
    mask_sel[0, 3 * DH0::STACK] = 1.0

    def ffn(gate, up, down):
        n = -(-gate.shape[0] // P)
        o = np.zeros((n, P, 3 * D), np.float32)
        for u, w in enumerate((gate, up)):
            full = np.zeros((n * P, D), np.float32)
            full[:w.shape[0]] = w
            o[:, :, u * D:(u + 1) * D] = full.reshape(n, P, KC, P).transpose(0, 3, 2, 1).reshape(n, P, D)
        full = np.zeros((n * P, D), np.float32)
        full[:down.shape[1]] = down.T
        o[:, :, 2 * D:] = full.reshape(n, P, D)
        return o

    w12, b12 = a["L1_ffn_w12"], a["L1_ffn_b12"]
    arrays = {
        "x": a["x"],
        "ctx": a["ctx_4096"],
        "ctxT": chunks(a["ctx_4096"].reshape(TOK, D)),
        "mask": a["mask_Bx1x4096_ff1"],
        "mask_row": a["mask_Bx1x4096_ff1"].reshape(NB, D),
        "mask1": a["mask_1x1xSxS2_ff0"].reshape(P, P),
        "wst": wst,
        "stack_col": stack_col,
        "mask_sel": mask_sel,
        "wv0": a["L0_xattn_Wv"].T,
        "bv0": a["L0_xattn_bv"].reshape(1, E0),
        "wo0": a["L0_xattn_Wo"].T,
        "bo0": a["L0_xattn_bo"].reshape(P, 1),
        "ffn0": ffn(a["L0_ffn_w_gate"], a["L0_ffn_w_up"], a["L0_ffn_w_down"]),
        "wk": chunks(a["L1_xattn_Wk"]),
        "wv": chunks(a["L1_xattn_Wv"]),
        "wq": a["L1_xattn_Wq"].reshape(KVH, GROUP, P, KC, P).transpose(0, 4, 1, 3, 2),
        "wo": a["L1_xattn_Wo"].T.reshape(KVH, GROUP, HD, D).transpose(0, 2, 1, 3),
        "norm_w": np.stack([a["L1_xattn_q_norm_w"], a["L1_xattn_k_norm_w"]], 1),
        "ffn1": ffn(w12[:D], w12[D:], a["L1_ffn_w3"]),
        "b12": b12.reshape(2, CH1, P).transpose(2, 0, 1),
        "b3": a["L1_ffn_b3"].reshape(1, D),
    }
    nc = _bacc.Bacc("TRN2", target_bir_lowering=False, num_devices=1)
    feeds, A = {}, {}
    for name, v in arrays.items():
        v = np.ascontiguousarray(v)
        feeds[f"in_{name}"] = v
        A[name] = nc.dram_tensor(f"in_{name}", v.shape, mybir.dt.from_np(v.dtype), kind="ExternalInput").ap()
    out = nc.dram_tensor("out_0", (NB, P, D), F32, kind="ExternalOutput").ap()
    build(nc, A, out)
    r = _run(nc, [feeds], core_ids=[0])
    return r.results[0]["out_0"]
```

```python
from contextlib import ExitStack

import concourse.bass as bass
from concourse import mybir

F32 = mybir.dt.float32
FR = mybir.dt.float32r
ACT = mybir.ActivationFunctionType
ALU = mybir.AluOpType
AX_X = mybir.AxisListType.X

P = 128
NB = 8
D = 512
KC = D // P
TOK = NB * P
HALF = TOK // 2
EPS = 1e-5

H0, DH0 = 8, 8
E0 = H0 * DH0
STACK = 32
NPATCH = D // P
MASKED = -1e30

KVH, GROUP, HD = 8, 4, 128

INTER = 1376
CH0 = (INTER + P - 1) // P
CH1 = D // P


def wait(eng, sem, value):
    if isinstance(value, int) and value <= 0:
        return
    eng.wait_ge(sem, value)


def build(nc, A, out):
    with ExitStack() as ctx:
        def alloc(stack):
            return lambda name, shape, dt=F32: stack.enter_context(nc.sbuf_tensor(name, shape, dt))

        def sem(name):
            return ctx.enter_context(nc.semaphore(name))

        ps = ctx.enter_context(nc.psum_tensor("ps", [P, 8, 512], F32))

        g_ = alloc(ctx)
        x = g_("x", [P, NB, D])
        ffn_stage = g_("ffn_stage", [P, 2, 3 * D])
        ident = g_("ident", [P, P])
        ones_col = g_("ones_col", [P, 1])
        neghalf = g_("neghalf", [P, NB * 4])
        kv_stage = ffn_stage[:].rearrange("p a n -> p (a n)").rearrange("p (a n) -> p a n", n=KVH * HD)
        stats = g_("stats", [P, NB, 6])
        meanvar = g_("meanvar", [P, NB, 2])
        vareps = g_("vareps", [P, NB])
        rstd = g_("rstd", [P, NB])

        kT_dram = nc.dram_tensor("kT_scratch", (KVH, HD, TOK), F32, kind="Internal").ap()
        v_dram = nc.dram_tensor("v_scratch", (KVH, P, NB, HD), F32, kind="Internal").ap()

        with ExitStack() as l0:
            a_ = alloc(l0)
            wkv_hi = a_("wkv_hi", [P, 2, KC, KVH * HD], FR)
            wkv_lo = a_("wkv_lo", [P, 2, KC, KVH * HD], FR)
            work0 = a_("work0", [P, 2, 4, 4, P])
            pT0 = a_("pT0", [P, 4, 4, P])
            v_aug = a_("v_aug", [P, NPATCH, H0, DH0 + 1])
            v_next = a_("v_next", [P, 2, H0, DH0])
            smax0 = a_("smax0", [P, 16])
            rden0 = a_("rden0", [P, 2, H0])
            wst_stage = a_("wst_stage", [P, 4, P])
            wst_hi = a_("wst_hi", [P, 4, P], FR)
            wst_lo = a_("wst_lo", [P, 4, P], FR)
            stack_col = a_("stack_col", [P, 10])
            wv0 = a_("wv0", [P, E0])
            bv0 = a_("bv0", [P, E0])
            mask_sel = a_("mask_sel", [1, P], FR)
            mask_sel_s = a_("mask_sel_s", [1, P])
            mask_row = a_("mask_row", [1, 512])
            mask_step = a_("mask_step", [1, 512])
            mask_bias = a_("mask_bias", [1, 512], FR)
            knorm_w = a_("knorm_w", [P, 3])
            o_tile = a_("o_tile", [P, NPATCH, E0])
            mask_b = a_("mask_b", [P, 512])
            wo0_stage = a_("wo0_stage", [P, 2, P])
            wo0_hi = a_("wo0_hi", [P, 2, P], FR)
            wo0_lo = a_("wo0_lo", [P, 2, P], FR)
            bo0 = a_("bo0", [P, 1])
            gel = a_("gel", [P, 2, P])
            gel_hi = a_("gel_hi", [P, 2, P], FR)
            gel_lo = a_("gel_lo", [P, 2, P], FR)
            delta0 = a_("delta0", [P, 512])
            q_stack = a_("q_stack", [P, 2, 512], FR)
            k_stack = a_("k_stack", [P, 2, 512], FR)
            neg_hi = a_("neg_hi", [P, 4, 512], FR)
            xn0 = a_("xn0", [P, 512])
            xn0_hi = a_("xn0_hi", [P, 512], FR)
            xn0_lo = a_("xn0_lo", [P, 512], FR)
            ctxT_stage = a_("ctxT_stage", [P, KC, P])
            ctxT_hi = a_("ctxT_hi", [P, KC, P], FR)
            ctxT_lo = a_("ctxT_lo", [P, KC, P], FR)
            k_raw = a_("k_raw", [P, KVH, HD])
            k_norm = a_("k_norm", [P, KVH, HD])
            kT_out = a_("kT_out", [P, KVH, P])
            v_out = a_("v_out", [P, KVH, HD])
            ksum = a_("ksum", [P, KVH])
            kvar = a_("kvar", [P, KVH])
            krstd = a_("krstd", [P, KVH])
            ctx_nat = a_("ctx_nat", [P, 512])

        rest = ctx.enter_context(ExitStack())
        r_ = alloc(rest)
        hT_hi = r_("hT_hi", [P, KC, TOK], FR)
        hT_lo = r_("hT_lo", [P, KC, TOK], FR)
        xn = r_("xn", [P, 4, D])
        wq_stage = r_("wq_stage", [P, GROUP, KC, P])
        wo_stage = r_("wo_stage", [P, GROUP, D])
        kT = r_("kT", [P, TOK])
        v_stage = r_("v_stage", [P, NB, HD])
        wq_hi = r_("wq_hi", [P, GROUP, KC, P], FR)
        wq_lo = r_("wq_lo", [P, GROUP, KC, P], FR)
        wo_hi = r_("wo_hi", [P, GROUP, D], FR)
        wo_lo = r_("wo_lo", [P, GROUP, D], FR)
        v_hi = r_("v_hi", [P, NB, HD], FR)
        v_lo = r_("v_lo", [P, NB, HD], FR)
        prob = r_("prob", [P, 4, GROUP, P])
        pT_hi = r_("pT_hi", [P, 2, GROUP * P], FR)
        pT_lo = r_("pT_lo", [P, 2, GROUP * P], FR)
        mask1 = r_("mask1", [P, P])
        qvar = r_("qvar", [P, 4, GROUP])
        rq = r_("rq", [P, 2, 4, GROUP])
        negmax = r_("negmax", [P, NB, GROUP])
        psum1 = r_("psum1", [P, NB, GROUP])
        rden1 = r_("rden1", [P, NB, GROUP])
        b12 = r_("b12", [P, 2, CH1])
        b3 = r_("b3", [P, D])
        with ExitStack() as att:
            t_ = alloc(att)
            qT = t_("qT", [P, GROUP, HALF])
            q_sq = t_("q_sq", [P, GROUP, HALF])
            oT_hi = t_("oT_hi", [P, 4, GROUP, P], FR)
            oT_lo = t_("oT_lo", [P, 4, GROUP, P], FR)
        with ExitStack() as ff:
            t_ = alloc(ff)
            ffn_w = t_("ffn_w", [P, 2, 2, 3 * D], FR)
            ffn_hi, ffn_lo = ffn_w[:, :, 0], ffn_w[:, :, 1]
            silu = t_("silu", [P, 2, 512])
            gated = t_("gated", [P, 2, 512])
            gT_hi = t_("gT_hi", [P, 2, 512], FR)
            gT_lo = t_("gT_lo", [P, 2, 512], FR)

        names = """const_in x_in0 x_in kvw_in0 kvw_in1 kvw_in2 ctxT_in ctx_in mask_in maskb_ready maskb_in kT_written
            v_written const_ready ident_zero ident_ready col_ready wst_hi_ready wst_lo_ready kvw_hi_ready wk_lo_ready
            wv_lo_ready factor_ready stat_step l0_rstd_ready xn_ready xh_ready xl_ready th_ready tl_ready vaug_ready
            k_done k_copied ksum_ready krstd_step knorm_ready stack_done neghi_ready stack_ready v0_done
            v0_ready vnext_ready v_done v_copied kT_done kT_copied
            s0_done max0_ready sub0_ready exp0_ready t0_done t0_by_act t0_by_dve pv0_done rden0_ready o0_ready
            oT0_done gelu_ready gelhi_ready gello_ready wo0_done delta0_ready x0_ready wo0_split
            wq_in wo_in kT_in v_in att_const_in out_written
            wq_hi_ready wq_lo_ready wo_hi_ready wo_lo_ready v_hi_ready v_lo_ready
            q_done sq_ready q_copied ss_done qvar_ready rq_step rq_ready
            s_done masked_ready negmax_ready exp_ready rden_ready pn_ready
            t_done pthi_ready ptlo_ready pv_done ohi_ready olo_ready wo_done x_added result_ready""".split()
        S = {n: sem(n) for n in names}
        LN = [{n: sem(f"ln{i}_{n}") for n in ("step", "rstd_ready", "xn_ready", "t_done", "hi_ready", "lo_ready")}
              for i in range(3)]
        FF = [{n: sem(f"ffn{i}_{n}") for n in (
            "w_in0", "w_in1", "whi_ready", "wlo_ready", "gu_done", "silu_ready", "gated_ready", "ghi_ready",
            "glo_ready", "down_done", "x_added")} for i in range(2)]

        A_BANK, B_BANK = 6, 7
        T_BANKS = 4, 6
        LN_BANKS = (((1, 3), (1, 3)), ((2, 3), (2, 3)), ((2, 3), (1, 3)))
        STACKS = ((1, 4), (2, 5), (0, B_BANK), (3, A_BANK))
        scores0 = ps[:, 0:4, :].rearrange("p a (s n) -> p a s n", s=4)

        block = ctx.enter_context(nc.Block())

        @block.sync
        def _(sp):
            sp.dma_start(x[:, 0], A["x"][0]).then_inc(S["x_in0"], 16)
            for dst, src in ((wst_stage[:], A["wst"]), (stack_col[:, 0:6], A["stack_col"]), (wv0[:], A["wv0"]),
                             (mask_sel_s[:], A["mask_sel"]),
                             (bv0[:], A["bv0"].partition_broadcast(P)), (wo0_stage[:], A["wo0"]),
                             (bo0[:], A["bo0"]), (knorm_w[:, 0:2], A["norm_w"])):
                sp.dma_start(dst, src).then_inc(S["const_in"], 16)
            sp.dma_start(mask_row[:], A["mask_row"][0:1]).then_inc(S["mask_in"], 16)
            sp.dma_start(ctx_nat[:], A["ctx"][0]).then_inc(S["ctx_in"], 16)
            sp.dma_start(ctxT_stage[:], A["ctxT"][:, :, 0:P]).then_inc(S["ctxT_in"], 16)

            def kvw_load(c):
                wait(sp, S["wk_lo_ready"], min(c - 2, KC))
                wait(sp, S["wv_lo_ready"], c - 2 - KC)
                sp.dma_start(kv_stage[:, c % 3], A["wkv"][:, c]).then_inc(S[f"kvw_in{c % 3}"], 16)
            for c in range(3):
                kvw_load(c)
            sp.dma_start(x[:, 1:], A["x"][1:].rearrange("b p s -> p b s")).then_inc(S["x_in"], 16)

            def l0_loads(b):
                sp.wait_ge(S["maskb_ready"], 2 * b + 2)
                sp.dma_start(mask_row[:], A["mask_row"][bass.ds(b + 1, 1)]).then_inc(S["mask_in"], 16)
                sp.wait_ge(S["th_ready"], b + 1)
                sp.wait_ge(S["tl_ready"], b + 1)
                sp.dma_start(ctxT_stage[:], A["ctxT"][:, :, bass.ds((b + 1) * P, P)]).then_inc(S["ctxT_in"], 16)
                sp.wait_ge(S["v0_done"], b + 1)
                sp.dma_start(ctx_nat[:], A["ctx"][bass.ds(b + 1, 1)].rearrange("a p s -> p (a s)"))\
                  .then_inc(S["ctx_in"], 16)

            def l0_stores(b):
                sp.wait_ge(S["v_copied"], 2 * b + 2)
                sp.dma_start(v_dram[:, :, bass.ds(b, 1), :].rearrange("g p a d -> p g (a d)"), v_out[:])\
                  .then_inc(S["v_written"], 16)
                sp.wait_ge(S["kT_copied"], 2 * b + 2)
                sp.dma_start(kT_dram[:, :, bass.ds(b * P, P)].rearrange("g d t -> d g t"), kT_out[:])\
                  .then_inc(S["kT_written"], 16)
                wait(sp, S["delta0_ready"], b)
                sp.dma_start(mask_b[:], A["mask"][bass.ds(b, 1)].rearrange("a o s -> (a o) s")
                             .partition_broadcast(P)).then_inc(S["maskb_in"], 16)

            for c in range(3, 7):
                kvw_load(c)
            l0_loads(0)
            kvw_load(7)
            l0_stores(0)
            sp.wait_ge(S["wv_lo_ready"], KC)
            for c in range(2):
                sp.dma_start(ffn_stage[:, c], A["ffn0"][c]).then_inc(FF[0][f"w_in{c}"], 16)
            l0_loads(1)
            l0_stores(1)
            with sp.Fori(2, NB - 1) as b:
                l0_loads(b)
                l0_stores(b)
            l0_stores(NB - 1)

            def ffn_load(i, c, slot):
                sp.wait_ge(FF[i]["wlo_ready"], c - 1)
                sp.dma_start(ffn_stage[:, slot], A[f"ffn{i}"][bass.ds(c, 1)].rearrange("a p n -> p (a n)"))\
                  .then_inc(FF[i][f"w_in{slot}"], 16)
            ffn_load(0, 2, 0)
            sp.wait_ge(S["x0_ready"], NB)
            sp.dma_start(mask1[:], A["mask1"]).then_inc(S["att_const_in"], 16)
            sp.dma_start(b12[:], A["b12"]).then_inc(S["att_const_in"], 16)
            sp.dma_start(b3[:], A["b3"].partition_broadcast(P)).then_inc(S["att_const_in"], 16)
            sp.wait_ge(S["kT_written"], 16 * NB)
            sp.wait_ge(S["v_written"], 16 * NB)

            def att_load(g):
                wait(sp, S["wq_lo_ready"], g)
                sp.dma_start(wq_stage[:], A["wq"][bass.ds(g, 1)].rearrange("a p h k n -> p (a h) k n"))\
                  .then_inc(S["wq_in"], 16)
                wait(sp, S["s_done"], 8 * g)
                sp.dma_start(kT[:], kT_dram[bass.ds(g, 1)].rearrange("a p n -> p (a n)")).then_inc(S["kT_in"], 16)
                wait(sp, S["v_lo_ready"], g)
                sp.dma_start(v_stage[:], v_dram[bass.ds(g, 1)].rearrange("a p b d -> p (a b) d")).then_inc(S["v_in"], 16)
                wait(sp, S["wo_lo_ready"], g)
                sp.dma_start(wo_stage[:], A["wo"][bass.ds(g, 1)].rearrange("a p h n -> p (a h) n"))\
                  .then_inc(S["wo_in"], 16)
            att_load(0)
            with sp.Fori(3, CH0 - 1, 2) as c:
                ffn_load(0, c, 1)
                ffn_load(0, c + 1, 0)
            with sp.Fori(1, KVH) as g:
                att_load(g)
            sp.wait_ge(FF[0]["wlo_ready"], CH0)
            for c in range(2):
                sp.dma_start(ffn_stage[:, c], A["ffn1"][c]).then_inc(FF[1][f"w_in{c}"], 16)
            for c in range(2, CH1):
                ffn_load(1, c, c % 2)
            for t in range(NB):
                sp.wait_ge(S["result_ready"], t + 1)
                sp.dma_start(out[t], x[:, t]).then_inc(S["out_written"], 16)
            sp.wait_ge(S["out_written"], 16 * NB)

        @block.gpsimd
        def _(pool):
            V = nc.gpsimd
            V.memset(ident[:], 0.0).then_inc(S["ident_zero"], 1)
            V.memset(neghalf[:], -0.5).then_inc(S["const_ready"], 1)
            V.memset(ones_col[:], 1.0).then_inc(S["const_ready"], 1)
            V.memset(v_aug[:], 1.0).then_inc(S["vaug_ready"], 1)
            pool.wait_ge(S["ident_zero"], 1)
            V.affine_select(out=ident[:], in_=ident[:], compare_op=ALU.not_equal, fill=1.0, base=0,
                            pattern=[[-1, P]], channel_multiplier=1).then_inc(S["ident_ready"], 1)
            pool.wait_ge(S["wst_hi_ready"], 1)
            V.tensor_tensor(wst_lo[:], wst_stage[:], wst_hi[:].bitcast(F32), ALU.subtract).then_inc(S["wst_lo_ready"], 1)
            pool.wait_ge(S["const_ready"], 2)
            pool.wait_ge(S["stat_step"], 3)
            V.tensor_tensor(rstd[:, 0:1], vareps[:, 0:1], neghalf[:, 0:1], ALU.pow).then_inc(S["l0_rstd_ready"], 1)

            def x_low(b):
                pool.wait_ge(S["xh_ready"], b + 1)
                V.tensor_tensor(xn0_lo[:], xn0[:], xn0_hi[:].bitcast(F32), ALU.subtract).then_inc(S["xl_ready"], 1)

            def t_low(b):
                pool.wait_ge(S["th_ready"], b + 1)
                V.tensor_tensor(ctxT_lo[:], ctxT_stage[:], ctxT_hi[:].bitcast(F32), ALU.subtract)\
                 .then_inc(S["tl_ready"], 1)

            def gel_low(b):
                pool.wait_ge(S["gelhi_ready"], b + 1)
                wait(pool, S["wo0_done"], b)
                V.tensor_tensor(gel_lo[:], gel[:], gel_hi[:].bitcast(F32), ALU.subtract).then_inc(S["gello_ready"], 1)
            x_low(0)
            t_low(0)
            for k in range(KC):
                if k == KC - 1:
                    pool.wait_ge(S["stat_step"], 3 + 2 * (NB - 1) + 1)
                    V.tensor_tensor(rstd[:, 1:], vareps[:, 1:], neghalf[:, 1:NB], ALU.pow)\
                     .then_inc(S["l0_rstd_ready"], 1)
                pool.wait_ge(S["kvw_hi_ready"], KC + k + 1)
                V.tensor_tensor(wkv_lo[:, 1, k], kv_stage[:, (KC + k) % 3], wkv_hi[:, 1, k].bitcast(F32), ALU.subtract)\
                 .then_inc(S["wv_lo_ready"], 1)

            def l0_step(b, first=False, last=False):
                if not last:
                    x_low(b + 1)
                pool.wait_ge(S["krstd_step"], 2 * b + 1)
                V.tensor_tensor(krstd[:], kvar[:], neghalf[:, 0:KVH], ALU.pow).then_inc(S["krstd_step"], 1)
                pool.wait_ge(S["krstd_step"], 2 * b + 2)
                V.tensor_tensor(k_norm[:], k_raw[:], krstd[:].unsqueeze(2).broadcast_to([P, KVH, HD]), ALU.mult)\
                 .then_inc(S["knorm_ready"], 1)
                if not first:
                    gel_low(b - 1)
                if not last:
                    t_low(b + 1)
            l0_step(0, first=True)
            l0_step(1)
            with pool.Fori(2, NB - 1) as b:
                l0_step(b)
            l0_step(NB - 1, last=True)

            def ln_rstd(i, half):
                pool.wait_ge(LN[i]["step"], 9 * half + 9)
                tiles = slice(4 * half, 4 * half + 4)
                V.tensor_tensor(rstd[:, tiles], vareps[:, tiles], neghalf[:, tiles], ALU.pow)\
                 .then_inc(LN[i]["rstd_ready"], 1)

            def ffn_low(i, c, slot):
                pool.wait_ge(FF[i]["whi_ready"], c + 1)
                V.tensor_tensor(ffn_lo[:, slot], ffn_stage[:, slot], ffn_hi[:, slot].bitcast(F32), ALU.subtract)\
                 .then_inc(FF[i]["wlo_ready"], 1)

            def ffn(i, n):
                ln_rstd(2 * i, 0)
                if i == 0:
                    gel_low(NB - 1)
                ffn_low(i, 0, 0)
                ln_rstd(2 * i, 1)
                ffn_low(i, 1, 1)
                if n > 4:
                    with pool.Fori(2, n - 1, 2) as c:
                        ffn_low(i, c, 0)
                        ffn_low(i, c + 1, 1)
                    ffn_low(i, n - 1, 0)
                else:
                    for c in range(2, n):
                        ffn_low(i, c, c % 2)

            ffn(0, CH0)

            def low(name, lo, stage, hi, g):
                pool.wait_ge(S[f"{name}_hi_ready"], g + 1)
                V.tensor_tensor(lo[:], stage[:], hi[:].bitcast(F32), ALU.subtract).then_inc(S[f"{name}_lo_ready"], 1)

            def q_rstd(g, half):
                pool.wait_ge(S["qvar_ready"], 2 * g + half + 1)
                V.tensor_tensor(rq[:, half], qvar[:], neghalf[:].rearrange("p (a b) -> p a b", b=GROUP)[:, 0:4],
                                ALU.pow).then_inc(S["rq_ready"], 1)

            def normalise(g, b):
                pool.wait_ge(S["rden_ready"], NB * g + b + 1)
                V.tensor_tensor(prob[:, b % 4], prob[:, b % 4],
                                rden1[:, b].unsqueeze(2).broadcast_to([P, GROUP, P]), ALU.mult)\
                 .then_inc(S["pn_ready"], 1)

            def att_step(g, last=False):
                q_rstd(g, 0)
                low("v", v_lo, v_stage, v_hi, g)
                for b in range(4):
                    normalise(g, b)
                low("wo", wo_lo, wo_stage, wo_hi, g)
                q_rstd(g, 1)
                if not last:
                    low("wq", wq_lo, wq_stage, wq_hi, g + 1)
                for b in range(4, 8):
                    normalise(g, b)
            low("wq", wq_lo, wq_stage, wq_hi, 0)
            ln_rstd(1, 0)
            ln_rstd(1, 1)
            with pool.Fori(0, KVH - 1) as g:
                att_step(g)
            att_step(KVH - 1, last=True)
            ffn(1, CH1)

        @block.scalar
        def _(act):
            def copy(o, i):
                return nc.scalar.activation(o, i, ACT.Copy)

            act.wait_ge(S["const_in"], 16 * 8)
            copy(wst_hi[:], wst_stage[:]).then_inc(S["wst_hi_ready"], 1)
            copy(mask_sel[:], mask_sel_s[:]).then_inc(S["wst_hi_ready"], 1)
            copy(wo0_hi[:], wo0_stage[:]).then_inc(S["wo0_split"], 1)

            def x_high(b):
                act.wait_ge(S["xn_ready"], b + 1)
                wait(act, S["stack_done"], 4 * b)
                copy(xn0_hi[:], xn0[:]).then_inc(S["xh_ready"], 1)

            def t_high(b):
                act.wait_ge(S["ctxT_in"], 16 * (b + 1))
                wait(act, S["v_done"], 2 * b)
                copy(ctxT_hi[:], ctxT_stage[:]).then_inc(S["th_ready"], 1)

            def kvw_high(c):
                act.wait_ge(S[f"kvw_in{c % 3}"], 16 * (c // 3 + 1))
                copy(wkv_hi[:, c // KC, c % KC], kv_stage[:, c % 3]).then_inc(S["kvw_hi_ready"], 1)

            def evac_t0(pair, r):
                act.wait_ge(S["t0_done"], 4 * pair + r + 1)
                wait(act, S["pv0_done"], pair)
                copy(pT0[:, r], ps[:, 4 + r % 2].rearrange("p (s n) -> p s n", s=4)).then_inc(S["t0_by_act"], 1)

            def exp0(pair, q):
                act.wait_ge(S["sub0_ready"], pair + 1)
                nc.scalar.activation(work0[:, q], work0[:, q], ACT.Exp, scale=float(DH0) ** -0.5)\
                  .then_inc(S["exp0_ready"], 1)

            def heads(bank):
                return ps[:, bank].rearrange("p (h d) -> p h d", h=4)

            def k_copy(b, n):
                act.wait_ge(S["k_done"], 2 * b + n + 1)
                wait(act, S["knorm_ready"], b)
                copy(k_raw[:, 4 * n:4 * n + 4], heads(A_BANK)).then_inc(S["k_copied"], 1)

            def v_copy(b, n):
                act.wait_ge(S["v_done"], 2 * b + n + 1)
                wait(act, S["v_written"], 16 * b)
                copy(v_out[:, 4 * n:4 * n + 4], heads(A_BANK)).then_inc(S["v_copied"], 1)

            def kT_copy(b, n):
                act.wait_ge(S["kT_done"], 2 * b + n + 1)
                wait(act, S["kT_written"], 16 * b)
                nc.scalar.activation(kT_out[:, 4 * n:4 * n + 4], heads((A_BANK, B_BANK)[n]), ACT.Copy, scale=knorm_w[:, 2:3])\
                  .then_inc(S["kT_copied"], 1)

            def neg_high(b, i):
                m, bank = STACKS[i]
                act.wait_ge(S["stack_done"], 4 * b + i + 1)
                wait(act, S["stack_ready"], 4 * b)
                nc.scalar.activation(neg_hi[:, m], ps[:, bank], ACT.Identity, bias=stack_col[:, 6 + m:7 + m],
                                     scale=stack_col[:, 4 + m % 2:5 + m % 2]).then_inc(S["neghi_ready"], 1)

            def gelu(b):
                act.wait_ge(S["oT0_done"], b + 1)
                wait(act, S["gello_ready"], b)
                nc.scalar.activation(gel[:], ps[:, B_BANK, 0:2 * P].rearrange("p (s n) -> p s n", s=2), ACT.Gelu).then_inc(S["gelu_ready"], 1)
                act.wait_ge(S["gelu_ready"], b + 1)
                wait(act, S["wo0_done"], b)
                copy(gel_hi[:], gel[:]).then_inc(S["gelhi_ready"], 1)

            x_high(0)
            act.wait_ge(S["col_ready"], 1)
            act.wait_ge(S["factor_ready"], 1)
            kvw_high(0)
            kvw_high(1)
            neg_high(0, 0)
            neg_high(0, 1)
            kvw_high(2)
            neg_high(0, 2)
            t_high(0)
            neg_high(0, 3)
            for c in range(3, 7):
                kvw_high(c)

            def l0_step(b, first=False, last=False):
                if not first:
                    evac_t0(2 * b - 1, 0)
                k_copy(b, 0)
                if not first:
                    evac_t0(2 * b - 1, 2)
                exp0(2 * b, 0)
                k_copy(b, 1)
                act.wait_ge(S["k_copied"], 2 * b + 2)
                wait(act, S["kT_done"], 2 * b)
                for h in range(KVH):
                    last_sq = nc.scalar.activation(k_norm[:, h], k_raw[:, h], ACT.Square, accum_out=ksum[:, h:h + 1])
                last_sq.then_inc(S["ksum_ready"], 1)
                if first:
                    kvw_high(7)
                if not last:
                    x_high(b + 1)
                evac_t0(2 * b, 0)
                if not first:
                    gelu(b - 1)
                v_copy(b, 0)
                evac_t0(2 * b, 2)
                exp0(2 * b + 1, 1)
                v_copy(b, 1)
                if not last:
                    t_high(b + 1)
                kT_copy(b, 0)
                if not last:
                    for i in range(4):
                        neg_high(b + 1, i)
                kT_copy(b, 1)

            l0_step(0, first=True)
            l0_step(1)
            with act.Fori(2, NB - 1) as b:
                l0_step(b)
            l0_step(NB - 1, last=True)

            def ln(i, tiles):
                for t in tiles:
                    act.wait_ge(LN[i]["t_done"], t + 1)
                    copy(hT_hi[:, :, t * P:(t + 1) * P],
                         ps[:, LN_BANKS[i][t // 4][t % 2]].rearrange("p (k n) -> p k n", k=KC))\
                        .then_inc(LN[i]["hi_ready"], 1)

            def ffn_high(i, c, slot):
                act.wait_ge(FF[i][f"w_in{slot}"], 8 * c + (8 if slot else 16))
                wait(act, FF[i]["down_done"], NB * (c - 1))
                copy(ffn_hi[:, slot], ffn_stage[:, slot]).then_inc(FF[i]["whi_ready"], 1)

            def ffn_act(i, c, slot, prefetch):
                for half in range(2):
                    act.wait_ge(FF[i]["gu_done"], 2 * c + half + 1)
                    wait(act, FF[i]["gated_ready"], 2 * c + half - 1)
                    bias = b12[:, 0, c:c + 1] if i == 1 else 0.0
                    nc.scalar.activation(silu[:, half], ps[:, half], ACT.Silu, bias=bias)\
                      .then_inc(FF[i]["silu_ready"], 1)
                    act.wait_ge(FF[i]["gated_ready"], 2 * c + half + 1)
                    wait(act, FF[i]["down_done"], NB * (c - 1) + 4 + 4 * half)
                    copy(gT_hi[:, half], gated[:, half]).then_inc(FF[i]["ghi_ready"], 1)
                    if half == 0 and prefetch:
                        ffn_high(i, c + 1, 1 - slot)

            def high(name, hi, stage, g):
                act.wait_ge(S[f"{name}_in"], 16 * (g + 1))
                copy(hi[:], stage[:]).then_inc(S[f"{name}_hi_ready"], 1)

            def ffn(i, n):
                ln(2 * i, range(4, NB))
                ffn_act(i, 0, 0, True)
                if n > 4:
                    with act.Fori(1, n - 2, 2) as c:
                        ffn_act(i, c, 1, True)
                        ffn_act(i, c + 1, 0, True)
                    ffn_act(i, n - 2, 1, True)
                    high("wq", wq_hi, wq_stage, 0)
                    ffn_act(i, n - 1, 0, False)
                else:
                    for c in range(1, n):
                        ffn_act(i, c, c % 2, c < n - 1)

            evac_t0(2 * NB - 1, 0)
            evac_t0(2 * NB - 1, 2)
            ln(0, range(2))
            gelu(NB - 1)
            ln(0, range(2, 4))
            act.wait_ge(S["kT_written"], 16 * NB)
            act.wait_ge(S["v_written"], 16 * NB)
            ffn_high(0, 0, 0)
            ffn(0, CH0)

            def q_out(g, half, h):
                n = 8 * g + 4 * half + h
                act.wait_ge(S["q_done"], n + 1)
                wait(act, S["ss_done"], n - 3)
                nc.scalar.activation(q_sq[:, h], ps[:, h % 2], ACT.Square).then_inc(S["sq_ready"], 1)

            def exps(g, b):
                act.wait_ge(S["negmax_ready"], 8 * g + b + 1)
                for h in range(GROUP):
                    e = nc.scalar.activation(prob[:, b % 4, h], prob[:, b % 4, h], ACT.Exp,
                                             bias=negmax[:, b, h:h + 1], accum_out=psum1[:, b, h:h + 1])
                e.then_inc(S["exp_ready"], 1)

            def p_part(g, b):
                n = 8 * g + b
                act.wait_ge(S["t_done"], n + 1)
                wait(act, S["pv_done"], n - 1)
                copy(pT_hi[:, b % 2], ps[:, T_BANKS[b % 2]]).then_inc(S["pthi_ready"], 1)

            def o_high(g, b):
                n = 8 * g + b
                act.wait_ge(S["pv_done"], n + 1)
                wait(act, S["wo_done"], n - 3)
                copy(oT_hi[:, b % 4], ps[:, 5].rearrange("p (h n) -> p h n", h=GROUP)).then_inc(S["ohi_ready"], 1)

            def att_step(g, first=False, last=False):
                for j in range(4):
                    q_out(g, 0, j)
                    if first:
                        ln(1, [4 + j])
                    else:
                        if j == 0:
                            exps(g - 1, 7)
                        p_part(g - 1, 4 + j)
                        if j >= 1:
                            o_high(g - 1, 3 + j)
                if not first:
                    o_high(g - 1, 7)
                high("v", v_hi, v_stage, g)
                for j in range(3):
                    exps(g, j)
                if not first:
                    act.wait_ge(S["wo_done"], 8 * g)
                high("wo", wo_hi, wo_stage, g)
                for j in range(4):
                    q_out(g, 1, j)
                    if j == 0:
                        exps(g, 3)
                    p_part(g, j)
                    if j >= 1:
                        o_high(g, j - 1)
                if not last:
                    act.wait_ge(S["q_done"], 8 * g + 8)
                    high("wq", wq_hi, wq_stage, g + 1)
                o_high(g, 3)
                for j in range(4, 7):
                    exps(g, j)

            ln(1, range(4))
            att_step(0, first=True)
            with act.Fori(1, KVH - 1) as g:
                att_step(g)
            att_step(KVH - 1, last=True)
            exps(KVH - 1, 7)
            for j in range(4):
                p_part(KVH - 1, 4 + j)
                if j >= 1:
                    o_high(KVH - 1, 3 + j)
            o_high(KVH - 1, 7)
            act.wait_ge(S["s_done"], NB * KVH)
            ffn_high(1, 0, 0)
            ln(2, range(4))
            ffn(1, CH1)

        @block.vector
        def _(dve):
            V = nc.vector

            dve.wait_ge(S["const_in"], 16 * 8)
            V.tensor_scalar(knorm_w[:, 2:3], knorm_w[:, 0:1], knorm_w[:, 1:2], float(HD) ** -0.5,
                            ALU.mult, ALU.mult).then_inc(S["factor_ready"], 1)
            V.tensor_tensor(stack_col[:, 6:10].rearrange("p (a b) -> p a b", b=2),
                            stack_col[:, 0:4].rearrange("p (a b) -> p a b", b=2),
                            stack_col[:, 4:6].unsqueeze(1).broadcast_to([P, 2, 2]), ALU.mult)\
             .then_inc(S["col_ready"], 1)

            def tile_stats(s, t):
                V.bn_stats(stats[:, t], x[:, t]).then_inc(s, 1)

            def variances(s, tiles, done):
                for n, t in enumerate(tiles):
                    dve.wait_ge(s, done + n + 1)
                    V.bn_aggr(meanvar[:, t], stats[:, t]).then_inc(s, 1)
                dve.wait_ge(s, done + 2 * len(tiles))
                V.tensor_scalar(vareps[:, tiles[0]:tiles[-1] + 1], meanvar[:, tiles[0]:tiles[-1] + 1, 1], EPS, None,
                                ALU.add).then_inc(s, 1)

            dve.wait_ge(S["x_in0"], 16)
            tile_stats(S["stat_step"], 0)
            variances(S["stat_step"], [0], 0)

            def normal0(b):
                wait(dve, S["xl_ready"], b)
                V.tensor_scalar(xn0[:], x[:, bass.ds(b, 1)].rearrange("p a s -> p (a s)"),
                                meanvar[:, bass.ds(b, 1), 0:1].rearrange("p a s -> p (a s)"),
                                rstd[:, bass.ds(b, 1)], ALU.subtract, ALU.mult).then_inc(S["xn_ready"], 1)
                dve.wait_ge(S["mask_in"], 16 * (b + 1))
                V.tensor_scalar(mask_step[:], mask_row[:], 0.0, -MASKED, ALU.is_gt, ALU.mult)\
                 .then_inc(S["maskb_ready"], 1)
                dve.wait_ge(S["maskb_ready"], 2 * b + 1)
                wait(dve, S["stack_done"], 4 * b)
                V.tensor_scalar(mask_bias[:], mask_step[:], MASKED, None, ALU.add).then_inc(S["maskb_ready"], 1)

            def evac_t0(pair, r):
                dve.wait_ge(S["t0_done"], 4 * pair + r + 1)
                wait(dve, S["pv0_done"], pair)
                V.tensor_copy(pT0[:, r], ps[:, 4 + r % 2].rearrange("p (s n) -> p s n", s=4))\
                 .then_inc(S["t0_by_dve"], 1)

            def out0(pair, q, turned):
                dve.wait_ge(S["pv0_done"], pair + 1)
                pv = ps[:, B_BANK, 0:2 * H0 * (DH0 + 1)].rearrange("p (s h e) -> p s h e", s=2, h=H0)
                V.reciprocal(rden0[:].unsqueeze(3), pv[:, :, :, DH0:DH0 + 1]).then_inc(S["rden0_ready"], 1)
                dve.wait_ge(S["rden0_ready"], pair + 1)
                wait(dve, S["oT0_done"], turned)
                o = o_tile[:, 2 * q:2 * q + 2].rearrange("p s (h e) -> p s h e", e=DH0)
                V.tensor_tensor(o, pv[:, :, :, 0:DH0], rden0[:].unsqueeze(3).broadcast_to([P, 2, H0, DH0]), ALU.mult)\
                 .then_inc(S["o0_ready"], 1)

            scores_flat = ps[:, 0:4].rearrange("p a (s n) -> p (a s) n", n=P)

            def max0(pair):
                dve.wait_ge(S["s0_done"], pair + 1)
                V.tensor_reduce(smax0[:], scores_flat, AX_X, ALU.max).then_inc(S["max0_ready"], 1)

            def sub0(pair, q):
                dve.wait_ge(S["max0_ready"], pair + 1)
                wait(dve, S["t0_done"], 4 * (pair - 1))
                V.tensor_tensor(work0[:, q].rearrange("p a s n -> p (a s) n"), scores_flat,
                                smax0[:].unsqueeze(2).broadcast_to([P, 16, P]), ALU.subtract)\
                 .then_inc(S["sub0_ready"], 1)

            def wk_low(k):
                dve.wait_ge(S["kvw_hi_ready"], k + 1)
                V.tensor_tensor(wkv_lo[:, 0, k], kv_stage[:, k % 3], wkv_hi[:, 0, k].bitcast(F32), ALU.subtract)\
                 .then_inc(S["wk_lo_ready"], 1)

            def stacks(b, between=lambda i: None):
                wait(dve, S["s0_done"], 2 * b)
                for i, (m, bank) in enumerate(STACKS):
                    between(i)
                    dve.wait_ge(S["neghi_ready"], 4 * b + i + 1)
                    dst = (k_stack, q_stack)[m % 2][:, m // 2]
                    V.scalar_tensor_tensor(dst, ps[:, bank], stack_col[:, m:m + 1], neg_hi[:, m].bitcast(F32),
                                           ALU.add, ALU.add).then_inc(S["stack_ready"], 1)

            def values(b):
                dve.wait_ge(S["v0_done"], b + 1)
                wait(dve, S["pv0_done"], 2 * b - 1)
                wait(dve, S["vnext_ready"], b)
                for dst, s in ((v_aug[:, 0:2, :, 0:DH0], 0), (v_next[:], 2)):
                    v = V.tensor_tensor(
                        dst, ps[:, A_BANK, s * E0:(s + 2) * E0].rearrange("p (s h e) -> p s h e", s=2, h=H0),
                        bv0[:].rearrange("p (h e) -> p h e", e=DH0).unsqueeze(1).broadcast_to([P, 2, H0, DH0]),
                        ALU.add)
                v.then_inc(S["v0_ready"], 1)

            def values_next(b):
                wait(dve, S["pv0_done"], 2 * b)
                dve.wait_ge(S["v0_ready"], b + 1)
                V.tensor_copy(v_aug[:, 2:4, :, 0:DH0], v_next[:]).then_inc(S["vnext_ready"], 1)

            def add0(b):
                dve.wait_ge(S["wo0_done"], b + 1)
                dve.wait_ge(S["maskb_in"], 16 * (b + 1))
                wait(dve, S["x0_ready"], b)
                V.scalar_tensor_tensor(delta0[:], ps[:, 4], bo0[:], mask_b[:], ALU.add, ALU.mult)\
                 .then_inc(S["delta0_ready"], 1)
                dve.wait_ge(S["delta0_ready"], b + 1)
                x_tile = x[:, bass.ds(b, 1)].rearrange("p a s -> p (a s)")
                V.tensor_tensor(x_tile, x_tile, delta0[:], ALU.add).then_inc(S["x0_ready"], 1)

            dve.wait_ge(S["l0_rstd_ready"], 1)
            normal0(0)
            dve.wait_ge(S["wo0_split"], 1)
            V.tensor_tensor(wo0_lo[:], wo0_stage[:], wo0_hi[:].bitcast(F32), ALU.subtract).then_inc(S["wo0_split"], 1)
            dve.wait_ge(S["vaug_ready"], 1)
            wk_low(0)
            wk_low(1)
            stacks(0, lambda i: wk_low(2) if i == 3 else None)
            values(0)
            wk_low(3)

            def l0_step(b, first=False, last=False):
                max0(2 * b)
                if not first:
                    evac_t0(2 * b - 1, 1)
                sub0(2 * b, 0)
                if first:
                    dve.wait_ge(S["x_in"], 16)
                    for t in range(1, NB):
                        tile_stats(S["stat_step"], t)
                    variances(S["stat_step"], range(1, NB), 3)
                    dve.wait_ge(S["l0_rstd_ready"], 2)
                else:
                    evac_t0(2 * b - 1, 3)
                if not last:
                    normal0(b + 1)
                if not first:
                    out0(2 * b - 1, 1, b - 1)
                values_next(b)
                dve.wait_ge(S["ksum_ready"], b + 1)
                V.tensor_scalar(kvar[:], ksum[:], 1.0 / HD, EPS, ALU.mult, ALU.add).then_inc(S["krstd_step"], 1)
                if last:
                    ln_half(0)
                max0(2 * b + 1)
                evac_t0(2 * b, 1)
                sub0(2 * b + 1, 1)
                evac_t0(2 * b, 3)
                out0(2 * b, 0, b)
                if not last:
                    stacks(b + 1)
                    values(b + 1)
                if not first:
                    add0(b - 1)

            def ln_stat(i, t, sem_x, added):
                dve.wait_ge(sem_x, added)
                tile_stats(LN[i]["step"], t)

            def ln_var(i, half):
                variances(LN[i]["step"], range(4 * half, 4 * half + 4), 9 * half)

            def ln_normal(i, half):
                dve.wait_ge(LN[i]["rstd_ready"], half + 1)
                for t in range(4 * half, 4 * half + 4):
                    if half:
                        dve.wait_ge(LN[i]["t_done"], t - 3)
                    V.tensor_scalar(xn[:, t % 4], x[:, t], meanvar[:, t, 0:1], rstd[:, t:t + 1],
                                    ALU.subtract, ALU.mult).then_inc(LN[i]["xn_ready"], 1)

            def ln_low(i, half):
                for t in range(4 * half, 4 * half + 4):
                    dve.wait_ge(LN[i]["hi_ready"], t + 1)
                    V.tensor_tensor(hT_lo[:, :, t * P:(t + 1) * P],
                                    ps[:, LN_BANKS[i][half][t % 2]].rearrange("p (k n) -> p k n", k=KC),
                                    hT_hi[:, :, t * P:(t + 1) * P].bitcast(F32), ALU.subtract)\
                     .then_inc(LN[i]["lo_ready"], 1)

            def ffn_gate(i, c, half):
                dve.wait_ge(FF[i]["silu_ready"], 2 * c + half + 1)
                bias = b12[:, 1, c:c + 1] if i == 1 else 0.0
                wait(dve, FF[i]["glo_ready"], 2 * c + half - 1)
                V.scalar_tensor_tensor(gated[:, half], ps[:, 2 + half], bias, silu[:, half], ALU.add, ALU.mult)\
                 .then_inc(FF[i]["gated_ready"], 1)
                dve.wait_ge(FF[i]["ghi_ready"], 2 * c + half + 1)
                V.tensor_tensor(gT_lo[:, half], gated[:, half], gT_hi[:, half].bitcast(F32), ALU.subtract)\
                 .then_inc(FF[i]["glo_ready"], 1)

            def ffn_add(i, c, half, after=lambda t: None):
                for t in range(4 * half, 4 * half + 4):
                    dve.wait_ge(FF[i]["down_done"], NB * c + t + 1)
                    V.tensor_tensor(x[:, t], x[:, t], ps[:, 4 + t % 4], ALU.add).then_inc(FF[i]["x_added"], 1)
                for t in range(4 * half, 4 * half + 4):
                    after(t)

            def ffn(i, n, ln_next=None):
                ln_normal(2 * i, 1)
                ln_low(2 * i, 1)
                ffn_gate(i, 0, 0)
                ffn_gate(i, 0, 1)
                ffn_add(i, 0, 0)

                def step(c):
                    ffn_gate(i, c, 0)
                    ffn_add(i, c - 1, 1)
                    ffn_gate(i, c, 1)
                    ffn_add(i, c, 0)
                if n > 4:
                    with dve.Fori(1, n - 1) as c:
                        step(c)
                else:
                    for c in range(1, n - 1):
                        step(c)

                def stat(t):
                    if ln_next is not None:
                        ln_stat(ln_next, t, FF[i]["x_added"], NB * (n - 1) + t + 1)
                ffn_gate(i, n - 1, 0)
                ffn_add(i, n - 2, 1)
                ffn_add(i, n - 1, 0, stat)
                if ln_next is not None:
                    ln_var(ln_next, 0)
                ffn_gate(i, n - 1, 1)
                if ln_next is not None:
                    ln_normal(ln_next, 0)
                ffn_add(i, n - 1, 1, stat)
                if ln_next is not None:
                    ln_var(ln_next, 1)
                    ln_low(ln_next, 0)

            def ln_half(half):
                for t in range(4 * half, 4 * half + 4):
                    ln_stat(0, t, S["x0_ready"], t + 1)
                ln_var(0, half)

            l0_step(0, first=True)
            l0_step(1)
            with dve.Fori(2, NB - 1) as b:
                l0_step(b)
            l0_step(NB - 1, last=True)
            evac_t0(2 * NB - 1, 1)
            dve.wait_ge(S["v_done"], 2 * NB)
            ln_normal(0, 0)
            evac_t0(2 * NB - 1, 3)
            out0(2 * NB - 1, 1, NB - 1)
            ln_low(0, 0)
            add0(NB - 1)
            ln_half(1)
            ffn(0, CH0, ln_next=1)

            def q_copy(g, half, h):
                n = 8 * g + 4 * half + h
                dve.wait_ge(S["sq_ready"], n + 1)
                if h == 0:
                    wait(dve, S["s_done"], 8 * g + 4 * half)
                V.tensor_copy(qT[:, h], ps[:, h % 2]).then_inc(S["q_copied"], 1)

            def q_var(g, half):
                dve.wait_ge(S["ss_done"], 8 * g + 4 * half + 4)
                wait(dve, S["rq_ready"], 2 * g + half)
                V.tensor_scalar(qvar[:], ps[:, 7, 0:16].rearrange("p (b h) -> p b h", b=4), 1.0 / HD, EPS,
                                ALU.mult, ALU.add).then_inc(S["qvar_ready"], 1)

            def soft(g, b):
                n = 8 * g + b
                dve.wait_ge(S["s_done"], n + 1)
                dve.wait_ge(S["rq_ready"], 2 * g + b // 4 + 1)
                wait(dve, S["t_done"], n - 3)
                for h in range(GROUP):
                    m = V.scalar_tensor_tensor(prob[:, b % 4, h], ps[:, 2 + b % 2, h * P:(h + 1) * P],
                                               rq[:, b // 4, b % 4, h:h + 1], mask1[:], ALU.mult, ALU.add)
                m.then_inc(S["masked_ready"], 1)
                dve.wait_ge(S["masked_ready"], n + 1)
                V.tensor_reduce(negmax[:, b], prob[:, b % 4], AX_X, ALU.max, negate=True)\
                 .then_inc(S["negmax_ready"], 1)

            def denominators(g, b):
                n = 8 * g + b
                dve.wait_ge(S["exp_ready"], n + 1)
                V.reciprocal(rden1[:, b], psum1[:, b]).then_inc(S["rden_ready"], 1)

            def p_part(g, b):
                n = 8 * g + b
                dve.wait_ge(S["pthi_ready"], n + 1)
                V.tensor_tensor(pT_lo[:, b % 2], ps[:, T_BANKS[b % 2]], pT_hi[:, b % 2].bitcast(F32), ALU.subtract)\
                 .then_inc(S["ptlo_ready"], 1)

            def o_low(g, b):
                n = 8 * g + b
                dve.wait_ge(S["ohi_ready"], n + 1)
                V.tensor_tensor(oT_lo[:, b % 4], ps[:, 5].rearrange("p (h n) -> p h n", h=GROUP),
                                oT_hi[:, b % 4].bitcast(F32), ALU.subtract).then_inc(S["olo_ready"], 1)

            def x_add(g, t):
                n = 8 * g + t
                dve.wait_ge(S["wo_done"], n + 1)
                V.tensor_tensor(x[:, t], x[:, t], ps[:, t % 2], ALU.add).then_inc(S["x_added"], 1)

            def att_step(g, first=False):
                for j in range(4):
                    q_copy(g, 0, j)
                    if first:
                        ln_one(4 + j)
                    else:
                        if j == 0:
                            denominators(g - 1, 7)
                        p_part(g - 1, 4 + j)
                        if j >= 1:
                            o_low(g - 1, 3 + j)
                for j in range(4):
                    if not first:
                        x_add(g - 1, 4 + j)
                        if j == 0:
                            o_low(g - 1, 7)
                    if j == 0:
                        q_var(g, 0)
                    soft(g, j)
                    if j >= 1:
                        denominators(g, j - 1)
                for j in range(4):
                    q_copy(g, 1, j)
                    if j == 0:
                        denominators(g, 3)
                    p_part(g, j)
                    if j >= 1:
                        o_low(g, j - 1)
                for j in range(4):
                    x_add(g, j)
                    if j == 0:
                        o_low(g, 3)
                        q_var(g, 1)
                    soft(g, 4 + j)
                    if j >= 1:
                        denominators(g, 4 + j - 1)

            def ln_one(t):
                dve.wait_ge(LN[1]["hi_ready"], t + 1)
                V.tensor_tensor(hT_lo[:, :, t * P:(t + 1) * P],
                                ps[:, LN_BANKS[1][1][t % 2]].rearrange("p (k n) -> p k n", k=KC),
                                hT_hi[:, :, t * P:(t + 1) * P].bitcast(F32), ALU.subtract)\
                 .then_inc(LN[1]["lo_ready"], 1)

            ln_normal(1, 1)
            dve.wait_ge(S["att_const_in"], 48)
            att_step(0, first=True)
            with dve.Fori(1, KVH) as g:
                att_step(g)
            denominators(KVH - 1, 7)
            for j in range(4):
                p_part(KVH - 1, 4 + j)
                if j >= 1:
                    o_low(KVH - 1, 3 + j)
                ln_stat(2, j, S["x_added"], NB * (KVH - 1) + j + 1)
            x_add(KVH - 1, 4)
            o_low(KVH - 1, 7)
            ln_var(2, 0)
            ln_normal(2, 0)
            for j in range(1, 4):
                x_add(KVH - 1, 4 + j)
            for j in range(4):
                ln_stat(2, 4 + j, S["x_added"], NB * (KVH - 1) + 5 + j)
            ln_var(2, 1)
            ln_low(2, 0)
            ffn(1, CH1)
            for t in range(NB):
                dve.wait_ge(FF[1]["x_added"], NB * (CH1 - 1) + t + 1)
                V.tensor_tensor(x[:, t], x[:, t], b3[:], ALU.add).then_inc(S["result_ready"], 1)

        @block.tensor
        def _(pe):
            T = nc.tensor

            def three(o, w_hi, w_lo, m_hi, m_lo, start, stop):
                T.matmul(o, w_hi, m_hi, start=start, stop=False)
                T.matmul(o, w_hi, m_lo, start=False, stop=False)
                return T.matmul(o, w_lo, m_hi, start=False, stop=stop)

            def project(o, w, bank, done):
                for k in range(KC):
                    last = three(o, ctxT_hi[:, k], ctxT_lo[:, k], wkv_hi[:, w, k, bank * 512:(bank + 1) * 512],
                                 wkv_lo[:, w, k, bank * 512:(bank + 1) * 512], k == 0, k == KC - 1)
                last.then_inc(S[done], 1)

            def scores(pair, q):
                wait(pe, S["sub0_ready"], pair)
                for s in range(4):
                    grp, patch = s // 2, 2 * q + s % 2
                    for h in range(4):
                        rows = slice(STACK * h, STACK * h + STACK)
                        cols = slice(patch * P, patch * P + P)
                        last = T.matmul(scores0[:, h, s], q_stack[rows, grp, cols], k_stack[rows, grp, cols],
                                        start=True, stop=True)
                last.then_inc(S["s0_done"], 1)

            def turn_p0(pair, q, r):
                wait(pe, S[("t0_by_act", "t0_by_dve")[r % 2]], 2 * pair + r // 2)
                for s in range(4):
                    last = T.transpose(ps[:, 4 + r % 2, s * P:(s + 1) * P], work0[:, q, r, s], ident[:])
                last.then_inc(S["t0_done"], 1)

            def times_v0(pair, q, r):
                pv = ps[:, B_BANK, 0:2 * H0 * (DH0 + 1)].rearrange("p (s h e) -> p s h e", s=2, h=H0)
                pe.wait_ge(S[("t0_by_act", "t0_by_dve")[r % 2]], 2 * pair + r // 2 + 1)
                for s in range(4):
                    head, patch = 4 * (s // 2) + r, s % 2
                    last = T.matmul(pv[:, patch, head], pT0[:, r, s], v_aug[:, 2 * q + patch, head],
                                    start=True, stop=True)
                return last

            def spread(pair, q, project_0, project_1, bank_read):
                pe.wait_ge(S["exp0_ready"], pair + 1)
                turn_p0(pair, q, 0)
                turn_p0(pair, q, 1)
                project_0()
                wait(pe, *bank_read)
                times_v0(pair, q, 0)
                turn_p0(pair, q, 2)
                times_v0(pair, q, 1)
                turn_p0(pair, q, 3)
                project_1()
                times_v0(pair, q, 2)
                times_v0(pair, q, 3).then_inc(S["pv0_done"], 1)

            def keys(b, n):
                if n == 0:
                    pe.wait_ge(S["tl_ready"], b + 1)
                    pe.wait_ge(S["v0_ready"], b + 1)
                else:
                    pe.wait_ge(S["k_copied"], 2 * b + 1)
                project(ps[:, A_BANK], 0, n, "k_done")

            def values(b, n):
                if n == 0:
                    pe.wait_ge(S["k_copied"], 2 * b + 2)
                else:
                    pe.wait_ge(S["v_copied"], 2 * b + 1)
                project(ps[:, A_BANK], 1, n, "v_done")

            def turn_keys(b, n, last=False):
                if n == 0:
                    pe.wait_ge(S["knorm_ready"], b + 1)
                    pe.wait_ge(S["v_copied"], 2 * b + 2)
                else:
                    if last:
                        pe.wait_ge(S["o0_ready"], 2 * b + 1)
                    else:
                        pe.wait_ge(S["stack_ready"], 4 * b + 7)
                for h in range(4):
                    last_turn = T.transpose(ps[:, (A_BANK, B_BANK)[n], h * P:(h + 1) * P], k_norm[:, 4 * n + h], ident[:])
                last_turn.then_inc(S["kT_done"], 1)

            def stack(b, i):
                m, bank = STACKS[i]
                if i == 0:
                    pe.wait_ge(S["xl_ready"], b + 1)
                    pe.wait_ge(S["maskb_ready"], 2 * b + 2)
                    wait(pe, S["t0_by_act"], 4 * b - 2)
                elif i == 1:
                    wait(pe, S["t0_by_dve"], 4 * b - 2)
                elif i == 2:
                    wait(pe, S["o0_ready"], 2 * b - 1)
                else:
                    wait(pe, S["kT_copied"], 2 * b - 1)
                last = three(ps[:, bank], wst_hi[:, m], wst_lo[:, m], xn0_hi[:], xn0_lo[:], True, m % 2 == 1)
                if m % 2 == 0:
                    last = T.matmul(ps[:, bank], mask_sel[:], mask_bias[:],
                                    start=False, stop=True)
                last.then_inc(S["stack_done"], 1)

            def values0(b):
                pe.wait_ge(S["ctx_in"], 16 * (b + 1))
                pe.wait_ge(S["stack_ready"], 4 * b + 4)
                for s in range(NPATCH):
                    last = T.matmul(ps[:, A_BANK, s * E0:(s + 1) * E0], ctx_nat[:, s * P:(s + 1) * P], wv0[:],
                                    start=True, stop=True)
                last.then_inc(S["v0_done"], 1)

            def turn_o(b):
                pe.wait_ge(S["o0_ready"], 2 * b + 2)
                for s in range(2):
                    last = T.transpose(ps[:, B_BANK, s * P:(s + 1) * P],
                                       o_tile[:, 2 * s:2 * s + 2].rearrange("p a e -> p (a e)"), ident[:])
                last.then_inc(S["oT0_done"], 1)

            def output0(b):
                pe.wait_ge(S["gello_ready"], b + 1)
                out_patches = ps[:, 4].rearrange("p (s a n) -> p a s n", s=2, a=2)
                for a in range(2):
                    last = three(out_patches[:, a], wo0_hi[:, a], wo0_lo[:, a], gel_hi[:], gel_lo[:], True, True)
                last.then_inc(S["wo0_done"], 1)

            def l0_step(b, first=False, last=False):
                pe.wait_ge(S["stack_ready"], 4 * b + 4)
                scores(2 * b, 0)
                if first:
                    pe.wait_ge(S["wk_lo_ready"], KC)
                    keys(b, 0)
                    keys(b, 1)
                else:
                    wait(pe, S["delta0_ready"], b - 1)
                    spread(2 * b - 1, 1, lambda: keys(b, 0), lambda: keys(b, 1), (S["kT_copied"], 2 * b))
                scores(2 * b + 1, 1)
                if not first:
                    turn_o(b - 1)
                if first:
                    pe.wait_ge(S["wv_lo_ready"], KC)
                spread(2 * b, 0, lambda: values(b, 0), lambda: values(b, 1), (S["gelu_ready"], b))
                pe.wait_ge(S["vnext_ready"], b + 1)
                turn_keys(b, 0)
                if not last:
                    for i in range(4):
                        stack(b + 1, i)
                if not first:
                    if last:
                        pe.wait_ge(S["t0_by_act"], 4 * b + 2)
                    else:
                        pe.wait_ge(S["stack_ready"], 4 * b + 5)
                    output0(b - 1)
                turn_keys(b, 1, last)
                if not last:
                    values0(b + 1)

            pe.wait_ge(S["ident_ready"], 1)
            pe.wait_ge(S["wst_hi_ready"], 2)
            pe.wait_ge(S["wst_lo_ready"], 1)
            for i in range(4):
                stack(0, i)
            values0(0)
            l0_step(0, first=True)
            l0_step(1)
            with pe.Fori(2, NB - 1) as b:
                l0_step(b)
            l0_step(NB - 1, last=True)

            def ln_turn(i, t):
                pe.wait_ge(LN[i]["xn_ready"], t + 1)
                wait(pe, LN[i]["lo_ready"], t - 1)
                bank = LN_BANKS[i][t // 4][t % 2]
                for k in range(KC):
                    last = T.transpose(ps[:, bank, k * P:(k + 1) * P], xn[:, t % 4, k * P:(k + 1) * P], ident[:])
                last.then_inc(LN[i]["t_done"], 1)

            pair = 2 * NB - 1
            pe.wait_ge(S["delta0_ready"], NB - 1)
            pe.wait_ge(S["exp0_ready"], pair + 1)
            turn_p0(pair, 1, 0)
            turn_p0(pair, 1, 1)
            pe.wait_ge(S["kT_copied"], 2 * NB)
            times_v0(pair, 1, 0)
            turn_p0(pair, 1, 2)
            times_v0(pair, 1, 1)
            turn_p0(pair, 1, 3)
            times_v0(pair, 1, 2)
            times_v0(pair, 1, 3).then_inc(S["pv0_done"], 1)
            ln_turn(0, 0)
            ln_turn(0, 1)
            turn_o(NB - 1)
            ln_turn(0, 2)
            ln_turn(0, 3)
            output0(NB - 1)

            def gate_up(i, c, slot, half, between=lambda u: None):
                pe.wait_ge(FF[i]["wlo_ready"], c + 1)
                wait(pe, FF[i]["gated_ready"], 2 * c + half - 1)
                for u, bank in ((0, half), (1, 2 + half)):
                    for k in range(KC):
                        cols = slice(u * D + k * P, u * D + (k + 1) * P)
                        toks = slice(half * HALF, (half + 1) * HALF)
                        last = three(ps[:, bank], ffn_hi[:, slot, cols], ffn_lo[:, slot, cols],
                                     hT_hi[:, k, toks], hT_lo[:, k, toks], k == 0, k == KC - 1)
                    if u == 1:
                        last.then_inc(FF[i]["gu_done"], 1)
                    between(u)

            def down(i, c, slot, half):
                pe.wait_ge(FF[i]["glo_ready"], 2 * c + half + 1)
                for t in range(4 * half, 4 * half + 4):
                    wait(pe, FF[i]["x_added"], NB * c + t - 3)
                    toks = slice((t % 4) * P, (t % 4 + 1) * P)
                    three(ps[:, 4 + t % 4], gT_hi[:, half, toks], gT_lo[:, half, toks],
                          ffn_hi[:, slot, 2 * D:], ffn_lo[:, slot, 2 * D:], True, True)\
                        .then_inc(FF[i]["down_done"], 1)

            def ffn(i, n):
                pe.wait_ge(LN[2 * i]["lo_ready"], 4)

                def turn_two(u):
                    ln_turn(2 * i, 4 + 2 * u)
                    ln_turn(2 * i, 5 + 2 * u)
                gate_up(i, 0, 0, 0, turn_two)
                pe.wait_ge(LN[2 * i]["lo_ready"], NB)
                gate_up(i, 0, 0, 1)
                down(i, 0, 0, 0)

                def step(c, slot):
                    gate_up(i, c, slot, 0)
                    down(i, c - 1, 1 - slot, 1)
                    gate_up(i, c, slot, 1)
                    down(i, c, slot, 0)
                if n > 4:
                    with pe.Fori(1, n - 2, 2) as c:
                        step(c, 1)
                        step(c + 1, 0)
                    step(n - 2, 1)
                else:
                    for c in range(1, n - 1):
                        step(c, c % 2)
                slot = (n - 1) % 2
                gate_up(i, n - 1, slot, 0)
                down(i, n - 2, 1 - slot, 1)
                down(i, n - 1, slot, 0)
                gate_up(i, n - 1, slot, 1)
                down(i, n - 1, slot, 1)

            ffn(0, CH0)

            def square_sums(g, half, h):
                pe.wait_ge(S["sq_ready"], 8 * g + 4 * half + h + 1)
                if h == 0:
                    wait(pe, S["qvar_ready"], 2 * g + half)
                for b in range(4):
                    last = T.matmul(ps[:, 7, 4 * b + h:4 * b + h + 1], q_sq[:, h, b * P:(b + 1) * P], ones_col[:],
                                    start=True, stop=True)
                last.then_inc(S["ss_done"], 1)

            def score(g, b):
                n = 8 * g + b
                if b == 0:
                    pe.wait_ge(S["kT_in"], 16 * (g + 1))
                if b % 4 == 0:
                    pe.wait_ge(S["q_copied"], n + 4)
                wait(pe, S["masked_ready"], n - 1)
                for h in range(GROUP):
                    q, k = slice((b % 4) * P, (b % 4 + 1) * P), slice(b * P, (b + 1) * P)
                    last = T.matmul(ps[:, 2 + b % 2, h * P:(h + 1) * P], qT[:, h, q], kT[:, k], start=True, stop=True)
                last.then_inc(S["s_done"], 1)

            def turn_p(g, b):
                n = 8 * g + b
                pe.wait_ge(S["pn_ready"], n + 1)
                wait(pe, S["ptlo_ready"], n - 1)
                for h in range(GROUP):
                    last = T.transpose(ps[:, T_BANKS[b % 2], h * P:(h + 1) * P], prob[:, b % 4, h], ident[:])
                last.then_inc(S["t_done"], 1)

            def times_v(g, b):
                n = 8 * g + b
                if b == 0:
                    pe.wait_ge(S["v_lo_ready"], g + 1)
                pe.wait_ge(S["ptlo_ready"], n + 1)
                wait(pe, S["olo_ready"], n)
                three(ps[:, 5], v_hi[:, b], v_lo[:, b], pT_hi[:, b % 2], pT_lo[:, b % 2], True, True)\
                    .then_inc(S["pv_done"], 1)

            def output(g, t, after_output=False):
                n = 8 * g + t
                if t == 0:
                    pe.wait_ge(S["wo_lo_ready"], g + 1)
                pe.wait_ge(S["olo_ready"], n + 1)
                if t % 4 < 2 and not after_output:
                    pe.wait_ge(S["q_copied"], 8 * g + (7 if t < 4 else 11) + t % 4)
                else:
                    pe.wait_ge(S["x_added"], n - 1)
                for h in range(GROUP):
                    last = three(ps[:, t % 2], oT_hi[:, t % 4, h], oT_lo[:, t % 4, h], wo_hi[:, h], wo_lo[:, h],
                                 h == 0, h == GROUP - 1)
                last.then_inc(S["wo_done"], 1)

            def att_step(g, first=False):
                for j in range(4):
                    queries_after(g, 0, j, first)
                    if first:
                        ln_turn(1, 4 + j)
                    if j >= 1:
                        square_sums(g, 0, j - 1)
                    if not first:
                        turn_p(g - 1, 4 + j)
                        if j >= 1:
                            times_v(g - 1, 3 + j)
                for j in range(4):
                    if not first:
                        output(g - 1, 4 + j)
                        if j == 0:
                            times_v(g - 1, 7)
                    if j == 0:
                        square_sums(g, 0, 3)
                        if first:
                            pe.wait_ge(LN[1]["lo_ready"], NB)
                    score(g, j)
                for j in range(4):
                    queries_after(g, 1, j, first)
                    if j >= 1:
                        square_sums(g, 1, j - 1)
                    turn_p(g, j)
                    if j >= 1:
                        times_v(g, j - 1)
                for j in range(4):
                    output(g, j)
                    if j == 0:
                        times_v(g, 3)
                        square_sums(g, 1, 3)
                    score(g, 4 + j)

            def queries_after(g, half, h, first):
                n = 8 * g + 4 * half + h
                pe.wait_ge(S["wq_lo_ready"], g + 1)
                if h >= 2:
                    pe.wait_ge(S["q_copied"], n - 1)
                elif half == 0 and not first:
                    pe.wait_ge(S["x_added"], 8 * g - 5 + h)
                elif half == 1 and not first:
                    pe.wait_ge(S["x_added"], 8 * g - 1 + h)
                elif half == 1:
                    pe.wait_ge(S["q_copied"], 3 + h)
                for k in range(KC):
                    toks = slice(half * HALF, (half + 1) * HALF)
                    last = three(ps[:, h % 2], wq_hi[:, h, k], wq_lo[:, h, k], hT_hi[:, k, toks], hT_lo[:, k, toks],
                                 k == 0, k == KC - 1)
                last.then_inc(S["q_done"], 1)

            for t in range(4):
                ln_turn(1, t)
            pe.wait_ge(LN[1]["lo_ready"], 4)
            att_step(0, first=True)
            with pe.Fori(1, KVH) as g:
                att_step(g)
            turn_p(KVH - 1, 4)
            for j in range(4):
                if j < 3:
                    turn_p(KVH - 1, 5 + j)
                times_v(KVH - 1, 4 + j)
                output(KVH - 1, 4 + j, after_output=True)
            for t in range(4):
                ln_turn(2, t)
            ffn(1, CH1)


def kernel(**inputs):
    import numpy as np
    import concourse.bacc as _bacc
    from concourse.bass_utils import run_bass_kernel_spmd as _run

    a = {k: np.asarray(v) for k, v in inputs.items()}

    def chunks(w, rows=P):
        return np.ascontiguousarray(w.T.reshape(-1, P, w.shape[0]).transpose(1, 0, 2))

    def stack(w, group, parts):
        o = np.zeros((P,) + w.shape[1:], w.dtype)
        for h in range(4):
            for r in range(parts):
                at = STACK * h + DH0 * r
                o[at:at + DH0] = w[(4 * group + h) * DH0:(4 * group + h + 1) * DH0]
        return o

    wst = np.zeros((P, 4, P), np.float32)
    stack_col = np.zeros((P, 6), np.float32)
    mask_sel = np.zeros((1, P), np.float32)
    for grp in range(2):
        wst[:, 2 * grp] = stack(a["L0_xattn_Wk"], grp, 3).T
        wst[:, 2 * grp + 1] = stack(a["L0_xattn_Wq"], grp, 3).T
        stack_col[:, 2 * grp] = stack(a["L0_xattn_bk"], grp, 3)
        stack_col[:, 2 * grp + 1] = stack(a["L0_xattn_bq"], grp, 3)
        stack_col[3 * DH0::STACK, 2 * grp + 1] = 1.0
    for h in range(4):
        stack_col[STACK * h + DH0:STACK * h + 2 * DH0, 4] = -1.0
        stack_col[STACK * h + 2 * DH0:STACK * h + 3 * DH0, 5] = -1.0
    mask_sel[0, 3 * DH0::STACK] = 1.0

    wo0 = np.zeros((P, 2, P), np.float32)
    for n in range(2):
        wo0[E0 * n:E0 * n + E0, n] = a["L0_xattn_Wo"].T

    def ffn(gate, up, down):
        n = -(-gate.shape[0] // P)
        o = np.zeros((n, P, 3 * D), np.float32)
        for u, w in enumerate((gate, up)):
            full = np.zeros((n * P, D), np.float32)
            full[:w.shape[0]] = w
            o[:, :, u * D:(u + 1) * D] = full.reshape(n, P, KC, P).transpose(0, 3, 2, 1).reshape(n, P, D)
        full = np.zeros((n * P, D), np.float32)
        full[:down.shape[1]] = down.T
        o[:, :, 2 * D:] = full.reshape(n, P, D)
        return o

    w12, b12 = a["L1_ffn_w12"], a["L1_ffn_b12"]
    arrays = {
        "x": a["x"],
        "ctx": a["ctx_4096"],
        "ctxT": chunks(a["ctx_4096"].reshape(TOK, D)),
        "mask": a["mask_Bx1x4096_ff1"],
        "mask_row": a["mask_Bx1x4096_ff1"].reshape(NB, D),
        "mask1": a["mask_1x1xSxS2_ff0"].reshape(P, P),
        "wst": wst,
        "stack_col": stack_col,
        "mask_sel": mask_sel,
        "wv0": a["L0_xattn_Wv"].T,
        "bv0": a["L0_xattn_bv"].reshape(1, E0),
        "wo0": wo0,
        "bo0": a["L0_xattn_bo"].reshape(P, 1),
        "ffn0": ffn(a["L0_ffn_w_gate"], a["L0_ffn_w_up"], a["L0_ffn_w_down"]),
        "wkv": np.concatenate([chunks(a["L1_xattn_Wk"]), chunks(a["L1_xattn_Wv"])], 1),
        "wq": a["L1_xattn_Wq"].reshape(KVH, GROUP, P, KC, P).transpose(0, 4, 1, 3, 2),
        "wo": a["L1_xattn_Wo"].T.reshape(KVH, GROUP, HD, D).transpose(0, 2, 1, 3),
        "norm_w": np.stack([a["L1_xattn_q_norm_w"], a["L1_xattn_k_norm_w"]], 1),
        "ffn1": ffn(w12[:D], w12[D:], a["L1_ffn_w3"]),
        "b12": b12.reshape(2, CH1, P).transpose(2, 0, 1),
        "b3": a["L1_ffn_b3"].reshape(1, D),
    }
    nc = _bacc.Bacc("TRN2", target_bir_lowering=False, num_devices=1)
    feeds, A = {}, {}
    for name, v in arrays.items():
        v = np.ascontiguousarray(v)
        feeds[f"in_{name}"] = v
        A[name] = nc.dram_tensor(f"in_{name}", v.shape, mybir.dt.from_np(v.dtype), kind="ExternalInput").ap()
    out = nc.dram_tensor("out_0", (NB, P, D), F32, kind="ExternalOutput").ap()
    build(nc, A, out)
    r = _run(nc, [feeds], core_ids=[0])
    return r.results[0]["out_0"]
```

```python
from contextlib import ExitStack

import concourse.bass as bass
from concourse import mybir

F32 = mybir.dt.float32
FR = mybir.dt.float32r
ACT = mybir.ActivationFunctionType
ALU = mybir.AluOpType
AX_X = mybir.AxisListType.X

P = 128
NB = 8
D = 512
KC = D // P
TOK = NB * P
HALF = TOK // 2
EPS = 1e-5

H0, DH0 = 8, 8
E0 = H0 * DH0
STACK = 32
NPATCH = D // P
MASKED = -1e30

KVH, GROUP, HD = 8, 4, 128

INTER = 1376
CH0 = (INTER + P - 1) // P
CH1 = D // P


def wait(eng, sem, value):
    if isinstance(value, int) and value <= 0:
        return
    eng.wait_ge(sem, value)


def build(nc, A, out):
    with ExitStack() as ctx:
        def alloc(stack):
            return lambda name, shape, dt=F32: stack.enter_context(nc.sbuf_tensor(name, shape, dt))

        def sem(name):
            return ctx.enter_context(nc.semaphore(name))

        ps = ctx.enter_context(nc.psum_tensor("ps", [P, 8, 512], F32))

        g_ = alloc(ctx)
        x = g_("x", [P, NB, D])
        ffn_stage = g_("ffn_stage", [P, 2, 3 * D])
        ident = g_("ident", [P, P])
        ones_col = g_("ones_col", [P, 1])
        neghalf = g_("neghalf", [P, NB * 4])
        kv_stage = ffn_stage[:].rearrange("p a n -> p (a n)").rearrange("p (a n) -> p a n", n=KVH * HD)
        stats = g_("stats", [P, NB, 6])
        meanvar = g_("meanvar", [P, NB, 2])
        vareps = g_("vareps", [P, NB])
        rstd = g_("rstd", [P, NB])

        kT_dram = nc.dram_tensor("kT_scratch", (KVH, HD, TOK), F32, kind="Internal").ap()
        v_dram = nc.dram_tensor("v_scratch", (KVH, P, NB, HD), F32, kind="Internal").ap()

        with ExitStack() as l0:
            a_ = alloc(l0)
            wkv_hi = a_("wkv_hi", [P, 2, KC, KVH * HD], FR)
            wkv_lo = a_("wkv_lo", [P, 2, KC, KVH * HD], FR)
            work0 = a_("work0", [P, 2, 4, 4, P])
            pT0 = a_("pT0", [P, 4, 4, P])
            v_aug = a_("v_aug", [P, NPATCH, H0, DH0 + 1])
            v_next = a_("v_next", [P, 2, H0, DH0])
            smax0 = a_("smax0", [P, 16])
            rden0 = a_("rden0", [P, 2, H0])
            wst_stage = a_("wst_stage", [P, 4, P])
            wst_hi = a_("wst_hi", [P, 4, P], FR)
            wst_lo = a_("wst_lo", [P, 4, P], FR)
            stack_col = a_("stack_col", [P, 10])
            wv0 = a_("wv0", [P, E0])
            bv0 = a_("bv0", [P, E0])
            mask_sel = a_("mask_sel", [1, P], FR)
            mask_sel_s = a_("mask_sel_s", [1, P])
            mask_row = a_("mask_row", [1, 512])
            mask_step = a_("mask_step", [1, 512])
            mask_bias = a_("mask_bias", [1, 512], FR)
            knorm_w = a_("knorm_w", [P, 3])
            o_tile = a_("o_tile", [P, NPATCH, E0])
            mask_b = a_("mask_b", [P, 512])
            wo0_stage = a_("wo0_stage", [P, 2, P])
            wo0_hi = a_("wo0_hi", [P, 2, P], FR)
            wo0_lo = a_("wo0_lo", [P, 2, P], FR)
            bo0 = a_("bo0", [P, 1])
            gel = a_("gel", [P, 2, P])
            gel_hi = a_("gel_hi", [P, 2, P], FR)
            gel_lo = a_("gel_lo", [P, 2, P], FR)
            delta0 = a_("delta0", [P, 512])
            q_stack = a_("q_stack", [P, 2, 512], FR)
            k_stack = a_("k_stack", [P, 2, 512], FR)
            neg_hi = a_("neg_hi", [P, 4, 512], FR)
            xn0 = a_("xn0", [P, 512])
            xn0_hi = a_("xn0_hi", [P, 512], FR)
            xn0_lo = a_("xn0_lo", [P, 512], FR)
            ctxT_stage = a_("ctxT_stage", [P, KC, P])
            ctxT_hi = a_("ctxT_hi", [P, KC, P], FR)
            ctxT_lo = a_("ctxT_lo", [P, KC, P], FR)
            k_raw = a_("k_raw", [P, KVH, HD])
            k_norm = a_("k_norm", [P, KVH, HD])
            kT_out = a_("kT_out", [P, KVH, P])
            v_out = a_("v_out", [P, KVH, HD])
            ksum = a_("ksum", [P, KVH])
            kvar = a_("kvar", [P, KVH])
            krstd = a_("krstd", [P, KVH])
            ctx_nat = a_("ctx_nat", [P, 512])

        rest = ctx.enter_context(ExitStack())
        r_ = alloc(rest)
        hT_hi = r_("hT_hi", [P, KC, TOK], FR)
        hT_lo = r_("hT_lo", [P, KC, TOK], FR)
        xn = r_("xn", [P, 4, D])
        wq_stage = r_("wq_stage", [P, GROUP, KC, P])
        wo_stage = r_("wo_stage", [P, GROUP, D])
        kT = r_("kT", [P, TOK])
        v_stage = r_("v_stage", [P, NB, HD])
        wq_hi = r_("wq_hi", [P, GROUP, KC, P], FR)
        wq_lo = r_("wq_lo", [P, GROUP, KC, P], FR)
        wo_hi = r_("wo_hi", [P, GROUP, D], FR)
        wo_lo = r_("wo_lo", [P, GROUP, D], FR)
        v_hi = r_("v_hi", [P, NB, HD], FR)
        v_lo = r_("v_lo", [P, NB, HD], FR)
        prob = r_("prob", [P, 4, GROUP, P])
        pT_hi = r_("pT_hi", [P, 2, GROUP * P], FR)
        pT_lo = r_("pT_lo", [P, 2, GROUP * P], FR)
        mask1 = r_("mask1", [P, P])
        qvar = r_("qvar", [P, 4, GROUP])
        rq = r_("rq", [P, 2, 4, GROUP])
        negmax = r_("negmax", [P, NB, GROUP])
        psum1 = r_("psum1", [P, NB, GROUP])
        rden1 = r_("rden1", [P, NB, GROUP])
        b12 = r_("b12", [P, 2, CH1])
        b3 = r_("b3", [P, D])
        with ExitStack() as att:
            t_ = alloc(att)
            qT = t_("qT", [P, GROUP, HALF])
            q_sq = t_("q_sq", [P, GROUP, HALF])
            oT_hi = t_("oT_hi", [P, 4, GROUP, P], FR)
            oT_lo = t_("oT_lo", [P, 4, GROUP, P], FR)
        with ExitStack() as ff:
            t_ = alloc(ff)
            ffn_w = t_("ffn_w", [P, 2, 2, 3 * D], FR)
            ffn_hi, ffn_lo = ffn_w[:, :, 0], ffn_w[:, :, 1]
            silu = t_("silu", [P, 2, 512])
            gated = t_("gated", [P, 2, 512])
            gT_hi = t_("gT_hi", [P, 2, 512], FR)
            gT_lo = t_("gT_lo", [P, 2, 512], FR)

        names = """const_in x_in0 x_in kvw_in0 kvw_in1 kvw_in2 ctxT_in ctx_in mask_in maskb_ready maskb_in kT_written
            v_written const_ready ident_zero ident_ready col_ready wst_hi_ready wst_lo_ready kvw_hi_ready wk_lo_ready
            wv_lo_ready factor_ready stat_step l0_rstd_ready xn_ready xh_ready xl_ready th_ready tl_ready vaug_ready
            k_done k_copied ksum_ready krstd_step knorm_ready stack_done neghi_ready stack_ready v0_done
            v0_ready vnext_ready v_done v_copied kT_done kT_copied
            s0_done max0_ready sub0_ready exp0_ready t0_done t0_by_act t0_by_dve pv0_done rden0_ready o0_ready
            oT0_done gelu_ready gelhi_ready gello_ready wo0_done delta0_ready x0_ready wo0_split
            wq_in wo_in kT_in v_in att_const_in out_written
            wq_hi_ready wq_lo_ready wo_hi_ready wo_lo_ready v_hi_ready v_lo_ready
            q_done sq_ready q_copied ss_done qvar_ready rq_ready
            s_done masked_ready negmax_ready exp_ready rden_ready pn_ready
            t_done pthi_ready ptlo_ready pv_done ohi_ready olo_ready wo_done x_added biased""".split()
        S = {n: sem(n) for n in names}
        LN = [{n: sem(f"ln{i}_{n}") for n in ("step", "rstd_ready", "xn_ready", "t_done", "hi_ready", "lo_ready")}
              for i in range(3)]
        FF = [{n: sem(f"ffn{i}_{n}") for n in (
            "w_in0", "w_in1", "whi_ready", "wlo_ready", "gu_done", "silu_ready", "gated_ready", "ghi_ready",
            "glo_ready", "down_done", "x_added")} for i in range(2)]

        A_BANK, B_BANK = 6, 7
        T_BANKS = 4, 6
        LN_BANKS = (((1, 3), (1, 3)), ((0, 2), (2, 3)), ((2, 3), (1, 3)))
        FIRST_TURNS = (), (4,), (5,), (6, 7)
        STACKS = ((1, 4), (0, B_BANK), (2, 5), (3, A_BANK))
        scores0 = ps[:, 0:4, :].rearrange("p a (s n) -> p a s n", s=4)

        block = ctx.enter_context(nc.Block())

        @block.sync
        def _(sp):
            sp.dma_start(x[:, 0], A["x"][0]).then_inc(S["x_in0"], 16)
            for dst, src in ((wst_stage[:], A["wst"]), (stack_col[:, 0:6], A["stack_col"]), (wv0[:], A["wv0"]),
                             (mask_sel_s[:], A["mask_sel"]),
                             (bv0[:], A["bv0"].partition_broadcast(P)), (wo0_stage[:], A["wo0"]),
                             (bo0[:], A["bo0"]), (knorm_w[:, 0:2], A["norm_w"])):
                sp.dma_start(dst, src).then_inc(S["const_in"], 16)
            sp.dma_start(mask_row[:], A["mask_row"][0:1]).then_inc(S["mask_in"], 16)
            sp.dma_start(ctx_nat[:], A["ctx"][0]).then_inc(S["ctx_in"], 16)
            sp.dma_start(ctxT_stage[:], A["ctxT"][:, :, 0:P]).then_inc(S["ctxT_in"], 16)

            def kvw_load(c):
                wait(sp, S["wk_lo_ready"], min(c - 2, KC))
                wait(sp, S["wv_lo_ready"], c - 2 - KC)
                sp.dma_start(kv_stage[:, c % 3], A["wkv"][:, c]).then_inc(S[f"kvw_in{c % 3}"], 16)
            for c in range(3):
                kvw_load(c)
            sp.dma_start(x[:, 1:], A["x"][1:].rearrange("b p s -> p b s")).then_inc(S["x_in"], 16)

            def l0_loads(b):
                sp.wait_ge(S["maskb_ready"], 2 * b + 2)
                sp.dma_start(mask_row[:], A["mask_row"][bass.ds(b + 1, 1)]).then_inc(S["mask_in"], 16)
                sp.wait_ge(S["th_ready"], b + 1)
                sp.wait_ge(S["tl_ready"], b + 1)
                sp.dma_start(ctxT_stage[:], A["ctxT"][:, :, bass.ds((b + 1) * P, P)]).then_inc(S["ctxT_in"], 16)
                sp.wait_ge(S["v0_done"], b + 1)
                sp.dma_start(ctx_nat[:], A["ctx"][bass.ds(b + 1, 1)].rearrange("a p s -> p (a s)"))\
                  .then_inc(S["ctx_in"], 16)

            def l0_stores(b):
                sp.wait_ge(S["v_copied"], 2 * b + 2)
                sp.dma_start(v_dram[:, :, bass.ds(b, 1), :].rearrange("g p a d -> p g (a d)"), v_out[:])\
                  .then_inc(S["v_written"], 16)
                sp.wait_ge(S["kT_copied"], 2 * b + 2)
                sp.dma_start(kT_dram[:, :, bass.ds(b * P, P)].rearrange("g d t -> d g t"), kT_out[:])\
                  .then_inc(S["kT_written"], 16)
                wait(sp, S["delta0_ready"], b)
                sp.dma_start(mask_b[:], A["mask"][bass.ds(b, 1)].rearrange("a o s -> (a o) s")
                             .partition_broadcast(P)).then_inc(S["maskb_in"], 16)

            for c in range(3, 7):
                kvw_load(c)
            l0_loads(0)
            kvw_load(7)
            l0_stores(0)
            sp.wait_ge(S["wv_lo_ready"], KC)
            for c in range(2):
                sp.dma_start(ffn_stage[:, c], A["ffn0"][c]).then_inc(FF[0][f"w_in{c}"], 16)
            l0_loads(1)
            l0_stores(1)
            with sp.Fori(2, NB - 1) as b:
                l0_loads(b)
                l0_stores(b)
            l0_stores(NB - 1)

            def ffn_load(i, c, slot):
                sp.wait_ge(FF[i]["wlo_ready"], c - 1)
                sp.dma_start(ffn_stage[:, slot], A[f"ffn{i}"][bass.ds(c, 1)].rearrange("a p n -> p (a n)"))\
                  .then_inc(FF[i][f"w_in{slot}"], 16)
            ffn_load(0, 2, 0)
            sp.wait_ge(S["x0_ready"], NB)
            sp.dma_start(mask1[:], A["mask1"]).then_inc(S["att_const_in"], 16)
            sp.dma_start(b12[:], A["b12"]).then_inc(S["att_const_in"], 16)
            sp.dma_start(b3[:], A["b3"].partition_broadcast(P)).then_inc(S["att_const_in"], 16)
            sp.wait_ge(S["kT_written"], 16 * NB)
            sp.wait_ge(S["v_written"], 16 * NB)

            def att_load(g):
                wait(sp, S["wq_lo_ready"], g)
                sp.dma_start(wq_stage[:], A["wq"][bass.ds(g, 1)].rearrange("a p h k n -> p (a h) k n"))\
                  .then_inc(S["wq_in"], 16)
                wait(sp, S["s_done"], 8 * g)
                sp.dma_start(kT[:], kT_dram[bass.ds(g, 1)].rearrange("a p n -> p (a n)")).then_inc(S["kT_in"], 16)
                wait(sp, S["v_lo_ready"], g)
                sp.dma_start(v_stage[:], v_dram[bass.ds(g, 1)].rearrange("a p b d -> p (a b) d")).then_inc(S["v_in"], 16)
                wait(sp, S["wo_lo_ready"], g)
                sp.dma_start(wo_stage[:], A["wo"][bass.ds(g, 1)].rearrange("a p h n -> p (a h) n"))\
                  .then_inc(S["wo_in"], 16)
            att_load(0)
            with sp.Fori(3, CH0 - 1, 2) as c:
                ffn_load(0, c, 1)
                ffn_load(0, c + 1, 0)
            with sp.Fori(1, KVH) as g:
                att_load(g)
            sp.wait_ge(FF[0]["wlo_ready"], CH0)
            for c in range(2):
                sp.dma_start(ffn_stage[:, c], A["ffn1"][c]).then_inc(FF[1][f"w_in{c}"], 16)
            for c in range(2, CH1):
                ffn_load(1, c, c % 2)
            for t in range(NB):
                sp.wait_ge(FF[1]["x_added"], NB * (CH1 - 1) + t + 1)
                sp.dma_start(out[t], x[:, t]).then_inc(S["out_written"], 16)
            sp.wait_ge(S["out_written"], 16 * NB)

        @block.gpsimd
        def _(pool):
            V = nc.gpsimd
            V.memset(ident[:], 0.0).then_inc(S["ident_zero"], 1)
            V.memset(neghalf[:], -0.5).then_inc(S["const_ready"], 1)
            V.memset(ones_col[:], 1.0).then_inc(S["const_ready"], 1)
            V.memset(v_aug[:], 1.0).then_inc(S["vaug_ready"], 1)
            pool.wait_ge(S["ident_zero"], 1)
            V.affine_select(out=ident[:], in_=ident[:], compare_op=ALU.not_equal, fill=1.0, base=0,
                            pattern=[[-1, P]], channel_multiplier=1).then_inc(S["ident_ready"], 1)
            pool.wait_ge(S["wst_hi_ready"], 1)
            V.tensor_tensor(wst_lo[:], wst_stage[:], wst_hi[:].bitcast(F32), ALU.subtract).then_inc(S["wst_lo_ready"], 1)
            pool.wait_ge(S["const_ready"], 2)
            pool.wait_ge(S["stat_step"], 3)
            V.tensor_tensor(rstd[:, 0:1], vareps[:, 0:1], neghalf[:, 0:1], ALU.pow).then_inc(S["l0_rstd_ready"], 1)

            def x_low(b):
                pool.wait_ge(S["xh_ready"], b + 1)
                V.tensor_tensor(xn0_lo[:], xn0[:], xn0_hi[:].bitcast(F32), ALU.subtract).then_inc(S["xl_ready"], 1)

            def t_low(b):
                pool.wait_ge(S["th_ready"], b + 1)
                V.tensor_tensor(ctxT_lo[:], ctxT_stage[:], ctxT_hi[:].bitcast(F32), ALU.subtract)\
                 .then_inc(S["tl_ready"], 1)

            def gel_low(b):
                pool.wait_ge(S["gelhi_ready"], b + 1)
                wait(pool, S["wo0_done"], b)
                V.tensor_tensor(gel_lo[:], gel[:], gel_hi[:].bitcast(F32), ALU.subtract).then_inc(S["gello_ready"], 1)
            x_low(0)
            t_low(0)
            for k in range(KC):
                pool.wait_ge(S["kvw_hi_ready"], KC + k + 1)
                V.tensor_tensor(wkv_lo[:, 1, k], kv_stage[:, (KC + k) % 3], wkv_hi[:, 1, k].bitcast(F32), ALU.subtract)\
                 .then_inc(S["wv_lo_ready"], 1)
            pool.wait_ge(S["stat_step"], 3 + 2 * (NB - 1) + 1)
            V.tensor_tensor(rstd[:, 1:], vareps[:, 1:], neghalf[:, 1:NB], ALU.pow).then_inc(S["l0_rstd_ready"], 1)

            def l0_step(b, first=False, last=False):
                if not last:
                    x_low(b + 1)
                pool.wait_ge(S["krstd_step"], 2 * b + 1)
                V.tensor_tensor(krstd[:], kvar[:], neghalf[:, 0:KVH], ALU.pow).then_inc(S["krstd_step"], 1)
                pool.wait_ge(S["krstd_step"], 2 * b + 2)
                V.tensor_tensor(k_norm[:], k_raw[:], krstd[:].unsqueeze(2).broadcast_to([P, KVH, HD]), ALU.mult)\
                 .then_inc(S["knorm_ready"], 1)
                if not first:
                    gel_low(b - 1)
                if not last:
                    t_low(b + 1)
            l0_step(0, first=True)
            l0_step(1)
            with pool.Fori(2, NB - 1) as b:
                l0_step(b)
            l0_step(NB - 1, last=True)

            def ln_rstd(i, half):
                pool.wait_ge(LN[i]["step"], 9 * half + 9)
                tiles = slice(4 * half, 4 * half + 4)
                V.tensor_tensor(rstd[:, tiles], vareps[:, tiles], neghalf[:, tiles], ALU.pow)\
                 .then_inc(LN[i]["rstd_ready"], 1)

            def ffn_low(i, c, slot):
                pool.wait_ge(FF[i]["whi_ready"], c + 1)
                V.tensor_tensor(ffn_lo[:, slot], ffn_stage[:, slot], ffn_hi[:, slot].bitcast(F32), ALU.subtract)\
                 .then_inc(FF[i]["wlo_ready"], 1)

            def ffn(i, n):
                if i == 0:
                    ln_rstd(0, 0)
                    ffn_low(0, 0, 0)
                    gel_low(NB - 1)
                else:
                    ffn_low(1, 0, 0)
                    ln_rstd(2, 0)
                ln_rstd(2 * i, 1)
                ffn_low(i, 1, 1)
                if n > 4:
                    with pool.Fori(2, n - 1, 2) as c:
                        ffn_low(i, c, 0)
                        ffn_low(i, c + 1, 1)
                    ffn_low(i, n - 1, 0)
                else:
                    for c in range(2, n):
                        ffn_low(i, c, c % 2)

            ffn(0, CH0)

            def low(name, lo, stage, hi, g):
                pool.wait_ge(S[f"{name}_hi_ready"], g + 1)
                V.tensor_tensor(lo[:], stage[:], hi[:].bitcast(F32), ALU.subtract).then_inc(S[f"{name}_lo_ready"], 1)

            def q_rstd(g, half):
                pool.wait_ge(S["qvar_ready"], 2 * g + half + 1)
                for b in (slice(0, 1), slice(1, 4)):
                    V.tensor_tensor(rq[:, half, b], qvar[:, b], neghalf[:].rearrange("p (a b) -> p a b", b=GROUP)[:, b],
                                    ALU.pow).then_inc(S["rq_ready"], 1)

            def normalise(g, b):
                pool.wait_ge(S["rden_ready"], NB * g + b + 1)
                V.tensor_tensor(prob[:, b % 4], prob[:, b % 4],
                                rden1[:, b].unsqueeze(2).broadcast_to([P, GROUP, P]), ALU.mult)\
                 .then_inc(S["pn_ready"], 1)

            def att_step(g, last=False):
                q_rstd(g, 0)
                low("v", v_lo, v_stage, v_hi, g)
                for b in range(4):
                    normalise(g, b)
                low("wo", wo_lo, wo_stage, wo_hi, g)
                q_rstd(g, 1)
                if not last:
                    low("wq", wq_lo, wq_stage, wq_hi, g + 1)
                for b in range(4, 8):
                    normalise(g, b)
            low("wq", wq_lo, wq_stage, wq_hi, 0)
            ln_rstd(1, 0)
            ln_rstd(1, 1)
            with pool.Fori(0, KVH - 1) as g:
                att_step(g)
            att_step(KVH - 1, last=True)
            ffn(1, CH1)

        @block.scalar
        def _(act):
            def copy(o, i):
                return nc.scalar.activation(o, i, ACT.Copy)

            act.wait_ge(S["const_in"], 16 * 8)
            copy(wst_hi[:], wst_stage[:]).then_inc(S["wst_hi_ready"], 1)
            copy(mask_sel[:], mask_sel_s[:]).then_inc(S["wst_hi_ready"], 1)
            copy(wo0_hi[:], wo0_stage[:]).then_inc(S["wo0_split"], 1)

            def x_high(b):
                act.wait_ge(S["xn_ready"], b + 1)
                wait(act, S["stack_done"], 4 * b)
                copy(xn0_hi[:], xn0[:]).then_inc(S["xh_ready"], 1)

            def t_high(b):
                act.wait_ge(S["ctxT_in"], 16 * (b + 1))
                wait(act, S["v_done"], 2 * b)
                copy(ctxT_hi[:], ctxT_stage[:]).then_inc(S["th_ready"], 1)

            def kvw_high(c):
                act.wait_ge(S[f"kvw_in{c % 3}"], 16 * (c // 3 + 1))
                copy(wkv_hi[:, c // KC, c % KC], kv_stage[:, c % 3]).then_inc(S["kvw_hi_ready"], 1)

            def evac_t0(pair, r):
                act.wait_ge(S["t0_done"], 4 * pair + r + 1)
                wait(act, S["pv0_done"], pair)
                copy(pT0[:, r], ps[:, 4 + r % 2].rearrange("p (s n) -> p s n", s=4)).then_inc(S["t0_by_act"], 1)

            def exp0(pair, q):
                act.wait_ge(S["sub0_ready"], pair + 1)
                nc.scalar.activation(work0[:, q], work0[:, q], ACT.Exp, scale=float(DH0) ** -0.5)\
                  .then_inc(S["exp0_ready"], 1)

            def heads(bank):
                return ps[:, bank].rearrange("p (h d) -> p h d", h=4)

            def k_copy(b, n):
                act.wait_ge(S["k_done"], 2 * b + n + 1)
                wait(act, S["knorm_ready"], b)
                copy(k_raw[:, 4 * n:4 * n + 4], heads(A_BANK)).then_inc(S["k_copied"], 1)

            def v_copy(b, n):
                act.wait_ge(S["v_done"], 2 * b + n + 1)
                wait(act, S["v_written"], 16 * b)
                copy(v_out[:, 4 * n:4 * n + 4], heads(A_BANK)).then_inc(S["v_copied"], 1)

            def kT_copy(b, n):
                act.wait_ge(S["kT_done"], 2 * b + n + 1)
                wait(act, S["kT_written"], 16 * b)
                nc.scalar.activation(kT_out[:, 4 * n:4 * n + 4], heads((A_BANK, B_BANK)[n]), ACT.Copy, scale=knorm_w[:, 2:3])\
                  .then_inc(S["kT_copied"], 1)

            def neg_high(b, i):
                m, bank = STACKS[i]
                act.wait_ge(S["stack_done"], 4 * b + i + 1)
                wait(act, S["stack_ready"], 4 * b)
                nc.scalar.activation(neg_hi[:, m], ps[:, bank], ACT.Identity, bias=stack_col[:, 6 + m:7 + m],
                                     scale=stack_col[:, 4 + m % 2:5 + m % 2]).then_inc(S["neghi_ready"], 1)

            def gelu(b):
                act.wait_ge(S["oT0_done"], b + 1)
                wait(act, S["gello_ready"], b)
                nc.scalar.activation(gel[:], ps[:, B_BANK, 0:2 * P].rearrange("p (s n) -> p s n", s=2), ACT.Gelu)\
                  .then_inc(S["gelu_ready"], 1)
                act.wait_ge(S["gelu_ready"], b + 1)
                wait(act, S["wo0_done"], b)
                copy(gel_hi[:], gel[:]).then_inc(S["gelhi_ready"], 1)

            x_high(0)
            act.wait_ge(S["col_ready"], 1)
            act.wait_ge(S["factor_ready"], 1)
            kvw_high(0)
            kvw_high(1)
            neg_high(0, 0)
            neg_high(0, 1)
            kvw_high(2)
            neg_high(0, 2)
            t_high(0)
            neg_high(0, 3)
            for c in range(3, 7):
                kvw_high(c)

            def l0_step(b, first=False, last=False):
                if not first:
                    evac_t0(2 * b - 1, 0)
                k_copy(b, 0)
                if not first:
                    evac_t0(2 * b - 1, 2)
                exp0(2 * b, 0)
                if first:
                    kvw_high(7)
                k_copy(b, 1)
                act.wait_ge(S["k_copied"], 2 * b + 2)
                wait(act, S["kT_done"], 2 * b)
                for h in range(KVH):
                    last_sq = nc.scalar.activation(k_norm[:, h], k_raw[:, h], ACT.Square, accum_out=ksum[:, h:h + 1])
                last_sq.then_inc(S["ksum_ready"], 1)
                if not last:
                    x_high(b + 1)
                evac_t0(2 * b, 0)
                if not first:
                    gelu(b - 1)
                v_copy(b, 0)
                evac_t0(2 * b, 2)
                exp0(2 * b + 1, 1)
                v_copy(b, 1)
                if not last:
                    t_high(b + 1)
                kT_copy(b, 0)
                if not last:
                    for i in range(4):
                        neg_high(b + 1, i)
                kT_copy(b, 1)

            l0_step(0, first=True)
            l0_step(1)
            with act.Fori(2, NB - 1) as b:
                l0_step(b)
            l0_step(NB - 1, last=True)

            def ln(i, tiles):
                for t in tiles:
                    act.wait_ge(LN[i]["t_done"], t + 1)
                    copy(hT_hi[:, :, t * P:(t + 1) * P],
                         ps[:, LN_BANKS[i][t // 4][t % 2]].rearrange("p (k n) -> p k n", k=KC))\
                        .then_inc(LN[i]["hi_ready"], 1)

            def ffn_high(i, c, slot):
                act.wait_ge(FF[i][f"w_in{slot}"], 8 * c + (8 if slot else 16))
                wait(act, FF[i]["down_done"], NB * (c - 1))
                copy(ffn_hi[:, slot], ffn_stage[:, slot]).then_inc(FF[i]["whi_ready"], 1)

            def ffn_act(i, c, slot, prefetch):
                for half in range(2):
                    act.wait_ge(FF[i]["gu_done"], 2 * c + half + 1)
                    wait(act, FF[i]["gated_ready"], 2 * c + half - 1)
                    bias = b12[:, 0, c:c + 1] if i == 1 else 0.0
                    nc.scalar.activation(silu[:, half], ps[:, half], ACT.Silu, bias=bias)\
                      .then_inc(FF[i]["silu_ready"], 1)
                    act.wait_ge(FF[i]["gated_ready"], 2 * c + half + 1)
                    wait(act, FF[i]["down_done"], NB * (c - 1) + 4 + 4 * half)
                    copy(gT_hi[:, half], gated[:, half]).then_inc(FF[i]["ghi_ready"], 1)
                    if half == 0 and prefetch:
                        ffn_high(i, c + 1, 1 - slot)

            def high(name, hi, stage, g):
                act.wait_ge(S[f"{name}_in"], 16 * (g + 1))
                copy(hi[:], stage[:]).then_inc(S[f"{name}_hi_ready"], 1)

            def ffn(i, n):
                ln(2 * i, range(4, NB))
                ffn_act(i, 0, 0, True)
                if n > 4:
                    with act.Fori(1, n - 2, 2) as c:
                        ffn_act(i, c, 1, True)
                        ffn_act(i, c + 1, 0, True)
                    ffn_act(i, n - 2, 1, True)
                    high("wq", wq_hi, wq_stage, 0)
                    ffn_act(i, n - 1, 0, False)
                else:
                    for c in range(1, n):
                        ffn_act(i, c, c % 2, c < n - 1)

            evac_t0(2 * NB - 1, 0)
            evac_t0(2 * NB - 1, 2)
            act.wait_ge(S["kT_written"], 16 * NB)
            act.wait_ge(S["v_written"], 16 * NB)
            ffn_high(0, 0, 0)
            ln(0, range(2))
            gelu(NB - 1)
            ln(0, range(2, 4))
            ffn(0, CH0)

            def q_out(g, half, h):
                n = 8 * g + 4 * half + h
                act.wait_ge(S["q_done"], n + 1)
                wait(act, S["ss_done"], n - 3)
                nc.scalar.activation(q_sq[:, h], ps[:, h % 2], ACT.Square).then_inc(S["sq_ready"], 1)

            def exps(g, b):
                act.wait_ge(S["negmax_ready"], 8 * g + b + 1)
                for h in range(GROUP):
                    e = nc.scalar.activation(prob[:, b % 4, h], prob[:, b % 4, h], ACT.Exp,
                                             bias=negmax[:, b, h:h + 1], accum_out=psum1[:, b, h:h + 1])
                e.then_inc(S["exp_ready"], 1)

            def p_part(g, b):
                n = 8 * g + b
                act.wait_ge(S["t_done"], n + 1)
                wait(act, S["pv_done"], n - 1)
                copy(pT_hi[:, b % 2], ps[:, T_BANKS[b % 2]]).then_inc(S["pthi_ready"], 1)

            def o_high(g, b):
                n = 8 * g + b
                act.wait_ge(S["pv_done"], n + 1)
                wait(act, S["wo_done"], n - 3)
                copy(oT_hi[:, b % 4], ps[:, 5].rearrange("p (h n) -> p h n", h=GROUP)).then_inc(S["ohi_ready"], 1)

            def att_step(g, first=False, last=False):
                for j in range(4):
                    q_out(g, 0, j)
                    if first:
                        ln(1, FIRST_TURNS[j])
                    else:
                        if j == 0:
                            exps(g - 1, 7)
                        p_part(g - 1, 4 + j)
                        if j >= 1:
                            o_high(g - 1, 3 + j)
                if not first:
                    o_high(g - 1, 7)
                high("v", v_hi, v_stage, g)
                if first:
                    high("wo", wo_hi, wo_stage, g)
                for j in range(3):
                    exps(g, j)
                if not first:
                    act.wait_ge(S["wo_done"], 8 * g)
                    high("wo", wo_hi, wo_stage, g)
                for j in range(4):
                    q_out(g, 1, j)
                    if j == 0:
                        exps(g, 3)
                    p_part(g, j)
                    if j >= 1:
                        o_high(g, j - 1)
                if not last:
                    act.wait_ge(S["q_done"], 8 * g + 8)
                    high("wq", wq_hi, wq_stage, g + 1)
                o_high(g, 3)
                for j in range(4, 7):
                    exps(g, j)

            ln(1, range(4))
            att_step(0, first=True)
            with act.Fori(1, KVH - 1) as g:
                att_step(g)
            att_step(KVH - 1, last=True)
            g = KVH - 1
            p_part(g, 4)
            p_part(g, 5)
            exps(g, 7)
            o_high(g, 4)
            p_part(g, 6)
            o_high(g, 5)
            p_part(g, 7)
            act.wait_ge(S["s_done"], NB * KVH)
            ffn_high(1, 0, 0)
            o_high(g, 6)
            o_high(g, 7)
            ln(2, range(4))
            ffn(1, CH1)

        @block.vector
        def _(dve):
            V = nc.vector

            dve.wait_ge(S["const_in"], 16 * 8)
            V.tensor_scalar(knorm_w[:, 2:3], knorm_w[:, 0:1], knorm_w[:, 1:2], float(HD) ** -0.5,
                            ALU.mult, ALU.mult).then_inc(S["factor_ready"], 1)
            V.tensor_tensor(stack_col[:, 6:10].rearrange("p (a b) -> p a b", b=2),
                            stack_col[:, 0:4].rearrange("p (a b) -> p a b", b=2),
                            stack_col[:, 4:6].unsqueeze(1).broadcast_to([P, 2, 2]), ALU.mult)\
             .then_inc(S["col_ready"], 1)

            def tile_stats(s, t):
                V.bn_stats(stats[:, t], x[:, t]).then_inc(s, 1)

            def variances(s, tiles, done):
                for n, t in enumerate(tiles):
                    dve.wait_ge(s, done + n + 1)
                    V.bn_aggr(meanvar[:, t], stats[:, t]).then_inc(s, 1)
                dve.wait_ge(s, done + 2 * len(tiles))
                V.tensor_scalar(vareps[:, tiles[0]:tiles[-1] + 1], meanvar[:, tiles[0]:tiles[-1] + 1, 1], EPS, None,
                                ALU.add).then_inc(s, 1)

            dve.wait_ge(S["x_in0"], 16)
            tile_stats(S["stat_step"], 0)
            variances(S["stat_step"], [0], 0)

            def normal0(b):
                wait(dve, S["xl_ready"], b)
                V.tensor_scalar(xn0[:], x[:, bass.ds(b, 1)].rearrange("p a s -> p (a s)"),
                                meanvar[:, bass.ds(b, 1), 0:1].rearrange("p a s -> p (a s)"),
                                rstd[:, bass.ds(b, 1)], ALU.subtract, ALU.mult).then_inc(S["xn_ready"], 1)
                dve.wait_ge(S["mask_in"], 16 * (b + 1))
                V.tensor_scalar(mask_step[:], mask_row[:], 0.0, -MASKED, ALU.is_gt, ALU.mult)\
                 .then_inc(S["maskb_ready"], 1)
                dve.wait_ge(S["maskb_ready"], 2 * b + 1)
                wait(dve, S["stack_done"], 4 * b)
                V.tensor_scalar(mask_bias[:], mask_step[:], MASKED, None, ALU.add).then_inc(S["maskb_ready"], 1)

            def evac_t0(pair, r):
                dve.wait_ge(S["t0_done"], 4 * pair + r + 1)
                wait(dve, S["pv0_done"], pair)
                V.tensor_copy(pT0[:, r], ps[:, 4 + r % 2].rearrange("p (s n) -> p s n", s=4))\
                 .then_inc(S["t0_by_dve"], 1)

            def out0(pair, q, turned):
                dve.wait_ge(S["pv0_done"], pair + 1)
                pv = ps[:, B_BANK, 0:2 * H0 * (DH0 + 1)].rearrange("p (s h e) -> p s h e", s=2, h=H0)
                V.reciprocal(rden0[:].unsqueeze(3), pv[:, :, :, DH0:DH0 + 1]).then_inc(S["rden0_ready"], 1)
                dve.wait_ge(S["rden0_ready"], pair + 1)
                wait(dve, S["oT0_done"], turned)
                o = o_tile[:, 2 * q:2 * q + 2].rearrange("p s (h e) -> p s h e", e=DH0)
                V.tensor_tensor(o, pv[:, :, :, 0:DH0], rden0[:].unsqueeze(3).broadcast_to([P, 2, H0, DH0]), ALU.mult)\
                 .then_inc(S["o0_ready"], 1)

            scores_flat = ps[:, 0:4].rearrange("p a (s n) -> p (a s) n", n=P)

            def max0(pair):
                dve.wait_ge(S["s0_done"], pair + 1)
                V.tensor_reduce(smax0[:], scores_flat, AX_X, ALU.max).then_inc(S["max0_ready"], 1)

            def sub0(pair, q):
                dve.wait_ge(S["max0_ready"], pair + 1)
                wait(dve, S["t0_done"], 4 * (pair - 1))
                V.tensor_tensor(work0[:, q].rearrange("p a s n -> p (a s) n"), scores_flat,
                                smax0[:].unsqueeze(2).broadcast_to([P, 16, P]), ALU.subtract)\
                 .then_inc(S["sub0_ready"], 1)

            def wk_low(k):
                dve.wait_ge(S["kvw_hi_ready"], k + 1)
                V.tensor_tensor(wkv_lo[:, 0, k], kv_stage[:, k % 3], wkv_hi[:, 0, k].bitcast(F32), ALU.subtract)\
                 .then_inc(S["wk_lo_ready"], 1)

            def stacks(b, between=lambda i: None):
                wait(dve, S["s0_done"], 2 * b)
                for i, (m, bank) in enumerate(STACKS):
                    between(i)
                    dve.wait_ge(S["neghi_ready"], 4 * b + i + 1)
                    dst = (k_stack, q_stack)[m % 2][:, m // 2]
                    V.scalar_tensor_tensor(dst, ps[:, bank], stack_col[:, m:m + 1], neg_hi[:, m].bitcast(F32),
                                           ALU.add, ALU.add).then_inc(S["stack_ready"], 1)

            def values(b):
                dve.wait_ge(S["v0_done"], b + 1)
                wait(dve, S["pv0_done"], 2 * b - 1)
                wait(dve, S["vnext_ready"], b)
                for dst, s in ((v_aug[:, 0:2, :, 0:DH0], 0), (v_next[:], 2)):
                    v = V.tensor_tensor(
                        dst, ps[:, 5, s * E0:(s + 2) * E0].rearrange("p (s h e) -> p s h e", s=2, h=H0),
                        bv0[:].rearrange("p (h e) -> p h e", e=DH0).unsqueeze(1).broadcast_to([P, 2, H0, DH0]),
                        ALU.add)
                v.then_inc(S["v0_ready"], 1)

            def values_next(b):
                wait(dve, S["pv0_done"], 2 * b)
                dve.wait_ge(S["v0_ready"], b + 1)
                V.tensor_copy(v_aug[:, 2:4, :, 0:DH0], v_next[:]).then_inc(S["vnext_ready"], 1)

            def add0(b):
                dve.wait_ge(S["wo0_done"], b + 1)
                dve.wait_ge(S["maskb_in"], 16 * (b + 1))
                wait(dve, S["x0_ready"], b)
                V.scalar_tensor_tensor(delta0[:], ps[:, 4], bo0[:], mask_b[:], ALU.add, ALU.mult)\
                 .then_inc(S["delta0_ready"], 1)
                dve.wait_ge(S["delta0_ready"], b + 1)
                x_tile = x[:, bass.ds(b, 1)].rearrange("p a s -> p (a s)")
                V.tensor_tensor(x_tile, x_tile, delta0[:], ALU.add).then_inc(S["x0_ready"], 1)

            dve.wait_ge(S["l0_rstd_ready"], 1)
            normal0(0)
            dve.wait_ge(S["wo0_split"], 1)
            V.tensor_tensor(wo0_lo[:], wo0_stage[:], wo0_hi[:].bitcast(F32), ALU.subtract).then_inc(S["wo0_split"], 1)
            dve.wait_ge(S["vaug_ready"], 1)
            wk_low(0)
            wk_low(1)
            stacks(0, lambda i: wk_low(2) if i == 3 else None)
            values(0)
            wk_low(3)

            def l0_step(b, first=False, last=False):
                max0(2 * b)
                if not first:
                    evac_t0(2 * b - 1, 1)
                sub0(2 * b, 0)
                if first:
                    dve.wait_ge(S["x_in"], 16)
                    for t in range(1, NB):
                        tile_stats(S["stat_step"], t)
                    variances(S["stat_step"], range(1, NB), 3)
                    dve.wait_ge(S["l0_rstd_ready"], 2)
                else:
                    evac_t0(2 * b - 1, 3)
                if not last:
                    normal0(b + 1)
                if not first:
                    out0(2 * b - 1, 1, b - 1)
                values_next(b)
                if last:
                    ln0_stats(range(2))
                dve.wait_ge(S["ksum_ready"], b + 1)
                V.tensor_scalar(kvar[:], ksum[:], 1.0 / HD, EPS, ALU.mult, ALU.add).then_inc(S["krstd_step"], 1)
                max0(2 * b + 1)
                evac_t0(2 * b, 1)
                sub0(2 * b + 1, 1)
                evac_t0(2 * b, 3)
                if last:
                    ln0_stats(range(2, 4))
                    ln_var(0, 0)
                out0(2 * b, 0, b)
                if not last:
                    stacks(b + 1)
                    values(b + 1)
                if not first:
                    add0(b - 1)

            def ln_stat(i, t, sem_x, added):
                dve.wait_ge(sem_x, added)
                tile_stats(LN[i]["step"], t)

            def ln_var(i, half):
                variances(LN[i]["step"], range(4 * half, 4 * half + 4), 9 * half)

            def ln_normal(i, half):
                dve.wait_ge(LN[i]["rstd_ready"], half + 1)
                for t in range(4 * half, 4 * half + 4):
                    if half:
                        dve.wait_ge(LN[i]["t_done"], t - 3)
                    V.tensor_scalar(xn[:, t % 4], x[:, t], meanvar[:, t, 0:1], rstd[:, t:t + 1],
                                    ALU.subtract, ALU.mult).then_inc(LN[i]["xn_ready"], 1)

            def ln_low(i, tiles):
                for t in tiles:
                    dve.wait_ge(LN[i]["hi_ready"], t + 1)
                    V.tensor_tensor(hT_lo[:, :, t * P:(t + 1) * P],
                                    ps[:, LN_BANKS[i][t // 4][t % 2]].rearrange("p (k n) -> p k n", k=KC),
                                    hT_hi[:, :, t * P:(t + 1) * P].bitcast(F32), ALU.subtract)\
                     .then_inc(LN[i]["lo_ready"], 1)

            def ffn_gate(i, c, half):
                dve.wait_ge(FF[i]["silu_ready"], 2 * c + half + 1)
                bias = b12[:, 1, c:c + 1] if i == 1 else 0.0
                wait(dve, FF[i]["glo_ready"], 2 * c + half - 1)
                V.scalar_tensor_tensor(gated[:, half], ps[:, 2 + half], bias, silu[:, half], ALU.add, ALU.mult)\
                 .then_inc(FF[i]["gated_ready"], 1)
                dve.wait_ge(FF[i]["ghi_ready"], 2 * c + half + 1)
                V.tensor_tensor(gT_lo[:, half], gated[:, half], gT_hi[:, half].bitcast(F32), ALU.subtract)\
                 .then_inc(FF[i]["glo_ready"], 1)

            def ffn_add(i, c, half, after=lambda t: None, before=lambda t: None):
                for t in range(4 * half, 4 * half + 4):
                    before(t)
                    dve.wait_ge(FF[i]["down_done"], NB * c + t + 1)
                    if i == 1 and isinstance(c, int) and c == 1:
                        dve.wait_ge(S["biased"], t + 1)
                    V.tensor_tensor(x[:, t], x[:, t], ps[:, 4 + t % 4], ALU.add).then_inc(FF[i]["x_added"], 1)
                    if t % 2:
                        after(t - 1)
                        after(t)

            def bias_add(tiles):
                for t in tiles:
                    dve.wait_ge(FF[1]["x_added"], t + 1)
                    V.tensor_tensor(x[:, t], x[:, t], b3[:], ALU.add).then_inc(S["biased"], 1)

            def ffn(i, n, ln_next=None):
                ln_normal(2 * i, 1)
                ln_low(2 * i, range(4, NB))
                ffn_gate(i, 0, 0)
                ffn_gate(i, 0, 1)
                ffn_add(i, 0, 0)

                def step(c):
                    ffn_gate(i, c, 0)
                    ffn_add(i, c - 1, 1)
                    if i == 1 and c == 1:
                        bias_add(range(4))
                    ffn_gate(i, c, 1)
                    ffn_add(i, c, 0)
                    if i == 1 and c == 1:
                        bias_add(range(4, NB))
                if n > 4:
                    with dve.Fori(1, n - 1) as c:
                        step(c)
                else:
                    for c in range(1, n - 1):
                        step(c)

                def stat(t):
                    if ln_next is not None:
                        ln_stat(ln_next, t, FF[i]["x_added"], NB * (n - 1) + t + 1)
                ffn_gate(i, n - 1, 0)
                ffn_add(i, n - 2, 1)
                if ln_next is not None:
                    ffn_add(i, n - 1, 0, stat)
                    ln_var(ln_next, 0)
                    ln_normal(ln_next, 0)
                    ffn_gate(i, n - 1, 1)
                else:
                    ffn_gate(i, n - 1, 1)
                    ffn_add(i, n - 1, 0)

                def low(t):
                    if ln_next is not None and t % 2 == 0:
                        ln_low(ln_next, range(t - 4, t - 2))
                ffn_add(i, n - 1, 1, stat, low)
                if ln_next is not None:
                    ln_var(ln_next, 1)

            def ln0_stats(tiles):
                for t in tiles:
                    ln_stat(0, t, S["x0_ready"], t + 1)

            l0_step(0, first=True)
            l0_step(1)
            with dve.Fori(2, NB - 1) as b:
                l0_step(b)
            l0_step(NB - 1, last=True)
            evac_t0(2 * NB - 1, 1)
            dve.wait_ge(S["v_done"], 2 * NB)
            ln_normal(0, 0)
            evac_t0(2 * NB - 1, 3)
            ln0_stats([4, 5])
            out0(2 * NB - 1, 1, NB - 1)
            ln_low(0, range(2))
            ln0_stats([6])
            ln_low(0, range(2, 4))
            add0(NB - 1)
            ln0_stats([7])
            ln_var(0, 1)
            ffn(0, CH0, ln_next=1)

            def q_copy(g, half, h):
                n = 8 * g + 4 * half + h
                dve.wait_ge(S["sq_ready"], n + 1)
                if h == 0:
                    wait(dve, S["s_done"], 8 * g + 4 * half)
                V.tensor_copy(qT[:, h], ps[:, h % 2]).then_inc(S["q_copied"], 1)

            def q_var(g, half):
                dve.wait_ge(S["ss_done"], 8 * g + 4 * half + 4)
                wait(dve, S["rq_ready"], 4 * g + 2 * half)
                V.tensor_scalar(qvar[:], ps[:, 7, 0:16].rearrange("p (b h) -> p b h", b=4), 1.0 / HD, EPS,
                                ALU.mult, ALU.add).then_inc(S["qvar_ready"], 1)

            def soft(g, b):
                n = 8 * g + b
                dve.wait_ge(S["s_done"], n + 1)
                dve.wait_ge(S["rq_ready"], 4 * g + 2 * (b // 4) + (1 if b % 4 == 0 else 2))
                wait(dve, S["t_done"], n - 3)
                for h in range(GROUP):
                    m = V.scalar_tensor_tensor(prob[:, b % 4, h], ps[:, 2 + b % 2, h * P:(h + 1) * P],
                                               rq[:, b // 4, b % 4, h:h + 1], mask1[:], ALU.mult, ALU.add)
                m.then_inc(S["masked_ready"], 1)
                dve.wait_ge(S["masked_ready"], n + 1)
                V.tensor_reduce(negmax[:, b], prob[:, b % 4], AX_X, ALU.max, negate=True)\
                 .then_inc(S["negmax_ready"], 1)

            def denominators(g, b):
                n = 8 * g + b
                dve.wait_ge(S["exp_ready"], n + 1)
                V.reciprocal(rden1[:, b], psum1[:, b]).then_inc(S["rden_ready"], 1)

            def p_part(g, b):
                n = 8 * g + b
                dve.wait_ge(S["pthi_ready"], n + 1)
                V.tensor_tensor(pT_lo[:, b % 2], ps[:, T_BANKS[b % 2]], pT_hi[:, b % 2].bitcast(F32), ALU.subtract)\
                 .then_inc(S["ptlo_ready"], 1)

            def o_low(g, b):
                n = 8 * g + b
                dve.wait_ge(S["ohi_ready"], n + 1)
                V.tensor_tensor(oT_lo[:, b % 4], ps[:, 5].rearrange("p (h n) -> p h n", h=GROUP),
                                oT_hi[:, b % 4].bitcast(F32), ALU.subtract).then_inc(S["olo_ready"], 1)

            def x_add(g, t):
                n = 8 * g + t
                dve.wait_ge(S["wo_done"], n + 1)
                V.tensor_tensor(x[:, t], x[:, t], ps[:, t % 2], ALU.add).then_inc(S["x_added"], 1)

            def att_step(g, first=False):
                for j in range(4):
                    q_copy(g, 0, j)
                    if first:
                        if j == 0:
                            ln_normal(1, 1)
                        ln_low(1, FIRST_TURNS[j])
                    else:
                        if j == 0:
                            denominators(g - 1, 7)
                        p_part(g - 1, 4 + j)
                        if j >= 1:
                            o_low(g - 1, 3 + j)
                for j in range(4):
                    if not first:
                        x_add(g - 1, 4 + j)
                        if j == 0:
                            o_low(g - 1, 7)
                    if j == 0:
                        q_var(g, 0)
                    soft(g, j)
                    if j >= 1:
                        denominators(g, j - 1)
                for j in range(4):
                    q_copy(g, 1, j)
                    if j == 0:
                        denominators(g, 3)
                    p_part(g, j)
                    if j >= 1:
                        o_low(g, j - 1)
                for j in range(4):
                    x_add(g, j)
                    if j == 0:
                        o_low(g, 3)
                        q_var(g, 1)
                    soft(g, 4 + j)
                    if j >= 1:
                        denominators(g, 4 + j - 1)

            dve.wait_ge(S["att_const_in"], 48)
            att_step(0, first=True)
            with dve.Fori(1, KVH) as g:
                att_step(g)
            g = KVH - 1

            def ln2_stat(t):
                ln_stat(2, t, S["x_added"], NB * g + t + 1)
            p_part(g, 4)
            p_part(g, 5)
            denominators(g, 7)
            o_low(g, 4)
            ln2_stat(0)
            p_part(g, 6)
            o_low(g, 5)
            ln2_stat(1)
            x_add(g, 4)
            p_part(g, 7)
            ln2_stat(2)
            o_low(g, 6)
            ln2_stat(3)
            ln_var(2, 0)
            x_add(g, 5)
            o_low(g, 7)
            ln2_stat(4)
            ln2_stat(5)
            ln_normal(2, 0)
            x_add(g, 6)
            ln_low(2, range(2))
            ln2_stat(6)
            x_add(g, 7)
            ln_low(2, range(2, 4))
            ln2_stat(7)
            ln_var(2, 1)
            ffn(1, CH1)

        @block.tensor
        def _(pe):
            T = nc.tensor

            def three(o, w_hi, w_lo, m_hi, m_lo, start, stop):
                T.matmul(o, w_hi, m_hi, start=start, stop=False)
                T.matmul(o, w_hi, m_lo, start=False, stop=False)
                return T.matmul(o, w_lo, m_hi, start=False, stop=stop)

            def project(o, w, n, half, done):
                for k in range(2 * half, 2 * half + 2):
                    last = three(o, ctxT_hi[:, k], ctxT_lo[:, k], wkv_hi[:, w, k, n * 512:(n + 1) * 512],
                                 wkv_lo[:, w, k, n * 512:(n + 1) * 512], k == 0, k == KC - 1)
                if half:
                    last.then_inc(S[done], 1)

            def scores(pair, q):
                wait(pe, S["sub0_ready"], pair)
                for s in range(4):
                    grp, patch = s // 2, 2 * q + s % 2
                    for h in range(4):
                        rows = slice(STACK * h, STACK * h + STACK)
                        cols = slice(patch * P, patch * P + P)
                        last = T.matmul(scores0[:, h, s], q_stack[rows, grp, cols], k_stack[rows, grp, cols],
                                        start=True, stop=True)
                last.then_inc(S["s0_done"], 1)

            def turn_p0(pair, q, r):
                wait(pe, S[("t0_by_act", "t0_by_dve")[r % 2]], 2 * pair + r // 2)
                for s in range(4):
                    last = T.transpose(ps[:, 4 + r % 2, s * P:(s + 1) * P], work0[:, q, r, s], ident[:])
                last.then_inc(S["t0_done"], 1)

            def times_v0(pair, q, r):
                pv = ps[:, B_BANK, 0:2 * H0 * (DH0 + 1)].rearrange("p (s h e) -> p s h e", s=2, h=H0)
                pe.wait_ge(S[("t0_by_act", "t0_by_dve")[r % 2]], 2 * pair + r // 2 + 1)
                for s in range(4):
                    head, patch = 4 * (s // 2) + r, s % 2
                    last = T.matmul(pv[:, patch, head], pT0[:, r, s], v_aug[:, 2 * q + patch, head],
                                    start=True, stop=True)
                return last

            def keys(b, n, half):
                if half == 0 and n == 0:
                    pe.wait_ge(S["tl_ready"], b + 1)
                elif half == 0:
                    pe.wait_ge(S["k_copied"], 2 * b + 1)
                project(ps[:, A_BANK], 0, n, half, "k_done")

            def values(b, n, half):
                if half == 0 and n == 0:
                    pe.wait_ge(S["k_copied"], 2 * b + 2)
                elif half == 0:
                    pe.wait_ge(S["v_copied"], 2 * b + 1)
                project(ps[:, A_BANK], 1, n, half, "v_done")

            def odd_pair(b):
                pair = 2 * b - 1
                wait(pe, S["delta0_ready"], b - 1)
                pe.wait_ge(S["v0_ready"], b + 1)
                pe.wait_ge(S["exp0_ready"], pair + 1)
                turn_p0(pair, 1, 0)
                turn_p0(pair, 1, 1)
                keys(b, 0, 0)
                pe.wait_ge(S["kT_copied"], 2 * b)
                times_v0(pair, 1, 0)
                turn_p0(pair, 1, 2)
                keys(b, 0, 1)
                times_v0(pair, 1, 1)
                turn_p0(pair, 1, 3)
                keys(b, 1, 0)
                times_v0(pair, 1, 2)
                keys(b, 1, 1)
                times_v0(pair, 1, 3).then_inc(S["pv0_done"], 1)

            def even_pair(b, first=False):
                pair = 2 * b
                pe.wait_ge(S["exp0_ready"], pair + 1)
                if first:
                    pe.wait_ge(S["v0_ready"], 1)
                turn_p0(pair, 0, 0)
                turn_p0(pair, 0, 1)
                if first:
                    pe.wait_ge(S["wv_lo_ready"], KC)
                values(b, 0, 0)
                turn_p0(pair, 0, 2)
                values(b, 0, 1)
                if not first:
                    pe.wait_ge(S["gelu_ready"], b)
                times_v0(pair, 0, 0)
                times_v0(pair, 0, 1)
                turn_p0(pair, 0, 3)
                values(b, 1, 0)
                values(b, 1, 1)
                times_v0(pair, 0, 2)
                times_v0(pair, 0, 3).then_inc(S["pv0_done"], 1)

            def turn_keys(b, n, last=False):
                if n == 0:
                    pe.wait_ge(S["knorm_ready"], b + 1)
                    pe.wait_ge(S["v_copied"], 2 * b + 2)
                else:
                    if last:
                        pe.wait_ge(S["o0_ready"], 2 * b + 1)
                    else:
                        pe.wait_ge(S["stack_ready"], 4 * b + 6)
                for h in range(4):
                    last_turn = T.transpose(ps[:, (A_BANK, B_BANK)[n], h * P:(h + 1) * P], k_norm[:, 4 * n + h],
                                            ident[:])
                last_turn.then_inc(S["kT_done"], 1)

            def stack(b, i):
                m, bank = STACKS[i]
                if i == 0:
                    pe.wait_ge(S["xl_ready"], b + 1)
                    pe.wait_ge(S["maskb_ready"], 2 * b + 2)
                    wait(pe, S["t0_by_act"], 4 * b - 2)
                elif i == 1:
                    wait(pe, S["o0_ready"], 2 * b - 1)
                elif i == 2:
                    wait(pe, S["t0_by_dve"], 4 * b - 2)
                else:
                    wait(pe, S["kT_copied"], 2 * b - 1)
                last = three(ps[:, bank], wst_hi[:, m], wst_lo[:, m], xn0_hi[:], xn0_lo[:], True, m % 2 == 1)
                if m % 2 == 0:
                    last = T.matmul(ps[:, bank], mask_sel[:], mask_bias[:],
                                    start=False, stop=True)
                last.then_inc(S["stack_done"], 1)

            def values0(b):
                pe.wait_ge(S["ctx_in"], 16 * (b + 1))
                pe.wait_ge(S["stack_ready"], 4 * b + 3)
                for s in range(NPATCH):
                    last = T.matmul(ps[:, 5, s * E0:(s + 1) * E0], ctx_nat[:, s * P:(s + 1) * P], wv0[:],
                                    start=True, stop=True)
                last.then_inc(S["v0_done"], 1)

            def turn_o(b):
                pe.wait_ge(S["o0_ready"], 2 * b + 2)
                for s in range(2):
                    last = T.transpose(ps[:, B_BANK, s * P:(s + 1) * P],
                                       o_tile[:, 2 * s:2 * s + 2].rearrange("p a e -> p (a e)"), ident[:])
                last.then_inc(S["oT0_done"], 1)

            def output0(b):
                pe.wait_ge(S["gello_ready"], b + 1)
                out_patches = ps[:, 4].rearrange("p (s a n) -> p a s n", s=2, a=2)
                for a in range(2):
                    last = three(out_patches[:, a], wo0_hi[:, a], wo0_lo[:, a], gel_hi[:], gel_lo[:], True, True)
                last.then_inc(S["wo0_done"], 1)

            def l0_step(b, first=False, last=False):
                pe.wait_ge(S["stack_ready"], 4 * b + 4)
                scores(2 * b, 0)
                if first:
                    pe.wait_ge(S["wk_lo_ready"], KC)
                    for n in range(2):
                        keys(b, n, 0)
                        keys(b, n, 1)
                else:
                    odd_pair(b)
                scores(2 * b + 1, 1)
                if not first:
                    turn_o(b - 1)
                even_pair(b, first)
                pe.wait_ge(S["vnext_ready"], b + 1)
                turn_keys(b, 0)
                if not last:
                    for i in range(4):
                        stack(b + 1, i)
                if not first:
                    if last:
                        pe.wait_ge(S["t0_by_act"], 4 * b + 2)
                    else:
                        pe.wait_ge(S["stack_ready"], 4 * b + 5)
                    output0(b - 1)
                turn_keys(b, 1, last)
                if not last:
                    values0(b + 1)

            pe.wait_ge(S["ident_ready"], 1)
            pe.wait_ge(S["wst_hi_ready"], 2)
            pe.wait_ge(S["wst_lo_ready"], 1)
            for i in range(4):
                stack(0, i)
            values0(0)
            l0_step(0, first=True)
            l0_step(1)
            with pe.Fori(2, NB - 1) as b:
                l0_step(b)
            l0_step(NB - 1, last=True)

            def ln_turn(i, t):
                pe.wait_ge(LN[i]["xn_ready"], t + 1)
                wait(pe, LN[i]["lo_ready"], t - 1)
                bank = LN_BANKS[i][t // 4][t % 2]
                for k in range(KC):
                    last = T.transpose(ps[:, bank, k * P:(k + 1) * P], xn[:, t % 4, k * P:(k + 1) * P], ident[:])
                last.then_inc(LN[i]["t_done"], 1)

            pair = 2 * NB - 1
            pe.wait_ge(S["delta0_ready"], NB - 1)
            pe.wait_ge(S["exp0_ready"], pair + 1)
            turn_p0(pair, 1, 0)
            turn_p0(pair, 1, 1)
            pe.wait_ge(S["kT_copied"], 2 * NB)
            times_v0(pair, 1, 0)
            turn_p0(pair, 1, 2)
            times_v0(pair, 1, 1)
            turn_p0(pair, 1, 3)
            times_v0(pair, 1, 2)
            times_v0(pair, 1, 3).then_inc(S["pv0_done"], 1)
            ln_turn(0, 0)
            ln_turn(0, 1)
            turn_o(NB - 1)
            ln_turn(0, 2)
            ln_turn(0, 3)
            output0(NB - 1)

            def gate_up(i, c, slot, half, between=lambda u, k: None):
                pe.wait_ge(FF[i]["wlo_ready"], c + 1)
                wait(pe, FF[i]["gated_ready"], 2 * c + half - 1)
                for u, bank in ((0, half), (1, 2 + half)):
                    for k in range(KC):
                        cols = slice(u * D + k * P, u * D + (k + 1) * P)
                        toks = slice(half * HALF, (half + 1) * HALF)
                        last = three(ps[:, bank], ffn_hi[:, slot, cols], ffn_lo[:, slot, cols],
                                     hT_hi[:, k, toks], hT_lo[:, k, toks], k == 0, k == KC - 1)
                        if u == 1 and k == KC - 1:
                            last.then_inc(FF[i]["gu_done"], 1)
                        between(u, k)

            def down(i, c, slot, half, tiles=range(4)):
                pe.wait_ge(FF[i]["glo_ready"], 2 * c + half + 1)
                for t in (4 * half + n for n in tiles):
                    wait(pe, FF[i]["x_added"], NB * c + t - 3)
                    toks = slice((t % 4) * P, (t % 4 + 1) * P)
                    three(ps[:, 4 + t % 4], gT_hi[:, half, toks], gT_lo[:, half, toks],
                          ffn_hi[:, slot, 2 * D:], ffn_lo[:, slot, 2 * D:], True, True)\
                        .then_inc(FF[i]["down_done"], 1)

            def ffn(i, n):
                pe.wait_ge(LN[2 * i]["lo_ready"], 4)

                def turn_two(u, k):
                    if (u, k) in ((0, KC - 1), (1, 1)):
                        ln_turn(2 * i, 4 + 2 * u)
                        ln_turn(2 * i, 5 + 2 * u)
                gate_up(i, 0, 0, 0, turn_two)
                pe.wait_ge(LN[2 * i]["lo_ready"], NB)
                gate_up(i, 0, 0, 1)
                down(i, 0, 0, 0)

                def step(c, slot):
                    gate_up(i, c, slot, 0)
                    down(i, c - 1, 1 - slot, 1)
                    gate_up(i, c, slot, 1)
                    down(i, c, slot, 0)
                if n > 4:
                    with pe.Fori(1, n - 2, 2) as c:
                        step(c, 1)
                        step(c + 1, 0)
                    step(n - 2, 1)
                else:
                    for c in range(1, n - 1):
                        step(c, c % 2)
                slot = (n - 1) % 2
                gate_up(i, n - 1, slot, 0)
                down(i, n - 2, 1 - slot, 1)
                if i == 0:
                    down(i, n - 1, slot, 0)
                    gate_up(i, n - 1, slot, 1)
                    ln_turn(1, 0)
                    ln_turn(1, 1)
                    down(i, n - 1, slot, 1, range(2))
                    ln_turn(1, 2)
                    ln_turn(1, 3)
                    down(i, n - 1, slot, 1, range(2, 4))
                else:
                    gate_up(i, n - 1, slot, 1)
                    down(i, n - 1, slot, 0)
                    down(i, n - 1, slot, 1)

            ffn(0, CH0)

            def square_sums(g, half, h):
                pe.wait_ge(S["sq_ready"], 8 * g + 4 * half + h + 1)
                if h == 0:
                    wait(pe, S["qvar_ready"], 2 * g + half)
                for b in range(4):
                    last = T.matmul(ps[:, 7, 4 * b + h:4 * b + h + 1], q_sq[:, h, b * P:(b + 1) * P], ones_col[:],
                                    start=True, stop=True)
                last.then_inc(S["ss_done"], 1)

            def score(g, b):
                n = 8 * g + b
                if b == 0:
                    pe.wait_ge(S["kT_in"], 16 * (g + 1))
                if b % 4 == 0:
                    pe.wait_ge(S["q_copied"], n + 4)
                wait(pe, S["masked_ready"], n - 1)
                for h in range(GROUP):
                    q, k = slice((b % 4) * P, (b % 4 + 1) * P), slice(b * P, (b + 1) * P)
                    last = T.matmul(ps[:, 2 + b % 2, h * P:(h + 1) * P], qT[:, h, q], kT[:, k], start=True, stop=True)
                last.then_inc(S["s_done"], 1)

            def turn_p(g, b):
                n = 8 * g + b
                pe.wait_ge(S["pn_ready"], n + 1)
                wait(pe, S["ptlo_ready"], n - 1)
                for h in range(GROUP):
                    last = T.transpose(ps[:, T_BANKS[b % 2], h * P:(h + 1) * P], prob[:, b % 4, h], ident[:])
                last.then_inc(S["t_done"], 1)

            def times_v(g, b):
                n = 8 * g + b
                if b == 0:
                    pe.wait_ge(S["v_lo_ready"], g + 1)
                pe.wait_ge(S["ptlo_ready"], n + 1)
                wait(pe, S["olo_ready"], n)
                three(ps[:, 5], v_hi[:, b], v_lo[:, b], pT_hi[:, b % 2], pT_lo[:, b % 2], True, True)\
                    .then_inc(S["pv_done"], 1)

            def output(g, t, after_output=False):
                n = 8 * g + t
                if t == 0:
                    pe.wait_ge(S["wo_lo_ready"], g + 1)
                pe.wait_ge(S["olo_ready"], n + 1)
                if t % 4 < 2 and not after_output:
                    pe.wait_ge(S["q_copied"], 8 * g + (7 if t < 4 else 11) + t % 4)
                else:
                    pe.wait_ge(S["x_added"], n - 1)
                for h in range(GROUP):
                    last = three(ps[:, t % 2], oT_hi[:, t % 4, h], oT_lo[:, t % 4, h], wo_hi[:, h], wo_lo[:, h],
                                 h == 0, h == GROUP - 1)
                last.then_inc(S["wo_done"], 1)

            def att_step(g, first=False):
                for j in range(4):
                    queries_after(g, 0, j, first)
                    if first:
                        for t in FIRST_TURNS[j]:
                            ln_turn(1, t)
                    if j >= 1:
                        square_sums(g, 0, j - 1)
                    if not first:
                        turn_p(g - 1, 4 + j)
                        if j >= 1:
                            times_v(g - 1, 3 + j)
                for j in range(4):
                    if not first:
                        output(g - 1, 4 + j)
                        if j == 0:
                            times_v(g - 1, 7)
                    if j == 0:
                        square_sums(g, 0, 3)
                        if first:
                            pe.wait_ge(LN[1]["lo_ready"], NB)
                    score(g, j)
                    if first and j % 2:
                        queries_after(g, 1, j // 2, first)
                for j in range(4):
                    if not first or j >= 2:
                        queries_after(g, 1, j, first)
                    if j >= 1:
                        square_sums(g, 1, j - 1)
                    turn_p(g, j)
                    if j >= 1:
                        times_v(g, j - 1)
                for j in range(4):
                    output(g, j)
                    if j == 0:
                        times_v(g, 3)
                        square_sums(g, 1, 3)
                    score(g, 4 + j)

            def queries_after(g, half, h, first):
                n = 8 * g + 4 * half + h
                pe.wait_ge(S["wq_lo_ready"], g + 1)
                if h >= 2:
                    pe.wait_ge(S["q_copied"], n - 1)
                elif half == 0 and not first:
                    pe.wait_ge(S["x_added"], 8 * g - 5 + h)
                elif half == 1 and not first:
                    pe.wait_ge(S["x_added"], 8 * g - 1 + h)
                elif half == 1:
                    pe.wait_ge(S["q_copied"], 3 + h)
                for k in range(KC):
                    toks = slice(half * HALF, (half + 1) * HALF)
                    last = three(ps[:, h % 2], wq_hi[:, h, k], wq_lo[:, h, k], hT_hi[:, k, toks], hT_lo[:, k, toks],
                                 k == 0, k == KC - 1)
                last.then_inc(S["q_done"], 1)

            pe.wait_ge(LN[1]["lo_ready"], 4)
            att_step(0, first=True)
            with pe.Fori(1, KVH) as g:
                att_step(g)
            g = KVH - 1
            turn_p(g, 4)
            turn_p(g, 5)
            times_v(g, 4)
            turn_p(g, 6)
            times_v(g, 5)
            output(g, 4, after_output=True)
            turn_p(g, 7)
            times_v(g, 6)
            output(g, 5, after_output=True)
            times_v(g, 7)
            output(g, 6, after_output=True)
            ln_turn(2, 0)
            ln_turn(2, 1)
            output(g, 7, after_output=True)
            ln_turn(2, 2)
            ln_turn(2, 3)
            ffn(1, CH1)


def kernel(**inputs):
    import numpy as np
    import concourse.bacc as _bacc
    from concourse.bass_utils import run_bass_kernel_spmd as _run

    a = {k: np.asarray(v) for k, v in inputs.items()}

    def chunks(w):
        return np.ascontiguousarray(w.T.reshape(-1, P, w.shape[0]).transpose(1, 0, 2))

    def stack(w, group, parts):
        o = np.zeros((P,) + w.shape[1:], w.dtype)
        for h in range(4):
            for r in range(parts):
                at = STACK * h + DH0 * r
                o[at:at + DH0] = w[(4 * group + h) * DH0:(4 * group + h + 1) * DH0]
        return o

    wst = np.zeros((P, 4, P), np.float32)
    stack_col = np.zeros((P, 6), np.float32)
    mask_sel = np.zeros((1, P), np.float32)
    for grp in range(2):
        wst[:, 2 * grp] = stack(a["L0_xattn_Wk"], grp, 3).T
        wst[:, 2 * grp + 1] = stack(a["L0_xattn_Wq"], grp, 3).T
        stack_col[:, 2 * grp] = stack(a["L0_xattn_bk"], grp, 3)
        stack_col[:, 2 * grp + 1] = stack(a["L0_xattn_bq"], grp, 3)
        stack_col[3 * DH0::STACK, 2 * grp + 1] = 1.0
    for h in range(4):
        stack_col[STACK * h + DH0:STACK * h + 2 * DH0, 4] = -1.0
        stack_col[STACK * h + 2 * DH0:STACK * h + 3 * DH0, 5] = -1.0
    mask_sel[0, 3 * DH0::STACK] = 1.0

    wo0 = np.zeros((P, 2, P), np.float32)
    for n in range(2):
        wo0[E0 * n:E0 * n + E0, n] = a["L0_xattn_Wo"].T

    def ffn(gate, up, down):
        n = -(-gate.shape[0] // P)
        o = np.zeros((n, P, 3 * D), np.float32)
        for u, w in enumerate((gate, up)):
            full = np.zeros((n * P, D), np.float32)
            full[:w.shape[0]] = w
            o[:, :, u * D:(u + 1) * D] = full.reshape(n, P, KC, P).transpose(0, 3, 2, 1).reshape(n, P, D)
        full = np.zeros((n * P, D), np.float32)
        full[:down.shape[1]] = down.T
        o[:, :, 2 * D:] = full.reshape(n, P, D)
        return o

    w12, b12 = a["L1_ffn_w12"], a["L1_ffn_b12"]
    arrays = {
        "x": a["x"],
        "ctx": a["ctx_4096"],
        "ctxT": chunks(a["ctx_4096"].reshape(TOK, D)),
        "mask": a["mask_Bx1x4096_ff1"],
        "mask_row": a["mask_Bx1x4096_ff1"].reshape(NB, D),
        "mask1": a["mask_1x1xSxS2_ff0"].reshape(P, P),
        "wst": wst,
        "stack_col": stack_col,
        "mask_sel": mask_sel,
        "wv0": a["L0_xattn_Wv"].T,
        "bv0": a["L0_xattn_bv"].reshape(1, E0),
        "wo0": wo0,
        "bo0": a["L0_xattn_bo"].reshape(P, 1),
        "ffn0": ffn(a["L0_ffn_w_gate"], a["L0_ffn_w_up"], a["L0_ffn_w_down"]),
        "wkv": np.concatenate([chunks(a["L1_xattn_Wk"]), chunks(a["L1_xattn_Wv"])], 1),
        "wq": a["L1_xattn_Wq"].reshape(KVH, GROUP, P, KC, P).transpose(0, 4, 1, 3, 2),
        "wo": a["L1_xattn_Wo"].T.reshape(KVH, GROUP, HD, D).transpose(0, 2, 1, 3),
        "norm_w": np.stack([a["L1_xattn_q_norm_w"], a["L1_xattn_k_norm_w"]], 1),
        "ffn1": ffn(w12[:D], w12[D:], a["L1_ffn_w3"]),
        "b12": b12.reshape(2, CH1, P).transpose(2, 0, 1),
        "b3": a["L1_ffn_b3"].reshape(1, D),
    }
    nc = _bacc.Bacc("TRN2", target_bir_lowering=False, num_devices=1)
    feeds, A = {}, {}
    for name, v in arrays.items():
        v = np.ascontiguousarray(v)
        feeds[f"in_{name}"] = v
        A[name] = nc.dram_tensor(f"in_{name}", v.shape, mybir.dt.from_np(v.dtype), kind="ExternalInput").ap()
    out = nc.dram_tensor("out_0", (NB, P, D), F32, kind="ExternalOutput").ap()
    build(nc, A, out)
    r = _run(nc, [feeds], core_ids=[0])
    return r.results[0]["out_0"]
```
